# Optimizing a Trainium2 kernel written in Bass

```python
import numpy as np
import jax
import jax.numpy as jnp

def _softmax(x, axis=-1):
    return jax.nn.softmax(x, axis=axis)

def _gelu(x):
    return jax.nn.gelu(x, approximate=True)

def _silu(x):
    return jax.nn.silu(x)

def _sigmoid(x):
    return jax.nn.sigmoid(x)

def _layernorm(x, axis=-1, eps=1e-05):
    m = jnp.mean(x, axis=axis, keepdims=True)
    v = jnp.var(x, axis=axis, keepdims=True)
    return (x - m) / jnp.sqrt(v + eps)

def _scatter_add(tgt, idx, src, axis=0):
    return tgt.at[idx].add(src)

def _segment_sum(src, seg, n):
    return jax.ops.segment_sum(src, seg, n)
kernel_name = 'mk_adaln_d1_jaxref_r8_c24b73'

def setup_inputs(seed: int=0):
    np.random.seed(seed)
    _w = jnp.asarray

    def _L0_attn_setup():
        import jax, jax.numpy as jnp
        import numpy as np
        B, S, D, H = (2, 256, 256, 16)
        HD = D // H
        key = jax.random.key(seed)
        kx, kq, kk, kv, ko = jax.random.split(key, 5)
        scale = 1.0 / np.sqrt(D)
        return {'x': jax.random.normal(kx, (B, S, D), dtype=jnp.float32), 'wq': jax.random.normal(kq, (D, D), dtype=jnp.float32) * scale, 'wk': jax.random.normal(kk, (D, D), dtype=jnp.float32) * scale, 'wv': jax.random.normal(kv, (D, D), dtype=jnp.float32) * scale, 'wo': jax.random.normal(ko, (D, D), dtype=jnp.float32) * scale}
    _L0_attn_in = _L0_attn_setup()

    def _L0_ffn_setup():
        import jax, jax.numpy as jnp
        import numpy as np
        HIDDEN = 256
        NUM_EXPERTS = 32
        TOP_K = 4
        D_MOE = 96
        D_SHARED = 512
        B, S = (1, 256)

        def _moe_forward(hidden_states, gate_w, gate_up_proj, down_proj, shared_gate_w, shared_up_w, shared_down_w, shared_expert_gate_w):
            Bb, Ss, d = hidden_states.shape
            x = hidden_states.reshape(-1, d)
            T = x.shape[0]
            router_logits = x @ gate_w.T
            routing_weights = jax.nn.softmax(router_logits.astype(jnp.float32), axis=-1)
            topk_w, topk_idx = jax.lax.top_k(routing_weights, TOP_K)
            topk_w = topk_w / (jnp.sum(topk_w, axis=-1, keepdims=True) + 1e-20)
            topk_w = topk_w.astype(x.dtype)
            comb = jnp.zeros((T, NUM_EXPERTS), x.dtype).at[jnp.arange(T)[:, None], topk_idx].add(topk_w)
            sh = jax.nn.silu(x @ shared_gate_w.T) * (x @ shared_up_w.T)
            shared_out = sh @ shared_down_w.T
            shared_gate = jax.nn.sigmoid(x @ shared_expert_gate_w.T)
            out0 = shared_gate * shared_out

            def body(acc, inp):
                gu_w, dn_w, w_e = inp
                gu = x @ gu_w.T
                gate, up = (gu[:, :D_MOE], gu[:, D_MOE:])
                h = jax.nn.silu(gate) * up
                y = h @ dn_w.T
                return (acc + w_e[:, None] * y, None)
            out, _ = jax.lax.scan(body, out0, (gate_up_proj, down_proj, comb.T))
            return out.reshape(Bb, Ss, d)
        key = jax.random.key(seed)
        ks = jax.random.split(key, 8)
        sc = 0.02
        return {'hidden_states': jax.random.normal(ks[0], (B, S, HIDDEN), jnp.float32), 'gate_w': jax.random.normal(ks[1], (NUM_EXPERTS, HIDDEN), jnp.float32) * sc, 'gate_up_proj': jax.random.normal(ks[2], (NUM_EXPERTS, 2 * D_MOE, HIDDEN), jnp.float32) * sc, 'down_proj': jax.random.normal(ks[3], (NUM_EXPERTS, HIDDEN, D_MOE), jnp.float32) * sc, 'shared_gate_w': jax.random.normal(ks[4], (D_SHARED, HIDDEN), jnp.float32) * sc, 'shared_up_w': jax.random.normal(ks[5], (D_SHARED, HIDDEN), jnp.float32) * sc, 'shared_down_w': jax.random.normal(ks[6], (HIDDEN, D_SHARED), jnp.float32) * sc, 'shared_expert_gate_w': jax.random.normal(ks[7], (1, HIDDEN), jnp.float32) * sc}
    _L0_ffn_in = _L0_ffn_setup()
    _L0_c = _w((lambda *s: np.random.randn(*s).astype(np.float32) * 0.05)(4, 256))
    _L0_wmod = _w((lambda *s: np.random.randn(*s).astype(np.float32) * 0.05)(256, 6 * 256) * 256 ** (-0.5))
    _d = {'L0_attn_x': _L0_attn_in['x'], 'L0_attn_wq': _L0_attn_in['wq'], 'L0_attn_wk': _L0_attn_in['wk'], 'L0_attn_wv': _L0_attn_in['wv'], 'L0_attn_wo': _L0_attn_in['wo'], 'L0_ffn_gate_w': _L0_ffn_in['gate_w'], 'L0_ffn_gate_up_proj': _L0_ffn_in['gate_up_proj'], 'L0_ffn_down_proj': _L0_ffn_in['down_proj'], 'L0_ffn_shared_gate_w': _L0_ffn_in['shared_gate_w'], 'L0_ffn_shared_up_w': _L0_ffn_in['shared_up_w'], 'L0_ffn_shared_down_w': _L0_ffn_in['shared_down_w'], 'L0_ffn_shared_expert_gate_w': _L0_ffn_in['shared_expert_gate_w'], 'L0_c': _L0_c, 'L0_wmod': _L0_wmod}
    _x0 = _d['L0_attn_x']
    _d['L0_attn_x'] = jax.random.normal(jax.random.fold_in(jax.random.key(seed), 1), (4, 512, 256), dtype=_x0.dtype)
    del _x0
    return _d

def reference(L0_attn_x, L0_attn_wq, L0_attn_wk, L0_attn_wv, L0_attn_wo, L0_ffn_gate_w, L0_ffn_gate_up_proj, L0_ffn_down_proj, L0_ffn_shared_gate_w, L0_ffn_shared_up_w, L0_ffn_shared_down_w, L0_ffn_shared_expert_gate_w, L0_c, L0_wmod):

    def _L0_attn_ref(x, wq, wk, wv, wo):
        import jax, jax.numpy as jnp
        import numpy as np
        B, S, D, H = (2, 256, 256, 16)
        HD = D // H
        bsz, seqlen, dim = x.shape
        xq = (x @ wq.T).reshape(bsz, seqlen, H, HD)
        xk = (x @ wk.T).reshape(bsz, seqlen, H, HD)
        xv = (x @ wv.T).reshape(bsz, seqlen, H, HD)
        scores = jnp.einsum('bqhd,bkhd->bhqk', xq, xk)
        probs = jax.nn.softmax(scores.astype(jnp.float32), axis=-1).astype(xq.dtype)
        out = jnp.einsum('bhqk,bkhd->bqhd', probs, xv).reshape(bsz, seqlen, dim)
        return out @ wo.T

    def _L0_ffn_ref(hidden_states, gate_w, gate_up_proj, down_proj, shared_gate_w, shared_up_w, shared_down_w, shared_expert_gate_w):
        import jax, jax.numpy as jnp
        import numpy as np
        HIDDEN = 256
        NUM_EXPERTS = 32
        TOP_K = 4
        D_MOE = 96
        D_SHARED = 512
        B, S = (1, 256)

        def _moe_forward(hidden_states, gate_w, gate_up_proj, down_proj, shared_gate_w, shared_up_w, shared_down_w, shared_expert_gate_w):
            Bb, Ss, d = hidden_states.shape
            x = hidden_states.reshape(-1, d)
            T = x.shape[0]
            router_logits = x @ gate_w.T
            routing_weights = jax.nn.softmax(router_logits.astype(jnp.float32), axis=-1)
            topk_w, topk_idx = jax.lax.top_k(routing_weights, TOP_K)
            topk_w = topk_w / (jnp.sum(topk_w, axis=-1, keepdims=True) + 1e-20)
            topk_w = topk_w.astype(x.dtype)
            comb = jnp.zeros((T, NUM_EXPERTS), x.dtype).at[jnp.arange(T)[:, None], topk_idx].add(topk_w)
            sh = jax.nn.silu(x @ shared_gate_w.T) * (x @ shared_up_w.T)
            shared_out = sh @ shared_down_w.T
            shared_gate = jax.nn.sigmoid(x @ shared_expert_gate_w.T)
            out0 = shared_gate * shared_out

            def body(acc, inp):
                gu_w, dn_w, w_e = inp
                gu = x @ gu_w.T
                gate, up = (gu[:, :D_MOE], gu[:, D_MOE:])
                h = jax.nn.silu(gate) * up
                y = h @ dn_w.T
                return (acc + w_e[:, None] * y, None)
            out, _ = jax.lax.scan(body, out0, (gate_up_proj, down_proj, comb.T))
            return out.reshape(Bb, Ss, d)
        return _moe_forward(hidden_states, gate_w, gate_up_proj, down_proj, shared_gate_w, shared_up_w, shared_down_w, shared_expert_gate_w)
    x = L0_attn_x
    mod = (_silu(L0_c) @ L0_wmod).reshape(L0_c.shape[0], 6, 1, -1)
    sa, ca, ga, sb, cb, gb = (mod[:, 0], mod[:, 1], mod[:, 2], mod[:, 3], mod[:, 4], mod[:, 5])
    ga = (2 * (ga >= 0) - 1) * jnp.maximum(jnp.abs(ga), 0.25)
    gb = (2 * (gb >= 0) - 1) * jnp.maximum(jnp.abs(gb), 0.25)
    h = _layernorm(x, axis=-1) * (1 + ca) + sa
    x = x + ga * _L0_attn_ref(h, L0_attn_wq, L0_attn_wk, L0_attn_wv, L0_attn_wo)
    h = _layernorm(x, axis=-1) * (1 + cb) + sb
    x = x + gb * _L0_ffn_ref(h, L0_ffn_gate_w, L0_ffn_gate_up_proj, L0_ffn_down_proj, L0_ffn_shared_gate_w, L0_ffn_shared_up_w, L0_ffn_shared_down_w, L0_ffn_shared_expert_gate_w)
    return x

_drawn_inputs = setup_inputs


def setup_inputs(seed=0):
    import zlib

    import numpy as np

    out = dict(_drawn_inputs(seed))
    spreads = {}
    factors = {'L0_ffn_gate_w': 8.0,
     'L0_ffn_gate_up_proj': 8.0,
     'L0_ffn_down_proj': 8.0,
     'L0_ffn_shared_gate_w': 8.0,
     'L0_ffn_shared_up_w': 8.0,
     'L0_ffn_shared_down_w': 8.0,
     'L0_ffn_shared_expert_gate_w': 8.0}
    for name, (base, spread) in spreads.items():
        noise = np.random.default_rng([zlib.crc32(name.encode()), seed]).standard_normal(out[name].shape)
        drawn = base * np.exp(spread * noise) if base else spread * noise
        out[name] = jnp.asarray(drawn.astype(out[name].dtype))
    for name, factor in factors.items():
        out[name] = (out[name] * factor).astype(out[name].dtype)
    return out
```

```python
from contextlib import ExitStack

import concourse.bass as bass
from concourse import mybir

ALU = mybir.AluOpType
ACT = mybir.ActivationFunctionType
AXX = mybir.AxisListType.X
F32 = mybir.dt.float32
F32R = mybir.dt.float32r
I32 = mybir.dt.int32
U32 = mybir.dt.uint32

P = 128
B, S, D = 4, 512, 256
H, HD = 16, 16
KD = D // P
TJ = S // P
NT = B * TJ
G = 4
NG = H // G
E, TOPK, DM, DS = 32, 4, 96, 512
CAP = B * S + P
MT = B * S * TOPK // P + E
ROW = D + 2
SKIP = 1 << 20
NY = B * S * TOPK
EPS = 1e-5


class Steps:

    def __init__(self, eng, sem):
        self.eng, self.sem, self.base, self.n = eng, sem, 0, 0

    def did(self, ins):
        ins.then_inc(self.sem, 1)
        self.n += 1

    def wait(self):
        self.eng.wait_ge(self.sem, self.base + self.n)

    def then(self, ins):
        self.did(ins)
        self.wait()

    def enter(self, i, per):
        self.total, self.base, self.n, self.per = self.n, self.n + i * per, 0, per

    def leave(self, turns):
        assert self.n == self.per, (self.n, self.per)
        self.base, self.n = 0, self.total + turns * self.per


def adaln_moe_kernel(nc, x_in, wq, wk, wv, wo, gate, up, down, sgate, sup, sdown, c_in, wmod_in, out):
    ctx = ExitStack()
    with ctx:
        def sb(name, shape, dt=F32):
            return ctx.enter_context(nc.sbuf_tensor(name, shape, dt))

        def sem(name):
            return ctx.enter_context(nc.semaphore(name))

        def overlay(first, second):
            made, ends = {}, []
            for specs in (first, second):
                with ExitStack() as here:
                    for name, shape, dt in specs:
                        made[name] = here.enter_context(nc.sbuf_tensor(name, shape, dt))
                    ends.append(nc.sbuf_base)
            sb(f"{first[0][0]}_{second[0][0]}", [P, max(ends) - nc.sbuf_base], mybir.dt.uint8)
            return made

        big = overlay([("q_stack", [P, H, S], F32R), ("k_stack", [P, H, S], F32R), ("probs", [P, 2 * G, S], F32)],
                      [("up_sb", [P, KD * E * 2 * DM], F32), ("down_sb", [DM, E * D], F32)])
        q_stack, k_stack, probs, up_sb, down_sb = (big[n] for n in ("q_stack", "k_stack", "probs", "up_sb", "down_sb"))
        comb = up_sb[:, 0:4 * TOPK * D].rearrange("p (r n) -> p r n", r=4)
        mid = overlay([("wmod", [P, KD, 6 * D], F32), ("c_rep", [P, KD, B, P], F32)], [("h2T", [P, KD * B * S], F32)])
        wmod, c_rep, h2T = mid["wmod"], mid["c_rep"], mid["h2T"]
        XR = 4
        rest = overlay(
            [("qk_hi", [P, 4, S], F32R), ("qk_lo", [P, 4, S], F32R), ("v_ext", [P, TJ, H, 32], F32), ("hT", [P, KD, S], F32),
             ("xn", [P, TJ, D], F32), ("oT_raw", [P, S], F32), ("lgT", [E + 1, S], F32), ("max_hi", [G, 2, S], F32R),
             ("max_lo", [G, 2, S], F32R), ("onehot", [P, TJ * TOPK, E], F32)],
            [("xe", [P, XR, ROW], F32), ("xeT", [P, 2, KD * P], F32), ("e_silu", [P, 2, DM], F32), ("e_hid", [P, 2, DM], F32),
             ("e_hidT", [DM, 2, P], F32), ("y_sb", [P, 4, D], F32), ("sh_hidT", [P, 4, S], F32), ("sh_silu", [P, 2, S], F32),
             ("sgate_sb", [P, KD, DS], F32), ("sup_sb", [P, KD, DS], F32), ("sdown_sb", [P, DS // P, D], F32)])
        qk_hi, qk_lo, v_ext, hT, xn, oT_raw, lgT, max_hi, max_lo, onehot = (rest[n] for n in (
            "qk_hi", "qk_lo", "v_ext", "hT", "xn", "oT_raw", "lgT", "max_hi", "max_lo", "onehot"))
        xe, xeT, e_silu, e_hid, e_hidT, y_sb, sh_hidT, sh_silu, sgate_sb, sup_sb, sdown_sb = (rest[n] for n in (
            "xe", "xeT", "e_silu", "e_hid", "e_hidT", "y_sb", "sh_hidT", "sh_silu", "sgate_sb", "sup_sb", "sdown_sb"))
        o_norm, oT = xn, hT

        x = sb("x", [P, NT * D])
        h2 = sb("h2", [P, TJ, ROW])
        wq_sb, wk_sb, wv_sb, wo_sb = (sb(n, [P, KD, D]) for n in ("wq_sb", "wk_sb", "wv_sb", "wo_sb"))
        wo_g = sb("wo_g", [P, B * KD * D])
        mod_b = sb("mod_b", [P, B * 3 * D])
        gate_sb = sb("gate_sb", [P, KD, E + 1])
        modT = sb("modT", [P, 2 * KD * B])
        ident = sb("ident", [P, P])
        ones = sb("ones", [P, P])
        upper = sb("upper", [P, P])
        cT = sb("cT", [P, KD * B])
        ctmp = sb("ctmp", [P, KD * B])
        gtmp = sb("gtmp", [P, 2, D])
        pad_rows = sb("pad_rows", [P, ROW])
        bn = sb("bn", [P, NT, 6])
        mv = sb("mv", [P, NT * 2])
        rstd = sb("rstd", [P, NT])
        mv2 = sb("mv2", [P, TJ, 2])
        rstd2 = sb("rstd2", [P, TJ])
        veps = sb("veps", [P, NT])
        mhalf = sb("mhalf", [P, NT])
        max_q = sb("max_q", [P, 2, TJ, G])
        rsum = sb("rsum", [P, TJ, G])
        iota_e = sb("iota_e", [P, E], I32)
        iota_ef = sb("iota_ef", [P, E])
        base_i = sb("base_i", [P, E], I32)
        base_f = sb("base_f", [P, E])
        thr_i = sb("thr_i", [P, NT], I32)
        thr_f = sb("thr_f", [P, NT])
        tile_i = sb("tile_i", [P, 1], I32)
        tile_f = sb("tile_f", [P, 1])
        home = sb("home", [P, NT * TOPK], I32)
        lg = sb("lg", [P, TJ, E + 1])
        v8 = sb("v8", [P, TJ, 8])
        i8 = sb("i8", [P, TJ, 8], U32)
        ex = sb("ex", [P, TJ, E + TOPK])
        z4 = sb("z4", [P, TJ])
        p4 = sb("p4", [P, TJ, TOPK])
        s4 = sb("s4", [P, TJ])
        w4 = sb("w4", [P, TJ, TOPK])
        e4 = sb("e4", [P, TJ, TOPK])
        sg = sb("sg", [P, NT])
        sgt = sb("sgt", [P, TJ])
        picked = sb("picked", [P, TJ * TOPK, E])
        chosen = sb("chosen", [P, TJ, E])
        before = sb("before", [P, TJ + 1, E])
        rank = sb("rank", [P, TJ, E])
        slot_f = sb("slot_f", [P, TJ * TOPK])
        slot_i = sb("slot_i", [P, TJ * TOPK], I32)
        cnt = sb("cnt", [P, E])
        ntile = sb("ntile", [P, E])
        ctile = sb("ctile", [P, E])
        past = sb("past", [P, E])
        past_n = sb("past_n", [P, E])
        tcol = sb("tcol", [P, 4])
        tcol2 = sb("tcol2", [P, 2])
        tab = sb("tab", [1, 2 * P], I32)
        pad_at = sb("pad_at", [P, E], I32)
        ps = ctx.enter_context(nc.psum_tensor("ps", [P, 8, 512], F32))

        scr = nc.dram_tensor("qk_scratch", [B * 8, P, S], F32, kind="Internal").ap()
        xs = nc.dram_tensor("dispatched", [E * CAP + P, ROW], F32, kind="Internal").ap()
        yk = nc.dram_tensor("results", [NY, D], F32, kind="Internal").ap()

        mod_ld, w_ld, sh_ld = sem("mod_ld"), sem("w_ld"), sem("sh_ld")
        x_ld = [sem(f"x_ld{i}") for i in range(B)]
        up_ld = sem("up_ld")
        pool_s, dve_s, act_s = sem("pool_s"), sem("dve_s"), sem("act_s")
        consts = sem("consts")
        c_exp, c_rep_s, stats, rstd_s = sem("c_exp"), sem("c_rep_s"), sem("stats"), sem("rstd_s")
        mod_ps, mod_free = sem("mod_ps"), sem("mod_free")
        xn_ready = sem("xn_ready")
        misc_full = [sem("misc0_full"), sem("misc1_full")]
        misc_free = [sem("misc0_free"), sem("misc1_free")]
        hi_done = sem("hi_done")
        spill = [sem("spill0"), sem("spill1")]
        stack_ld = [sem("stack_ld0"), sem("stack_ld1")]
        sc_full, max_done = sem("sc_full"), sem("max_done")
        neg_hi = sem("neg_hi")
        maxrow = [sem("maxrow0"), sem("maxrow1")]
        st_full, exp_done, pv_done, o_free = sem("st_full"), sem("exp_done"), sem("pv_done"), sem("o_free")
        stats2, rstd2_s, h2_ready = (sem(n) for n in ("stats2", "rstd2_s", "h2_ready"))
        lg_ready, ex_in, ex_out, chosen_s, slots_s, disp = (sem(n) for n in ("lg_ready", "ex_in", "ex_out", "chosen_s", "slots_s", "disp"))
        cnt_ps, tcol_s, tab_ps, tab_s, pad_s = (sem(n) for n in ("cnt_ps", "tcol_s", "tab_ps", "tab_s", "pad_s"))
        gu_full, silu_s, shh_s, sd_full, sd_free = (sem(n) for n in ("gu_full", "silu_s", "shh_s", "sd_full", "sd_free"))
        xe_ld = [sem(f"xe_ld{i}") for i in range(XR)]
        t_full, t_done, u_full, esilu_s, hid_s, ht_full, ht_done, y_full, y_done = (
            sem(n) for n in ("t_full", "t_done", "u_full", "esilu_s", "hid_s", "ht_full", "ht_done", "y_full", "y_done"))
        y_out = [sem(f"y_out{i}") for i in range(4)]
        comb_ld = [sem(f"comb_ld{i}") for i in range(4)]
        x3_done, stored = sem("x3_done"), sem("stored")

        SC, ST, O, MISC = (0, 1), (2, 3, 4), 5, (6, 7)
        TP1, QK, VV, GRP, OT, WO, TP2, RT, RK = 0, 1, 3, 4, 8, 9, 10, 11, 12
        USES = (13, 12)

        passed = sem("passed")

        def apart(eng):
            eng.sem_inc(passed, 1)

        block = ctx.enter_context(nc.Block())

        @block.sync
        def _(sp):
            sp.dma_start(cT[:, :].rearrange("p (k b) -> p k b", k=KD), c_in.rearrange("(k p) b -> p k b", p=P)).then_inc(mod_ld, 16)
            sp.dma_start(wmod[:, :, :], wmod_in.rearrange("(k p) n -> p k n", p=P)).then_inc(mod_ld, 16)
            for w_d, w_s in ((wq, wq_sb), (wk, wk_sb), (wv, wv_sb), (wo, wo_sb)):
                sp.dma_start(w_s[:, :, :], w_d.rearrange("(k p) n -> p k n", p=P)).then_inc(w_ld, 16)
            sp.dma_start(gate_sb[:, :, :], gate.rearrange("(k p) n -> p k n", p=P)).then_inc(w_ld, 16)
            with sp.Fori(0, B, 1) as b:
                for half in range(2):
                    for m in range(2):
                        sp.wait_ge(misc_free[m], USES[m] * b + QK + half + 1)
                        apart(sp)
                    for comp, src in ((0, qk_hi), (1, qk_lo)):
                        sp.dma_start(scr[bass.ds(8 * b + 4 * half + 2 * comp, 2), :, :].rearrange("q p n -> p q n"),
                                     src[:, 2 * half:2 * half + 2, :].bitcast(F32)).then_inc(spill[half], 16)
                    sp.wait_ge(spill[half], 32 * b + 32)
                    apart(sp)
                    sp.wait_ge(pv_done, 4 * NG * b)
                    apart(sp)
                    for r in range(4):
                        for qk, stack, comp in ((0, q_stack, r % 2), (1, k_stack, r // 2)):
                            sp.dma_start(stack[16 * r:16 * r + 16, 8 * half:8 * half + 8, :].bitcast(F32),
                                         scr[bass.ds(8 * b + 4 * half + 2 * comp + qk, 1), :, :].rearrange(
                                             "o (h d) n -> (o d) h n", d=HD)).then_inc(stack_ld[half], 16)
                for g in range(NG):
                    sp.wait_ge(misc_free[0], USES[0] * b + GRP + g + 1)
                    for row, src in ((64, max_hi), (65, max_lo)):
                        sp.dma_start(q_stack[row:row + 1, G * g:G * g + G, :].bitcast(F32),
                                     src[0:G, g % 2, :].bitcast(F32)).then_inc(maxrow[g % 2], 16)
            sp.wait_ge(pv_done, 4 * NG * B)
            for k in range(KD):
                sp.dma_start(up_sb[:, k * E * 2 * DM:(k + 1) * E * 2 * DM],
                             up[k * P:(k + 1) * P, :]).then_inc(up_ld, 16)
            sp.dma_start(down_sb[:, :], down).then_inc(up_ld, 16)
            sp.wait_ge(slots_s, B)
            sp.dma_start(sgate_sb[:, :, :], sgate.rearrange("(k p) n -> p k n", p=P)).then_inc(sh_ld, 16)
            sp.dma_start(sup_sb[:, :, :], sup.rearrange("(k p) n -> p k n", p=P)).then_inc(sh_ld, 16)
            sp.dma_start(sdown_sb[:, :, :], sdown.rearrange("(k p) n -> p k n", p=P)).then_inc(sh_ld, 16)
            sp.wait_ge(tab_s, 1)
            sp.dma_start(xs[E * CAP:E * CAP + P, :], pad_rows[:, :]).then_inc(pad_s, 16)
            with sp.Fori(0, E, 1) as e:
                at = sp.value_load(pad_at[0:1, bass.ds(e, 1)], min_val=0, max_val=E * CAP)
                sp.dma_start(xs[bass.ds(at, P), :], pad_rows[:, :]).then_inc(pad_s, 16)
            sp.wait_ge(pad_s, 16 * (E + 1))
            sp.wait_ge(disp, 16 * NT * TOPK)
            with sp.Fori(0, MT // XR, 1) as i:
                for r in range(XR):
                    sp.wait_ge(y_out[r], 16 * i)
                    apart(sp)
                    at = sp.value_load(tab[0:1, bass.ds(P + XR * i + r, 1)], min_val=0, max_val=E * CAP)
                    sp.dma_start(xe[:, r, :], xs[bass.ds(at, P), :]).then_inc(xe_ld[r], 16)
            for r in range(4):
                sp.wait_ge(y_out[r], 16 * (MT // 4))
            for t in range(NT):
                if t >= 4:
                    sp.wait_ge(x3_done, t - 3)
                sp.dma_start(comb[:, t % 4, :], yk[t * P * TOPK:(t + 1) * P * TOPK, :].rearrange(
                    "(p k) d -> p (k d)", k=TOPK)).then_inc(comb_ld[t % 4], 16)

        @block.gpsimd
        def _(pool):
            st = Steps(pool, pool_s)
            st.did(pool.memset(ident[:, :], 0.0))
            st.did(pool.memset(ones[:, :], 1.0))
            st.did(pool.memset(upper[:, :], 1.0))
            st.did(pool.iota(iota_e[:, :], pattern=[[1, E]], base=0, channel_multiplier=0))
            st.did(pool.iota(base_i[:, :], pattern=[[CAP, E]], base=0, channel_multiplier=0))
            st.did(pool.iota(thr_i[:, :], pattern=[[P, NT]], base=0, channel_multiplier=0))
            st.did(pool.iota(tile_i[:, :], pattern=[[0, 1]], base=0, channel_multiplier=1))
            st.did(pool.iota(home[:, :], pattern=[[P * TOPK, NT], [1, TOPK]], base=0, channel_multiplier=TOPK))
            st.did(pool.memset(mhalf[:, :], -0.5))
            st.did(pool.memset(pad_rows[:, :], 0.0))
            st.did(pool.memset(before[:, TJ, :], 0.0))
            st.wait()
            st.did(pool.affine_select(out=ident[:, :], in_=ident[:, :], compare_op=ALU.not_equal, fill=1.0, base=0,
                                      pattern=[[-1, P]], channel_multiplier=1))
            st.did(pool.affine_select(out=upper[:, :], in_=upper[:, :], compare_op=ALU.is_gt, fill=0.0, base=0,
                                      pattern=[[1, P]], channel_multiplier=-1))
            st.did(pool.iota(pad_rows[:, D:D + 1].bitcast(I32), pattern=[[0, 1]], base=SKIP, channel_multiplier=0))
            st.wait()
            pool.memset(v_ext[:, :, :, :], 1.0).then_inc(consts, 1)
            pool.wait_ge(consts, 1)
            st.then(pool.memset(k_stack[64:128, :, :].bitcast(F32), 0.0))
            pool.memset(k_stack[64:66, :, :].bitcast(F32), 1.0).then_inc(consts, 1)
            pool.wait_ge(consts, 2)
            pool.memset(q_stack[64:128, :, :].bitcast(F32), 0.0).then_inc(consts, 1)
            pool.wait_ge(consts, 3)
            pool.wait_ge(stats, 1)
            st.then(pool.tensor_scalar(veps[:, :], mv[:, :].rearrange("p (t s) -> p t s", s=2)[:, :, 1], EPS, None, ALU.add))
            pool.tensor_tensor(rstd[:, :], veps[:, :], mhalf[:, :], ALU.pow).then_inc(rstd_s, 1)
            pool.wait_ge(rstd_s, 1)
            with pool.Fori(0, B, 1) as b:
                st.enter(b, 1 + 2 * TOPK)
                pool.wait_ge(stats2, b + 1)
                apart(pool)
                st.then(pool.tensor_scalar(veps[:, 0:TJ], mv2[:, :, 1], EPS, None, ALU.add))
                pool.tensor_tensor(rstd2[:, :], veps[:, 0:TJ], mhalf[:, 0:TJ], ALU.pow).then_inc(rstd2_s, 1)
                pool.wait_ge(rstd2_s, b + 1)
                pool.wait_ge(slots_s, b + 1)
                for k in range(TOPK):
                    pool.wait_ge(disp, 16 * NT * b + 16 * TJ * k)
                    apart(pool)
                    st.then(pool.tensor_copy(h2[:, :, D:D + 1].bitcast(I32),
                                            home[:, bass.ds(TJ * TOPK * b, TJ * TOPK)].rearrange("p (j k) -> p j k", k=TOPK)[:, :, k:k + 1]))
                    apart(pool)
                    st.then(pool.tensor_copy(h2[:, :, D + 1:D + 2], w4[:, :, k:k + 1]))
                    apart(pool)
                    for j in range(TJ):
                        pool.indirect_dma_start(out=xs, out_offset=bass.IndirectOffsetOnAxis(
                            ap=slot_i[:, TOPK * j + k:TOPK * j + k + 1], axis=0), in_=h2[:, j, :], in_offset=None).then_inc(disp, 16)
            st.leave(B)
            with pool.Fori(0, MT // 4, 1) as i:
                for r in range(4):
                    pool.wait_ge(y_done, 4 * i + r + 1)
                    apart(pool)
                    pool.indirect_dma_start(out=yk, out_offset=bass.IndirectOffsetOnAxis(
                        ap=xe[:, r, D:D + 1].bitcast(I32), axis=0), in_=y_sb[:, r, :], in_offset=None,
                        bounds_check=NY - 1, oob_is_err=False).then_inc(y_out[r], 16)

        @block.scalar
        def _(act):
            for b in range(B):
                act.dma_start(x[:, b * TJ * D:(b + 1) * TJ * D].rearrange("p (j d) -> p j d", d=D),
                              x_in[b].rearrange("(j p) d -> p j d", p=P)).then_inc(x_ld[b], 16)
            act.wait_ge(mod_ld, 32)
            act.activation(ctmp[:, :], cT[:, :], ACT.Exp, scale=-1.0).then_inc(c_exp, 1)
            act.wait_ge(mod_free, 1)
            with act.Fori(0, B, 1) as b:
                for k in range(KD):
                    act.wait_ge(misc_full[k], USES[k] * b + TP1 + 1)
                    act.activation(hT[:, k, :], ps[:, MISC[k], :], ACT.Identity,
                                   scale=modT[:, bass.ds((2 + k) * B + b, 1)],
                                   bias=modT[:, bass.ds(k * B + b, 1)]).then_inc(misc_free[k], 1)
                for c in range(4):
                    act.wait_ge(misc_full[c % 2], USES[c % 2] * b + QK + c // 2 + 1)
                    act.wait_ge(spill[c // 2], 32 * b)
                    act.activation(qk_hi[:, c, :], ps[:, MISC[c % 2], :], ACT.Copy).then_inc(hi_done, 1)
                act.wait_ge(pv_done, 4 * NG * b)
                act.wait_ge(consts, 3)
                for m in range(2):
                    act.wait_ge(misc_full[m], USES[m] * b + VV + 1)
                    act.activation(v_ext[:, 2 * m:2 * m + 2, :, 0:HD],
                                   ps[:, MISC[m], :].rearrange("p (j h d) -> p j h d", j=2, d=HD), ACT.Copy).then_inc(misc_free[m], 1)

                def neg_max_hi(g):
                    act.wait_ge(misc_full[0], USES[0] * b + GRP + g + 1)
                    act.wait_ge(maxrow[g % 2], 64 * b + 32 * (g // 2))
                    act.activation(max_hi[:, g % 2, :], ps[0:G, MISC[0], :], ACT.Copy, scale=-1.0).then_inc(neg_hi, 1)

                neg_max_hi(0)
                neg_max_hi(1)
                for g in range(NG):
                    for u in range(16 * g, 16 * g + 16):
                        act.wait_ge(st_full, 64 * b + u + 1)
                        if u % 4 == 0:
                            act.wait_ge(pv_done, 16 * b + max(u // 4 - 1, 0))
                        act.activation(probs[:, u % 8, :], ps[:, ST[u % 3], :], ACT.Exp).then_inc(exp_done, 1)
                    act.wait_ge(pv_done, 16 * b + 4 * g + 4)
                    act.activation(oT_raw[:, :], ps[:, O, :], ACT.Copy).then_inc(o_free, 1)
                    if g + 2 < NG:
                        neg_max_hi(g + 2)
                for k in range(KD):
                    act.wait_ge(misc_full[k], USES[k] * b + OT + 1)
                    act.activation(oT[:, k, :], ps[:, MISC[k], :], ACT.Copy).then_inc(misc_free[k], 1)
                for k in range(KD):
                    act.wait_ge(misc_full[k], USES[k] * b + TP2 + 1)
                    act.activation(h2T[:, bass.ds(k * B * S + b * S, S)], ps[:, MISC[k], :], ACT.Copy).then_inc(misc_free[k], 1)
                act.wait_ge(misc_full[0], USES[0] * b + RT + 1)
                act.activation(lgT[:, :], ps[0:E + 1, MISC[0], :], ACT.Copy).then_inc(misc_free[0], 1)
                act.wait_ge(misc_full[1], USES[1] * b + RT + 1)
                act.activation(lg[:, :, :], ps[:, MISC[1], 0:TJ * 64].rearrange("p (j e) -> p j e", j=TJ)[:, :, 0:E + 1],
                               ACT.Copy).then_inc(misc_free[1], 1)
                act.wait_ge(ex_in, 2 * b + 2)
                act.activation(ex[:, :, :], ex[:, :, :], ACT.Exp).then_inc(ex_out, 1)
                act.activation(sgt[:, :], lg[:, :, E], ACT.Exp, scale=-1.0).then_inc(ex_out, 1)
            for b in range(B):
                for c in range(4):
                    u = 4 * b + c
                    act.wait_ge(gu_full, 2 * u + 1)
                    if u >= 2:
                        act.wait_ge(shh_s, u - 1)
                    act.activation(sh_silu[:, u % 2, :], ps[:, 2 * (u % 2), :], ACT.Silu).then_inc(silu_s, 1)
            with act.Fori(0, MT // 4, 1) as i:
                for r in range(4):
                    act.wait_ge(u_full, 4 * i + r + 1)
                    act.wait_ge(hid_s, 4 * i + max(r - 1, 0))
                    act.activation(e_silu[:, r % 2, :], ps[:, 2 + r % 2, 0:DM], ACT.Silu).then_inc(esilu_s, 1)
                    act.wait_ge(ht_full, 4 * i + r + 1)
                    act.wait_ge(y_full, 4 * i + max(r - 1, 0))
                    act.activation(e_hidT[:, r % 2, :], ps[0:DM, 4 + r % 2, 0:P], ACT.Copy).then_inc(ht_done, 1)
                    act.wait_ge(y_full, 4 * i + r + 1)
                    act.wait_ge(y_out[r], 16 * i)
                    act.activation(y_sb[:, r, :], ps[:, 6 + r % 2, 0:D], ACT.Copy).then_inc(y_done, 1)
            for t in range(NT):
                act.wait_ge(x3_done, t + 1)
                b, j = divmod(t, TJ)
                act.dma_start(out[b, j * P:(j + 1) * P, :], x[:, t * D:(t + 1) * D]).then_inc(stored, 16)
            act.wait_ge(stored, 16 * NT)

        @block.tensor
        def _(pe):
            pe.wait_ge(mod_ld, 32)
            pe.wait_ge(c_rep_s, 1)
            for c in range(2 * KD):
                for k in range(KD):
                    mm = pe.matmul(ps[:, 0, c * B:(c + 1) * B], wmod[:, k, c * P:(c + 1) * P], c_rep[:, k, :, 0],
                                   start=(k == 0), stop=(k == KD - 1))
            mm.then_inc(mod_ps, 1)
            for b in range(B):
                for s in range(2):
                    u = 2 * b + s
                    if u >= 6:
                        pe.wait_ge(mod_free, u - 5)
                    for k in range(KD):
                        mm = pe.matmul(ps[:, 2 + u % 6, :], c_rep[:, k, b, :], wmod[:, k, (2 + 2 * s) * D:(4 + 2 * s) * D],
                                       start=(k == 0), stop=(k == KD - 1))
                    mm.then_inc(mod_ps, 1)
            pe.wait_ge(consts, 3)
            pe.wait_ge(mod_free, 2 * B)
            pe.wait_ge(w_ld, 80)
            with pe.Fori(0, B, 1) as b:
                def misc(m, use):
                    pe.wait_ge(misc_free[m], USES[m] * b + use)

                pe.wait_ge(xn_ready, TJ * b + TJ)
                for k in range(KD):
                    misc(k, TP1)
                    for j in range(TJ):
                        mm = pe.transpose(ps[:, MISC[k], j * P:(j + 1) * P], xn[:, j, k * P:(k + 1) * P], ident[:, :])
                    mm.then_inc(misc_full[k], 1)
                pe.wait_ge(misc_free[0], USES[0] * b + TP1 + 1)
                pe.wait_ge(misc_free[1], USES[1] * b + TP1 + 1)
                for c in range(4):
                    misc(c % 2, QK + c // 2)
                    w = (wq_sb, wk_sb)[c % 2]
                    for k in range(KD):
                        mm = pe.matmul(ps[:, MISC[c % 2], :], w[:, k, (c // 2) * P:(c // 2 + 1) * P], hT[:, k, :],
                                       start=(k == 0), stop=(k == KD - 1))
                    mm.then_inc(misc_full[c % 2], 1)
                for j in range(TJ):
                    if j % 2 == 0:
                        misc(j // 2, VV)
                    for k in range(KD):
                        mm = pe.matmul(ps[:, MISC[j // 2], (j % 2) * D:(j % 2 + 1) * D], hT[:, k, j * P:(j + 1) * P],
                                       wv_sb[:, k, :], start=(k == 0), stop=(k == KD - 1))
                    if j % 2:
                        mm.then_inc(misc_full[j // 2], 1)

                def score(g, n):
                    qt, i = divmod(n, G)
                    u = 16 * g + n
                    h = G * g + i
                    pe.wait_ge(max_done, 64 * b + max(u - 1, 0))
                    pe.matmul(ps[:, SC[u % 2], :], q_stack[0:64, h, qt * P:(qt + 1) * P], k_stack[0:64, h, :],
                              start=True, stop=True).then_inc(sc_full, 1)

                def turn_max(g):
                    pe.wait_ge(max_done, 64 * b + 16 * g + 16)
                    misc(0, GRP + g)
                    for qt in range(TJ):
                        mm = pe.transpose(ps[0:G, MISC[0], qt * P:(qt + 1) * P], max_q[:, g % 2, qt, :], ident[:, :])
                    mm.then_inc(misc_full[0], 1)

                def scoreT(g, n):
                    kt, i = divmod(n, G)
                    u = 16 * g + n
                    h = G * g + i
                    pe.wait_ge(exp_done, 64 * b + max(u - 2, 0))
                    pe.matmul(ps[:, ST[u % 3], :], k_stack[:, h, kt * P:(kt + 1) * P], q_stack[:, h, :],
                              start=True, stop=True).then_inc(st_full, 1)

                def values(g, kt):
                    pe.wait_ge(exp_done, 64 * b + 16 * g + 4 * kt + 4)
                    if kt == 0:
                        pe.wait_ge(o_free, NG * b + g)
                    for i in range(G):
                        mm = pe.matmul(ps[32 * i:32 * i + 32, O, :], v_ext[:, kt, G * g + i, :],
                                       probs[:, (4 * kt + i) % 8, :], start=(kt == 0), stop=(kt == TJ - 1),
                                       tile_position=(0, 32 * i))
                    mm.then_inc(pv_done, 1)

                for g in range(2):
                    if g == 0:
                        pe.wait_ge(stack_ld[0], 128 * b + 128)
                    for n in range(16):
                        score(g, n)
                    turn_max(g)
                pe.wait_ge(stack_ld[1], 128 * b + 128)
                pe.wait_ge(misc_free[0], USES[0] * b + VV + 1)
                pe.wait_ge(misc_free[1], USES[1] * b + VV + 1)
                for g in range(NG):
                    pe.wait_ge(maxrow[g % 2], 64 * b + 32 * (g // 2) + 32)
                    for kt in range(TJ):
                        for i in range(G):
                            scoreT(g, G * kt + i)
                            if g + 2 < NG:
                                score(g + 2, G * kt + i)
                        if kt:
                            values(g, kt - 1)
                    values(g, TJ - 1)
                    if g + 2 < NG:
                        turn_max(g + 2)
                    pe.wait_ge(o_free, NG * b + g + 1)
                    misc(1, GRP + g)
                    for qt in range(TJ):
                        mm = pe.transpose(ps[:, MISC[1], qt * P:(qt + 1) * P], oT_raw[:, qt * P:(qt + 1) * P], ident[:, :])
                    mm.then_inc(misc_full[1], 1)
                pe.wait_ge(misc_free[1], USES[1] * b + GRP + NG)
                for k in range(KD):
                    misc(k, OT)
                    for j in range(TJ):
                        mm = pe.transpose(ps[:, MISC[k], j * P:(j + 1) * P], o_norm[:, j, k * P:(k + 1) * P], ident[:, :])
                    mm.then_inc(misc_full[k], 1)
                for j in range(TJ):
                    if j % 2 == 0:
                        misc(0, WO)
                        misc(1, WO)
                    for k in range(KD):
                        mm = pe.matmul(ps[:, MISC[j // 2], (j % 2) * D:(j % 2 + 1) * D], oT[:, k, j * P:(j + 1) * P],
                                       wo_g[:, bass.ds(b * (KD * D) + k * D, D)], start=(k == 0), stop=(k == KD - 1))
                    if j % 2:
                        mm.then_inc(misc_full[j // 2], 1)
                pe.wait_ge(h2_ready, b + 1)
                for k in range(KD):
                    misc(k, TP2)
                    for j in range(TJ):
                        mm = pe.transpose(ps[:, MISC[k], j * P:(j + 1) * P], h2[:, j, k * P:(k + 1) * P], ident[:, :])
                    mm.then_inc(misc_full[k], 1)
                pe.wait_ge(misc_free[0], USES[0] * b + RT)
                pe.wait_ge(misc_free[1], USES[1] * b + RT)
                for k in range(KD):
                    mm = pe.matmul(ps[0:E + 1, MISC[0], :], gate_sb[:, k, :], h2T[:, bass.ds(b * S + k * B * S, S)],
                                   start=(k == 0), stop=(k == KD - 1))
                mm.then_inc(misc_full[0], 1)
                pe.wait_ge(misc_free[0], USES[0] * b + RT + 1)
                apart(pe)
                for j in range(TJ):
                    mm = pe.transpose(ps[:, MISC[1], 64 * j:64 * j + E + 1], lgT[:, j * P:(j + 1) * P],
                                      ident[0:E + 1, 0:E + 1])
                mm.then_inc(misc_full[1], 1)
                pe.wait_ge(chosen_s, b + 1)
                pe.matmul(ps[:, MISC[0], 0:TJ * E], upper[:, :], chosen[:, :, :], start=True, stop=False)
                pe.matmul(ps[:, MISC[0], 0:TJ * E], ones[:, :], before[:, 0:TJ, :],
                          start=False, stop=True).then_inc(misc_full[0], 1)
            pe.wait_ge(misc_free[0], USES[0] * B)
            pe.wait_ge(misc_free[1], USES[1] * B)
            pe.matmul(ps[:, 6, 0:E], ones[:, :], before[:, TJ, :], start=True, stop=True).then_inc(cnt_ps, 1)
            pe.wait_ge(tcol_s, 1)
            for c in range(2):
                mm = pe.matmul(ps[0:1, 7, c * P:(c + 1) * P], tcol2[:, c:c + 1], ident[:, :], start=True, stop=True)
            mm.then_inc(tab_ps, 1)
            pe.wait_ge(sh_ld, 48)
            for b in range(B):
                for c in range(4):
                    u = 4 * b + c
                    if u >= 2:
                        pe.wait_ge(shh_s, u - 1)
                    for w, bank in ((sgate_sb, 0), (sup_sb, 1)):
                        for k in range(KD):
                            mm = pe.matmul(ps[:, 2 * (u % 2) + bank, :], w[:, k, c * P:(c + 1) * P],
                                           h2T[:, k * B * S + b * S:k * B * S + (b + 1) * S], start=(k == 0), stop=(k == KD - 1))
                        mm.then_inc(gu_full, 1)
                pe.wait_ge(shh_s, 4 * b + 4)
                for j in range(TJ):
                    n = TJ * b + j
                    if n >= 2:
                        pe.wait_ge(sd_free, n - 1)
                    for c in range(4):
                        mm = pe.matmul(ps[:, 4 + n % 2, 0:D], sh_hidT[:, c, j * P:(j + 1) * P], sdown_sb[:, c, :],
                                       start=(c == 0), stop=(c == 3))
                    mm.then_inc(sd_full, 1)
            pe.wait_ge(up_ld, 48)
            pe.wait_ge(tab_s, 1)
            pe.wait_ge(sd_free, NT)

            def turn(i, r):
                pe.wait_ge(xe_ld[r % XR], 16 * i + 16)
                pe.wait_ge(t_done, 4 * i + max(r - 1, 0))
                for k in range(KD):
                    mm = pe.transpose(ps[:, r % 2, k * P:(k + 1) * P], xe[:, r, k * P:(k + 1) * P], ident[:, :])
                mm.then_inc(t_full, 1)

            def widen(i, r, e):
                pe.wait_ge(t_done, 4 * i + r + 1)
                pe.wait_ge(hid_s, 4 * i + max(r - 1, 0))
                for k in range(KD):
                    mm = pe.matmul(ps[:, 2 + r % 2, 0:2 * DM], xeT[:, r % 2, k * P:(k + 1) * P],
                                   up_sb[:, bass.ds(e * (2 * DM) + k * E * 2 * DM, 2 * DM)], start=(k == 0), stop=(k == KD - 1))
                mm.then_inc(u_full, 1)

            def turn_hidden(i, r):
                pe.wait_ge(hid_s, 4 * i + r + 1)
                pe.wait_ge(ht_done, 4 * i + max(r - 1, 0))
                pe.transpose(ps[0:DM, 4 + r % 2, 0:P], e_hid[:, r % 2, :], ident[:, :]).then_inc(ht_full, 1)

            def narrow(i, r, e):
                pe.wait_ge(ht_done, 4 * i + r + 1)
                pe.wait_ge(y_done, 4 * i + max(r - 1, 0))
                pe.matmul(ps[:, 6 + r % 2, 0:D], e_hidT[:, r % 2, :], down_sb[:, bass.ds(e * D, D)],
                          start=True, stop=True).then_inc(y_full, 1)

            with pe.Fori(0, MT // 4, 1) as i:
                es = [None] * 4
                for r in range(4):
                    es[r] = pe.value_load(tab[0:1, bass.ds(4 * i + r, 1)], min_val=0, max_val=E - 1)
                    turn(i, r)
                    widen(i, r, es[r])
                    if r:
                        turn_hidden(i, r - 1)
                        narrow(i, r - 1, es[r - 1])
                turn_hidden(i, 3)
                narrow(i, 3, es[3])

        @block.vector
        def _(dve):
            st = Steps(dve, dve_s)
            for t in range(NT):
                if t % TJ == 0:
                    dve.wait_ge(x_ld[t // TJ], 16)
                st.did(dve.bn_stats(bn[:, t, :], x[:, t * D:(t + 1) * D]))
            st.wait()
            for t in range(NT):
                ins = dve.bn_aggr(mv[:, 2 * t:2 * t + 2], bn[:, t, :])
            ins.then_inc(stats, 1)
            dve.wait_ge(c_exp, 1)
            st.then(dve.tensor_scalar(ctmp[:, :], ctmp[:, :], 1.0, None, ALU.add))
            st.then(dve.reciprocal(ctmp[:, :], ctmp[:, :]))
            st.then(dve.tensor_tensor(cT[:, :], cT[:, :], ctmp[:, :], ALU.mult))
            dve.tensor_copy(c_rep[:, :, :, :].rearrange("p k b n -> p (k b) n"),
                            cT[:, :].unsqueeze(2).to_broadcast([P, KD * B, P])).then_inc(c_rep_s, 1)
            dve.wait_ge(consts, 1)
            for to, of in ((iota_ef, iota_e), (base_f, base_i), (thr_f, thr_i), (tile_f, tile_i)):
                st.did(dve.tensor_copy(to[:, :], of[:, :]))
            dve.wait_ge(mod_ps, 1)
            st.did(dve.tensor_copy(modT[:, 0:KD * B], ps[:, 0, 0:KD * B]))
            st.did(dve.tensor_scalar(modT[:, KD * B:], ps[:, 0, KD * B:2 * KD * B], 1.0, None, ALU.add))
            dve.wait_ge(w_ld, 80)

            def guarded_gate(to, src):
                st.then(dve.tensor_scalar(gtmp[:, 0, :], src, 0.0, 2.0, ALU.is_ge, ALU.mult))
                st.then(dve.tensor_scalar(gtmp[:, 0, :], gtmp[:, 0, :], -1.0, None, ALU.add))
                st.then(dve.tensor_tensor(gtmp[:, 1, :], src, gtmp[:, 0, :], ALU.mult))
                st.then(dve.scalar_tensor_tensor(out=to, in0=gtmp[:, 1, :], scalar=0.25, in1=gtmp[:, 0, :],
                                                 op0=ALU.max, op1=ALU.mult))

            for b in range(B):
                m = 3 * D * b
                u = 2 * b
                bank = ps[:, 2 + u % 6, :]
                dve.wait_ge(mod_ps, u + 2)
                guarded_gate(gtmp[:, 0, :], bank[:, 0:D])
                for k in range(KD):
                    st.did(dve.tensor_tensor(wo_g[:, (b * KD + k) * D:(b * KD + k + 1) * D], wo_sb[:, k, :], gtmp[:, 0, :], ALU.mult))
                st.wait()
                dve.tensor_copy(mod_b[:, m:m + D], bank[:, D:2 * D]).then_inc(mod_free, 1)
                u += 1
                bank = ps[:, 2 + u % 6, :]
                dve.wait_ge(mod_ps, u + 2)
                guarded_gate(mod_b[:, m + 2 * D:m + 3 * D], bank[:, D:2 * D])
                dve.tensor_scalar(mod_b[:, m + D:m + 2 * D], bank[:, 0:D], 1.0, None, ALU.add).then_inc(mod_free, 1)
            dve.wait_ge(mod_free, 2 * B)
            dve.wait_ge(rstd_s, 1)
            with dve.Fori(0, B, 1) as b:
                st.enter(b, 39)
                dve.wait_ge(misc_free[1], USES[1] * b)
                for j in range(TJ):
                    t = TJ * b + j
                    dve.tensor_scalar(xn[:, j, :], x[:, bass.ds(t * D, D)], mv[:, bass.ds(t * 2, 1)],
                                      rstd[:, bass.ds(t, 1)], ALU.subtract, ALU.mult).then_inc(xn_ready, 1)
                for c in range(4):
                    dve.wait_ge(hi_done, 4 * b + c + 1)
                    dve.tensor_tensor(qk_lo[:, c, :], ps[:, MISC[c % 2], :], qk_hi[:, c, :].bitcast(F32),
                                      ALU.subtract).then_inc(misc_free[c % 2], 1)

                def score_max(g, n):
                    qt, i = divmod(n, G)
                    u = 16 * g + n
                    dve.wait_ge(sc_full, 64 * b + u + 1)
                    dve.tensor_reduce(max_q[:, g % 2, qt, i:i + 1], ps[:, SC[u % 2], :], AXX, ALU.max).then_inc(max_done, 1)

                def neg_max_lo(g):
                    dve.wait_ge(neg_hi, NG * b + g + 1)
                    dve.scalar_tensor_tensor(out=max_lo[:, g % 2, :], in0=ps[0:G, MISC[0], :], scalar=-1.0,
                                             in1=max_hi[:, g % 2, :].bitcast(F32), op0=ALU.mult,
                                             op1=ALU.subtract).then_inc(misc_free[0], 1)

                for g in range(2):
                    for n in range(16):
                        score_max(g, n)
                    neg_max_lo(g)
                for g in range(NG):
                    if g + 2 < NG:
                        for n in range(16):
                            score_max(g + 2, n)
                        neg_max_lo(g + 2)
                    dve.wait_ge(misc_full[1], USES[1] * b + GRP + g + 1)
                    heads = ps[:, MISC[1], :].rearrange("p (q i d) -> p q i d", q=TJ, i=G)
                    st.then(dve.reciprocal(rsum[:, :, :], heads[:, :, :, HD]))
                    dve.tensor_tensor(o_norm[:, :, G * HD * g:G * HD * (g + 1)].rearrange("p q (i d) -> p q i d", i=G),
                                      heads[:, :, :, 0:HD], rsum[:, :, :].unsqueeze(3).to_broadcast([P, TJ, G, HD]),
                                      ALU.mult).then_inc(misc_free[1], 1)
                for m in range(2):
                    dve.wait_ge(misc_full[m], USES[m] * b + WO + 1)
                    two = x[:, bass.ds(b * (TJ * D) + 2 * m * D, 2 * D)]
                    dve.tensor_tensor(two, ps[:, MISC[m], :], two, ALU.add).then_inc(misc_free[m], 1)
                for m in range(2):
                    dve.wait_ge(misc_free[m], USES[m] * b + WO + 1)
                apart(dve)
                for j in range(TJ):
                    st.did(dve.bn_stats(bn[:, j, :], x[:, bass.ds((TJ * b + j) * D, D)]))
                st.wait()
                apart(dve)
                for j in range(TJ):
                    ins = dve.bn_aggr(mv2[:, j, :], bn[:, j, :])
                ins.then_inc(stats2, 1)
                dve.wait_ge(rstd2_s, b + 1)
                dve.wait_ge(disp, 16 * NT * b)
                for j in range(TJ):
                    st.did(dve.tensor_scalar(h2[:, j, 0:D], x[:, bass.ds((TJ * b + j) * D, D)], mv2[:, j, 0:1],
                                             rstd2[:, j:j + 1], ALU.subtract, ALU.mult))
                st.wait()
                st.then(dve.tensor_tensor(h2[:, :, 0:D], h2[:, :, 0:D],
                                          mod_b[:, bass.ds(b * (3 * D) + D, D)].unsqueeze(1).to_broadcast([P, TJ, D]), ALU.mult))
                dve.tensor_tensor(h2[:, :, 0:D], h2[:, :, 0:D],
                                  mod_b[:, bass.ds(b * (3 * D), D)].unsqueeze(1).to_broadcast([P, TJ, D]), ALU.add).then_inc(h2_ready, 1)
                dve.wait_ge(misc_free[1], USES[1] * b + RT + 1)
                apart(dve)
                for j in range(TJ):
                    st.did(dve.max(v8[:, j, :], lg[:, j, 0:E]))
                st.wait()
                apart(dve)
                for j in range(TJ):
                    st.did(dve.max_index(i8[:, j, :], v8[:, j, :], lg[:, j, 0:E]))
                top = v8[:, :, 0:1]
                dve.tensor_tensor(ex[:, :, 0:E], lg[:, :, 0:E], top.to_broadcast([P, TJ, E]), ALU.subtract).then_inc(ex_in, 1)
                dve.tensor_tensor(ex[:, :, E:E + TOPK], v8[:, :, 0:TOPK], top.to_broadcast([P, TJ, TOPK]),
                                  ALU.subtract).then_inc(ex_in, 1)
                st.wait()
                st.then(dve.tensor_copy(e4[:, :, :], i8[:, :, 0:TOPK]))
                st.then(dve.tensor_tensor(onehot[:, :, :], iota_ef[:, :].unsqueeze(1).to_broadcast([P, TJ * TOPK, E]),
                                          e4[:, :, :].rearrange("p j k -> p (j k)").unsqueeze(2).to_broadcast([P, TJ * TOPK, E]),
                                          ALU.is_equal))
                st.did(dve.tensor_copy(before[:, 0, :], before[:, TJ, :]))
                st.then(dve.tensor_reduce(chosen[:, :, :], onehot[:, :, :].rearrange("p (j k) e -> p j e k", k=TOPK), AXX, ALU.add))
                for j in range(TJ - 1):
                    st.then(dve.tensor_tensor(before[:, j + 1, :], before[:, j, :], chosen[:, j, :], ALU.add))
                dve.tensor_tensor(before[:, TJ, :], before[:, TJ - 1, :], chosen[:, TJ - 1, :], ALU.add).then_inc(chosen_s, 1)
                dve.wait_ge(ex_out, 2 * b + 2)
                st.then(dve.tensor_reduce(z4[:, :], ex[:, :, 0:E], AXX, ALU.add))
                st.then(dve.reciprocal(z4[:, :], z4[:, :]))
                st.then(dve.tensor_tensor(p4[:, :, :], ex[:, :, E:E + TOPK], z4[:, :].unsqueeze(2).to_broadcast([P, TJ, TOPK]), ALU.mult))
                st.then(dve.tensor_reduce(s4[:, :], p4[:, :, :], AXX, ALU.add))
                st.then(dve.tensor_scalar(s4[:, :], s4[:, :], 1e-20, None, ALU.add))
                st.then(dve.reciprocal(s4[:, :], s4[:, :]))
                st.did(dve.tensor_tensor(w4[:, :, :], p4[:, :, :], s4[:, :].unsqueeze(2).to_broadcast([P, TJ, TOPK]), ALU.mult))
                st.then(dve.tensor_scalar(sgt[:, :], sgt[:, :], 1.0, None, ALU.add))
                st.did(dve.reciprocal(sg[:, bass.ds(b * TJ, TJ)], sgt[:, :]))
                st.wait()
                dve.wait_ge(misc_full[0], USES[0] * b + RK + 1)
                dve.tensor_tensor(rank[:, :, :], ps[:, MISC[0], 0:TJ * E].rearrange("p (j e) -> p j e", e=E),
                                  base_f[:, :].unsqueeze(1).to_broadcast([P, TJ, E]), ALU.add).then_inc(misc_free[0], 1)
                dve.wait_ge(misc_free[0], USES[0] * b + RK + 1)
                st.then(dve.tensor_tensor(picked[:, :, :].rearrange("p (j k) e -> p j k e", k=TOPK),
                                          onehot[:, :, :].rearrange("p (j k) e -> p j k e", k=TOPK),
                                          rank[:, :, :].unsqueeze(2).to_broadcast([P, TJ, TOPK, E]), ALU.mult))
                st.then(dve.tensor_reduce(slot_f[:, :], picked[:, :, :], AXX, ALU.add))
                dve.tensor_copy(slot_i[:, :], slot_f[:, :]).then_inc(slots_s, 1)
            st.leave(B)
            dve.wait_ge(cnt_ps, 1)
            st.then(dve.tensor_copy(cnt[:, :], ps[:, 6, 0:E]))
            st.did(dve.tensor_tensor(pad_at[:, :], base_f[:, :], cnt[:, :], ALU.add))
            over = picked[:, :, :].rearrange("p a e -> p (a e)").rearrange("p (e r) -> p e r", r=NT)
            st.then(dve.tensor_tensor(over, cnt[:, :].unsqueeze(2).to_broadcast([P, E, NT]),
                                      thr_f[:, :].unsqueeze(1).to_broadcast([P, E, NT]), ALU.is_gt))
            st.then(dve.tensor_reduce(ntile[:, :], over, AXX, ALU.add))
            st.then(dve.tensor_tensor_scan(ctile[:, :], ones[:, 0:E], ntile[:, :], 0.0, ALU.mult, ALU.add))
            st.then(dve.tensor_scalar(past[:, :], ctile[:, :], tile_f[:, 0:1], None, ALU.is_le))
            st.did(dve.tensor_reduce(tcol[:, 0:1], past[:, :], AXX, ALU.add))
            st.then(dve.tensor_tensor(past_n[:, :], past[:, :], ntile[:, :], ALU.mult))
            st.then(dve.tensor_reduce(tcol[:, 1:2], past_n[:, :], AXX, ALU.add))
            st.did(dve.tensor_tensor(tcol[:, 2:3], tile_f[:, :], tcol[:, 1:2], ALU.subtract))
            st.did(dve.tensor_scalar(tcol[:, 3:4], tcol[:, 0:1], float(CAP), None, ALU.mult))
            st.then(dve.tensor_scalar(tcol2[:, 0:1], tcol[:, 0:1], float(E - 1), None, ALU.min))
            st.then(dve.scalar_tensor_tensor(out=tcol[:, 1:2], in0=tcol[:, 2:3], scalar=float(P), in1=tcol[:, 3:4],
                                             op0=ALU.mult, op1=ALU.add))
            dve.tensor_scalar(tcol2[:, 1:2], tcol[:, 1:2], float(E * CAP), None, ALU.min).then_inc(tcol_s, 1)
            dve.wait_ge(tab_ps, 1)
            dve.tensor_copy(tab[:, :], ps[0:1, 7, 0:2 * P]).then_inc(tab_s, 1)
            for b in range(B):
                for c in range(4):
                    u = 4 * b + c
                    dve.wait_ge(gu_full, 2 * u + 2)
                    dve.wait_ge(silu_s, u + 1)
                    if b:
                        dve.wait_ge(sd_full, TJ * b)
                    dve.tensor_tensor(sh_hidT[:, c, :], ps[:, 2 * (u % 2) + 1, :], sh_silu[:, u % 2, :], ALU.mult).then_inc(shh_s, 1)
                for j in range(TJ):
                    t = TJ * b + j
                    dve.wait_ge(sd_full, t + 1)
                    dve.scalar_tensor_tensor(out=gtmp[:, t % 2, :], in0=ps[:, 4 + t % 2, 0:D], scalar=sg[:, t:t + 1],
                                             in1=mod_b[:, (3 * b + 2) * D:(3 * b + 3) * D], op0=ALU.mult,
                                             op1=ALU.mult).then_inc(sd_free, 1)
                    dve.wait_ge(sd_free, t + 1)
                    st.did(dve.tensor_tensor(x[:, t * D:(t + 1) * D], x[:, t * D:(t + 1) * D], gtmp[:, t % 2, :], ALU.add))
            with dve.Fori(0, MT // 4, 1) as i:
                for r in range(4):
                    dve.wait_ge(t_full, 4 * i + r + 1)
                    dve.wait_ge(u_full, 4 * i + max(r - 1, 0))
                    dve.tensor_copy(xeT[:, r % 2, :], ps[:, r % 2, 0:KD * P]).then_inc(t_done, 1)
                    dve.wait_ge(esilu_s, 4 * i + r + 1)
                    dve.wait_ge(ht_full, 4 * i + max(r - 1, 0))
                    dve.scalar_tensor_tensor(out=e_hid[:, r % 2, :], in0=ps[:, 2 + r % 2, DM:2 * DM],
                                             scalar=xe[:, r, D + 1:D + 2], in1=e_silu[:, r % 2, :], op0=ALU.mult,
                                             op1=ALU.mult).then_inc(hid_s, 1)
            st.wait()
            for t in range(NT):
                b = t // TJ
                dve.wait_ge(comb_ld[t % 4], 16 * (t // 4) + 16)
                st.then(dve.tensor_reduce(gtmp[:, t % 2, :], comb[:, t % 4, :].rearrange("p (k d) -> p d k", k=TOPK), AXX, ALU.add))
                st.then(dve.tensor_tensor(gtmp[:, t % 2, :], gtmp[:, t % 2, :], mod_b[:, (3 * b + 2) * D:(3 * b + 3) * D], ALU.mult))
                dve.tensor_tensor(x[:, t * D:(t + 1) * D], x[:, t * D:(t + 1) * D], gtmp[:, t % 2, :], ALU.add).then_inc(x3_done, 1)


def kernel(**inputs):
    import numpy as _np
    import concourse.bacc as _bacc
    from concourse import mybir as _mybir
    from concourse.bass_utils import run_bass_kernel_spmd as _run

    i = {k[3:]: _np.asarray(v) for k, v in inputs.items()}
    arrays = {
        "x": i["attn_x"],
        "wq": i["attn_wq"].T, "wk": i["attn_wk"].T, "wv": i["attn_wv"].T, "wo": i["attn_wo"].T,
        "gate": _np.concatenate([i["ffn_gate_w"], i["ffn_shared_expert_gate_w"]], axis=0).T,
        "up": i["ffn_gate_up_proj"].transpose(2, 0, 1).reshape(D, E * 2 * DM),
        "down": i["ffn_down_proj"].transpose(2, 0, 1).reshape(DM, E * D),
        "sgate": i["ffn_shared_gate_w"].T, "sup": i["ffn_shared_up_w"].T, "sdown": i["ffn_shared_down_w"].T,
        "c": i["c"].T, "wmod": i["wmod"],
    }
    arrays = {f"in_{k}": _np.ascontiguousarray(v) for k, v in arrays.items()}
    nc = _bacc.Bacc("TRN2", target_bir_lowering=False, num_devices=1)
    args = [nc.dram_tensor(k, v.shape, _mybir.dt.from_np(v.dtype), kind="ExternalInput").ap() for k, v in arrays.items()]
    out = nc.dram_tensor("out", (B, S, D), _mybir.dt.float32, kind="ExternalOutput").ap()
    adaln_moe_kernel(nc, *args, out)
    r = _run(nc, [arrays], core_ids=[0])
    return r.results[0]["out"]
```

```python
from contextlib import ExitStack

import concourse.bass as bass
from concourse import mybir

ALU = mybir.AluOpType
ACT = mybir.ActivationFunctionType
AXX = mybir.AxisListType.X
F32 = mybir.dt.float32
F32R = mybir.dt.float32r
I32 = mybir.dt.int32
U32 = mybir.dt.uint32

P = 128
B, S, D = 4, 512, 256
H, HD = 16, 16
KD = D // P
TJ = S // P
NT = B * TJ
G = 4
NG = H // G
E, TOPK, DM, DS = 32, 4, 96, 512
CAP = B * S + P
MT = B * S * TOPK // P + E
ROW = D + 2
SKIP = 1 << 20
NY = B * S * TOPK
EPS = 1e-5
XR = 8
CR = 4
DVE_STEPS = 43


class Steps:

    def __init__(self, eng, sem):
        self.eng, self.sem, self.base, self.n = eng, sem, 0, 0

    def did(self, ins):
        ins.then_inc(self.sem, 1)
        self.n += 1

    def wait(self):
        self.eng.wait_ge(self.sem, self.base + self.n)

    def then(self, ins):
        self.did(ins)
        self.wait()

    def enter(self, i, per):
        self.total, self.base, self.n, self.per = self.n, self.n + i * per, 0, per

    def leave(self, turns):
        assert self.n == self.per, (self.n, self.per)
        self.base, self.n = 0, self.total + turns * self.per


class Turn:

    ORDER = (
        ("MAX0", "att"), ("TP0", "pre"), ("TP1", "pre"), ("OUT3", "post"), ("MOD0", "mod"), ("QK0", "pre"), ("OT0", "post"), ("OT1", "post"),
        ("QK1", "pre"), ("WO0", "post"), ("MOD1", "mod"), ("QK2", "pre"), ("WO1", "post"), ("QK3", "pre"),
        ("MAX1", "att"), ("OUT0", "att"), ("V0", "pre"), ("V1", "pre"), ("MOD2", "mod"), ("HT0", "post"), ("HT1", "post"),
        ("MOD3", "mod"), ("LOG", "post"), ("LGT", "post"), ("SG0", "post"), ("SU0", "post"),
        ("MAX2", "att"), ("SG1", "post"), ("OUT1", "att"), ("SU1", "post"), ("RANK", "post"), ("MOD4", "mod"), ("SG2", "post"),
        ("MOD5", "mod"), ("SU2", "post"),
        ("MAX3", "pre"), ("SG3", "post"), ("OUT2", "att"), ("SU3", "post"), ("MOD6", "mod"), ("SD0", "post"), ("MOD7", "mod"), ("SD1", "post"))

    def __init__(self, b, kinds, before, loop_from=None):
        self.b, self.kinds = b, kinds
        self.att, self.pre, self.post, self.mod = ("att" in kinds, "pre" in kinds, "post" in kinds, "mod" in kinds)
        self.uses, self.count = {}, [0, 0]
        for n, name in enumerate(name for name, kind in self.ORDER if kind in kinds):
            self.uses[name] = (n % 2, self.count[n % 2])
            self.count[n % 2] += 1
        self.base = list(before) if loop_from is None else [
            before[m] + (b - loop_from) * self.count[m] for m in range(2)]

    def use(self, name):
        m, n = self.uses[name]
        return m, self.base[m] + n


def adaln_moe_kernel(nc, x_in, wq, wk, wv, wo, gate, up, down, sgate, sup, sdown, c_in, wmod_in, out):
    ctx = ExitStack()
    with ctx:
        def sb(name, shape, dt=F32):
            return ctx.enter_context(nc.sbuf_tensor(name, shape, dt))

        def sem(name):
            return ctx.enter_context(nc.semaphore(name))

        def overlay(first, second):
            made, ends = [], []
            for specs in (first, second):
                with ExitStack() as here:
                    for name, shape, dt in specs:
                        made.append(here.enter_context(nc.sbuf_tensor(name, shape, dt)))
                    ends.append(nc.sbuf_base)
            sb(f"{first[0][0]}_{second[0][0]}", [P, max(ends) - nc.sbuf_base], mybir.dt.uint8)
            return made

        q_stack, k_stack, probs, up_sb, down_sb = overlay(
            [("q_stack", [P, H, S], F32R), ("k_stack", [P, H, S], F32R), ("probs", [P, 2 * G, S], F32)],
            [("up_sb", [P, KD * E * 2 * DM], F32), ("down_sb", [DM, E * D], F32)])
        comb = up_sb[:, 0:CR * TOPK * D].rearrange("p (r n) -> p r n", r=CR)
        wmod, c_rep, wo_sb, h2, sh_tanh, onehot, picked, lgT, ex, rank, chosen = overlay(
            [("wmod", [P, KD, 6 * D], F32), ("c_rep", [P, KD, B, P], F32), ("wo_sb", [P, KD, D], F32)],
            [("h2", [P, TJ, ROW], F32), ("sh_tanh", [P, 2, S], F32), ("onehot", [P, TJ * TOPK, E], F32),
             ("picked", [P, TJ * TOPK, E], F32), ("lgT", [E + 1, S], F32), ("ex", [P, TJ, E + TOPK], F32),
             ("rank", [P, TJ, E], F32), ("chosen", [P, TJ, E], F32)])
        qk_hi, sh_hidT = overlay([("qk_hi", [P, 4, S], F32R)], [("sh_hidT", [P, 4, S], F32)])
        xn, qk_lo = overlay([("xn", [P, TJ, D], F32)], [("qk_lo", [P, 4, S], F32R)])
        v_ext, v_new, hT, oT_raw, max_hi, max_lo, xe, y_sb, xeT, e_silu, e_hid, e_hidT, tab, cnt, past, past_n = overlay(
            [("v_ext", [P, TJ, H, 32], F32), ("v_new", [P, TJ, H, HD], F32), ("hT", [P, KD, S], F32),
             ("oT_raw", [P, S], F32), ("max_hi", [G, S], F32R), ("max_lo", [G, S], F32R)],
            [("xe", [P, XR, ROW], F32), ("y_sb", [P, XR, D], F32), ("xeT", [P, 2, KD * P], F32), ("e_silu", [P, 2, DM], F32),
             ("e_hid", [P, 2, DM], F32), ("e_hidT", [DM, 2, P], F32), ("tab", [1, 2 * P], I32), ("cnt", [P, E], F32),
             ("past", [P, E], F32), ("past_n", [P, E], F32)])
        o_norm = sb("o_norm", [P, TJ, D])
        oT = sb("oT", [P, KD, S])
        h2T = oT

        x = sb("x", [P, NT * D])
        wq_sb, wk_sb, wv_sb = (sb(n, [P, KD, D]) for n in ("wq_sb", "wk_sb", "wv_sb"))
        wo_g = sb("wo_g", [P, B * KD * D])
        mod_b = sb("mod_b", [P, B * 3 * D])
        gate_sb = sb("gate_sb", [P, KD, E + 1])
        sgate_sb, sup_sb = (sb(n, [P, KD, DS]) for n in ("sgate_sb", "sup_sb"))
        sdown_sb = sb("sdown_sb", [P, DS // P, D])
        modT = sb("modT", [P, 2 * KD * B])
        ident, ones, upper = (sb(n, [P, P]) for n in ("ident", "ones", "upper"))
        cT = sb("cT", [P, KD * B])
        ctmp = sb("ctmp", [P, KD * B])
        gtmp = sb("gtmp", [P, 2, D])
        pad_rows = sb("pad_rows", [P, ROW])
        bn = sb("bn", [P, NT, 6])
        mv = sb("mv", [P, NT, 2])
        rstd = sb("rstd", [P, NT])
        nmr = sb("nmr", [P, NT])
        mv2 = sb("mv2", [P, TJ, 2])
        rstd2 = sb("rstd2", [P, TJ])
        veps = sb("veps", [P, NT])
        mhalf = sb("mhalf", [P, NT])
        max_q = sb("max_q", [P, 2, TJ, G])
        rsum = sb("rsum", [P, TJ, G])
        iota_e, base_i = sb("iota_e", [P, E], I32), sb("base_i", [P, E], I32)
        iota_ef, base_f = sb("iota_ef", [P, E]), sb("base_f", [P, E])
        thr_i, thr_f = sb("thr_i", [P, NT], I32), sb("thr_f", [P, NT])
        tile_i, tile_f = sb("tile_i", [P, 1], I32), sb("tile_f", [P, 1])
        home = sb("home", [P, NT * TOPK], I32)
        lg = sb("lg", [P, TJ, E + 1])
        v8 = sb("v8", [P, TJ, 8])
        i8 = sb("i8", [P, TJ, 8], U32)
        z4, s4, sgt = (sb(n, [P, TJ]) for n in ("z4", "s4", "sgt"))
        p4, w4, e4 = (sb(n, [P, TJ, TOPK]) for n in ("p4", "w4", "e4"))
        sg = sb("sg", [P, NT])
        before = sb("before", [P, TJ + 1, E])
        slot_f = sb("slot_f", [P, TJ * TOPK])
        slot_i = sb("slot_i", [P, TJ * TOPK], I32)
        ntile, ctile = sb("ntile", [P, E]), sb("ctile", [P, E])
        tcol = sb("tcol", [P, 4])
        tcol2 = sb("tcol2", [P, 2])
        pad_at = sb("pad_at", [P, E], I32)
        ps = ctx.enter_context(nc.psum_tensor("ps", [P, 8, 512], F32))

        scr = nc.dram_tensor("qk_scratch", [B * 8, P, S], F32, kind="Internal").ap()
        xs = nc.dram_tensor("dispatched", [E * CAP + P, ROW], F32, kind="Internal").ap()
        yk = nc.dram_tensor("results", [NY, D], F32, kind="Internal").ap()

        mod_ld, w_ld, sh_ld, up_ld = sem("mod_ld"), sem("w_ld"), sem("sh_ld"), sem("up_ld")
        x_ld = [sem(f"x_ld{i}") for i in range(B)]
        pool_s, dve_s, consts = sem("pool_s"), sem("dve_s"), sem("consts")
        c_exp, c_rep_s, stats, rstd_s, nmr_s, modT_ps, modT_s = (
            sem(n) for n in ("c_exp", "c_rep_s", "stats", "rstd_s", "nmr_s", "modT_ps", "modT_s"))
        xn_ready, hi_done = sem("xn_ready"), sem("hi_done")
        misc_full = [sem("misc0_full"), sem("misc1_full")]
        misc_free = [sem("misc0_free"), sem("misc1_free")]
        spill = [sem("spill0"), sem("spill1")]
        stack_ld = [sem(f"stack_ld{g}") for g in range(NG)]
        sc_full, max_done, neg_hi, maxrow = sem("sc_full"), sem("max_done"), sem("neg_hi"), sem("maxrow")
        st_full, exp_done, pv_done, o_free, v_in_place = (
            sem(n) for n in ("st_full", "exp_done", "pv_done", "o_free", "v_in_place"))
        stats2, rstd2_s, tanh_s = sem("stats2"), sem("rstd2_s"), sem("tanh_s")
        h2_ready, ex_in, ex_out, chosen_s, slots_s = (
            sem(n) for n in ("h2_ready", "ex_in", "ex_out", "chosen_s", "slots_s"))
        disp = [sem(f"disp{j}") for j in range(TJ)]
        cnt_ps, tcol_s, tab_ps, tab_s, pad_s = (sem(n) for n in ("cnt_ps", "tcol_s", "tab_ps", "tab_s", "pad_s"))
        xe_ld = [sem(f"xe_ld{i}") for i in range(XR)]
        t_full, t_done, u_full, esilu_s, hid_s, ht_full, ht_done, y_full, y_done = (
            sem(n) for n in ("t_full", "t_done", "u_full", "esilu_s", "hid_s", "ht_full", "ht_done", "y_full", "y_done"))
        y_out = [sem(f"y_out{i}") for i in range(XR)]
        comb_ld = [sem(f"comb_ld{i}") for i in range(CR)]
        part_s, x3_done, stored = sem("part_s"), sem("x3_done"), sem("stored")
        passed = sem("passed")

        SC, ST, O, MISC = (0, 1), (2, 3, 4), 5, (6, 7)

        LOOP0, LOOP1 = 1, B - 1
        lead = Turn(-1, {"pre"}, [0, 0])
        first = Turn(0, {"att", "pre", "mod"}, lead.count)
        at_loop = [lead.count[m] + first.count[m] for m in range(2)]

        def middle(b):
            return Turn(b, {"att", "pre", "post"}, at_loop, LOOP0)

        per_turn = middle(LOOP0).count
        last = Turn(B - 1, {"att", "post"}, [at_loop[m] + (LOOP1 - LOOP0) * per_turn[m] for m in range(2)])
        drain = Turn(B, {"post"}, [last.base[m] + last.count[m] for m in range(2)])
        all_uses = [drain.base[m] + drain.count[m] for m in range(2)]

        def apart(eng):
            eng.sem_inc(passed, 1)

        def full(eng, t, name):
            m, n = t.use(name)
            eng.wait_ge(misc_full[m], n + 1)
            return ps[:, MISC[m], :]

        def frees(ins, t, name):
            ins.then_inc(misc_free[t.use(name)[0]], 1)

        def own_free(eng, t, name):
            m, n = t.use(name)
            eng.wait_ge(misc_free[m], n + 1)

        def above(eng, sem_, value):
            if not isinstance(value, int) or value > 0:
                eng.wait_ge(sem_, value)

        block = ctx.enter_context(nc.Block())

        @block.sync
        def _(sp):
            sp.dma_start(cT[:, :].rearrange("p (k b) -> p k b", k=KD), c_in.rearrange("(k p) b -> p k b", p=P)).then_inc(mod_ld, 16)
            sp.dma_start(wmod[:, :, :], wmod_in.rearrange("(k p) n -> p k n", p=P)).then_inc(mod_ld, 16)
            for w_d, w_s in ((wq, wq_sb), (wk, wk_sb), (wv, wv_sb), (wo, wo_sb), (gate, gate_sb)):
                sp.dma_start(w_s[:, :, :], w_d.rearrange("(k p) n -> p k n", p=P)).then_inc(w_ld, 16)
            for w_d, w_s in ((sgate, sgate_sb), (sup, sup_sb), (sdown, sdown_sb)):
                sp.dma_start(w_s[:, :, :], w_d.rearrange("(k p) n -> p k n", p=P)).then_inc(sh_ld, 16)

            def spill_half(t, half):
                for c in (2 * half, 2 * half + 1):
                    m, n = t.use(f"QK{c}")
                    sp.wait_ge(misc_free[m], n + 1)
                    apart(sp)
                for comp, src in ((0, qk_hi), (1, qk_lo)):
                    sp.dma_start(scr[bass.ds(8 * (t.b + 1) + 4 * half + 2 * comp, 2), :, :].rearrange("q p n -> p q n"),
                                 src[:, 2 * half:2 * half + 2, :].bitcast(F32)).then_inc(spill[half], 16)

            def load_group(b, g):
                sp.wait_ge(spill[g // 2], 32 * b + 32)
                apart(sp)
                above(sp, pv_done, 16 * b + 4 * g - 12 if not isinstance(b, int) or b else 0)
                apart(sp)
                for r in range(4):
                    for qk, stack, comp in ((0, q_stack, r % 2), (1, k_stack, r // 2)):
                        rows = scr[bass.ds(8 * b + 4 * (g // 2) + 2 * comp + qk, 1), 64 * (g % 2):64 * (g % 2) + 64, :]
                        sp.dma_start(stack[16 * r:16 * r + 16, G * g:G * g + G, :].bitcast(F32),
                                     rows.rearrange("o (h d) n -> (o d) h n", d=HD)).then_inc(stack_ld[g], 16)

            def max_rows(t, g):
                sp.wait_ge(consts, 3)
                m, n = t.use(f"MAX{g}")
                sp.wait_ge(misc_free[m], n + 1)
                apart(sp)
                h = G * ((g + 1) % NG)
                for row, src in ((64, max_hi), (65, max_lo)):
                    sp.dma_start(q_stack[row:row + 1, h:h + G, :].bitcast(F32), src[:, :].bitcast(F32)).then_inc(maxrow, 16)

            def turn(t):
                max_rows(t, 0)
                load_group(t.b, 3)
                if t.pre:
                    spill_half(t, 0)
                    spill_half(t, 1)
                for g in (1, 2):
                    max_rows(t, g)
                    if t.pre:
                        load_group(t.b + 1, g - 1)
                if t.pre:
                    max_rows(t, 3)
                    load_group(t.b + 1, 2)

            for half in range(2):
                spill_half(lead, half)
                load_group(0, 2 * half)
                if half == 0:
                    load_group(0, 1)
            max_rows(lead, 3)
            turn(first)
            with sp.Fori(LOOP0, LOOP1, 1) as b:
                turn(middle(b))
            turn(last)
            sp.wait_ge(pv_done, 4 * NG * B)
            for k in range(KD):
                sp.dma_start(up_sb[:, k * E * 2 * DM:(k + 1) * E * 2 * DM],
                             up[k * P:(k + 1) * P, :]).then_inc(up_ld, 16)
            sp.dma_start(down_sb[:, :], down).then_inc(up_ld, 16)
            sp.wait_ge(tab_s, 1)
            sp.dma_start(xs[E * CAP:E * CAP + P, :], pad_rows[:, :]).then_inc(pad_s, 16)
            with sp.Fori(0, E, 1) as e:
                at = sp.value_load(pad_at[0:1, bass.ds(e, 1)], min_val=0, max_val=E * CAP)
                sp.dma_start(xs[bass.ds(at, P), :], pad_rows[:, :]).then_inc(pad_s, 16)
            sp.wait_ge(pad_s, 16 * (E + 1))
            for j in range(TJ):
                sp.wait_ge(disp[j], 16 * B * TOPK)

            def load_tile(n, r):
                at = sp.value_load(tab[0:1, bass.ds(P + n, 1)], min_val=0, max_val=E * CAP)
                sp.dma_start(xe[:, r, :], xs[bass.ds(at, P), :]).then_inc(xe_ld[r], 16)

            for r in range(XR):
                load_tile(r, r)
            with sp.Fori(1, MT // XR, 1) as i:
                for r in range(XR):
                    sp.wait_ge(y_out[r], 16 * i)
                    apart(sp)
                    load_tile(XR * i + r, r)
            for r in range(XR):
                sp.wait_ge(y_out[r], 16 * (MT // XR))
            for t in range(NT):
                if t >= CR:
                    sp.wait_ge(part_s, t - CR + 1)
                sp.dma_start(comb[:, t % CR, :], yk[t * P * TOPK:(t + 1) * P * TOPK, :].rearrange(
                    "(p k) d -> p (k d)", k=TOPK)).then_inc(comb_ld[t % CR], 16)

        @block.gpsimd
        def _(pool):
            st = Steps(pool, pool_s)
            st.did(pool.memset(ident[:, :], 0.0))
            st.did(pool.memset(ones[:, :], 1.0))
            st.did(pool.memset(upper[:, :], 1.0))
            st.did(pool.iota(iota_e[:, :], pattern=[[1, E]], base=0, channel_multiplier=0))
            st.did(pool.iota(base_i[:, :], pattern=[[CAP, E]], base=0, channel_multiplier=0))
            st.did(pool.iota(thr_i[:, :], pattern=[[P, NT]], base=0, channel_multiplier=0))
            st.did(pool.iota(tile_i[:, :], pattern=[[0, 1]], base=0, channel_multiplier=1))
            st.did(pool.iota(home[:, :], pattern=[[P * TOPK, NT], [1, TOPK]], base=0, channel_multiplier=TOPK))
            st.did(pool.memset(mhalf[:, :], -0.5))
            st.did(pool.memset(pad_rows[:, :], 0.0))
            st.did(pool.memset(before[:, TJ, :], 0.0))
            st.wait()
            st.did(pool.affine_select(out=ident[:, :], in_=ident[:, :], compare_op=ALU.not_equal, fill=1.0, base=0,
                                      pattern=[[-1, P]], channel_multiplier=1))
            st.did(pool.affine_select(out=upper[:, :], in_=upper[:, :], compare_op=ALU.is_gt, fill=0.0, base=0,
                                      pattern=[[1, P]], channel_multiplier=-1))
            st.did(pool.iota(pad_rows[:, D:D + 1].bitcast(I32), pattern=[[0, 1]], base=SKIP, channel_multiplier=0))
            st.wait()
            pool.sem_inc(consts, 1)

            def deviations(lo, hi, turn):
                pool.wait_ge(stats, turn)
                st.then(pool.tensor_scalar(veps[:, lo:hi], mv[:, lo:hi, 1], EPS, None, ALU.add))
                pool.tensor_tensor(rstd[:, lo:hi], veps[:, lo:hi], mhalf[:, lo:hi], ALU.pow).then_inc(rstd_s, 1)
                pool.wait_ge(rstd_s, turn)

            deviations(0, TJ, 1)
            pool.memset(v_ext[:, :, :, :], 1.0).then_inc(consts, 1)
            pool.wait_ge(consts, 2)
            st.then(pool.memset(k_stack[64:128, :, :].bitcast(F32), 0.0))
            st.then(pool.memset(k_stack[64:66, :, :].bitcast(F32), 1.0))
            pool.memset(q_stack[64:128, :, :].bitcast(F32), 0.0).then_inc(consts, 1)
            pool.wait_ge(consts, 3)
            deviations(TJ, NT, 2)

            def place_values(b, g, t):
                if t is not None:
                    m, n = t.use("V1")
                    pool.wait_ge(misc_free[m], n + 1)
                    apart(pool)
                above(pool, pv_done, 16 * b + 4 * g - 12 if not isinstance(b, int) or b else 0)
                apart(pool)
                pool.tensor_copy(v_ext[:, :, G * g:G * g + G, 0:HD], v_new[:, :, G * g:G * g + G, :]).then_inc(v_in_place, 1)
                pool.wait_ge(v_in_place, 4 * b + g + 1)
                apart(pool)

            def turn(t):
                place_values(t.b, 3, None)
                if t.post:
                    p = t.b - 1
                    pool.wait_ge(stats2, p + 1)
                    apart(pool)
                    st.then(pool.tensor_scalar(veps[:, 0:TJ], mv2[:, :, 1], EPS, None, ALU.add))
                    pool.tensor_tensor(rstd2[:, :], veps[:, 0:TJ], mhalf[:, 0:TJ], ALU.pow).then_inc(rstd2_s, 1)
                    pool.wait_ge(rstd2_s, p + 1)
                    apart(pool)
                if t.pre:
                    place_values(t.b + 1, 0, t)
                    place_values(t.b + 1, 1, None)
                if t.post:
                    dispatch(t)
                if t.pre:
                    place_values(t.b + 1, 2, None)

            def dispatch(t):
                p = t.b - 1
                pool.wait_ge(slots_s, p + 1)
                apart(pool)
                for k in range(TOPK):
                    for j in range(TJ):
                        if k:
                            pool.wait_ge(disp[j], 64 * p + 16 * k)
                            apart(pool)
                        at = TJ * TOPK * p + TOPK * j + k
                        st.then(pool.tensor_copy(h2[:, j, D:D + 1].bitcast(I32), home[:, bass.ds(at, 1)]))
                        apart(pool)
                        st.then(pool.tensor_copy(h2[:, j, D + 1:D + 2], w4[:, j, k:k + 1]))
                        apart(pool)
                        pool.indirect_dma_start(out=xs, out_offset=bass.IndirectOffsetOnAxis(
                            ap=slot_i[:, TOPK * j + k:TOPK * j + k + 1], axis=0), in_=h2[:, j, :], in_offset=None).then_inc(disp[j], 16)
                for j in range(TJ):
                    pool.wait_ge(disp[j], 64 * p + 64)
                    apart(pool)

            place_values(0, 0, lead)
            place_values(0, 1, None)
            place_values(0, 2, None)
            turn(first)
            with pool.Fori(LOOP0, LOOP1, 1) as b:
                st.enter(b - LOOP0, 1 + 2 * TOPK * TJ)
                turn(middle(b))
            st.leave(LOOP1 - LOOP0)
            turn(last)
            pool_tail = drain
            p = pool_tail.b - 1
            pool.wait_ge(stats2, p + 1)
            st.then(pool.tensor_scalar(veps[:, 0:TJ], mv2[:, :, 1], EPS, None, ALU.add))
            pool.tensor_tensor(rstd2[:, :], veps[:, 0:TJ], mhalf[:, 0:TJ], ALU.pow).then_inc(rstd2_s, 1)
            pool.wait_ge(rstd2_s, p + 1)
            dispatch(drain)
            with pool.Fori(0, MT // XR, 1) as i:
                for r in range(XR):
                    pool.wait_ge(y_done, XR * i + r + 1)
                    apart(pool)
                    pool.indirect_dma_start(out=yk, out_offset=bass.IndirectOffsetOnAxis(
                        ap=xe[:, r, D:D + 1].bitcast(I32), axis=0), in_=y_sb[:, r, :], in_offset=None,
                        bounds_check=NY - 1, oob_is_err=False).then_inc(y_out[r], 16)

        @block.scalar
        def _(act):
            for b in range(B):
                act.dma_start(x[:, b * TJ * D:(b + 1) * TJ * D].rearrange("p (j d) -> p j d", d=D),
                              x_in[b].rearrange("(j p) d -> p j d", p=P)).then_inc(x_ld[b], 16)
            act.wait_ge(mod_ld, 32)
            act.activation(ctmp[:, :], cT[:, :], ACT.Exp, scale=-1.0).then_inc(c_exp, 1)

            def normalise(t):
                n = t.b + 1
                for half in range(2):
                    above(act, spill[half], 32 * n)
                    apart(act)
                for j in range(TJ):
                    act.activation(xn[:, j, :], x[:, bass.ds((TJ * n + j) * D, D)], ACT.Identity,
                                   scale=rstd[:, bass.ds(TJ * n + j, 1)], bias=nmr[:, bass.ds(TJ * n + j, 1)]).then_inc(xn_ready, 1)

            def to_hT(t, k):
                n = t.b + 1
                frees(act.activation(hT[:, k, :], full(act, t, f"TP{k}"), ACT.Identity,
                                     scale=modT[:, bass.ds((2 + k) * B + n, 1)], bias=modT[:, bass.ds(k * B + n, 1)]), t, f"TP{k}")

            def round_qk(t, c):
                act.activation(qk_hi[:, c, :], full(act, t, f"QK{c}"), ACT.Copy).then_inc(hi_done, 1)

            def values_out(t, m):
                src = full(act, t, f"V{m}")
                above(act, v_in_place, 4 * (t.b + 1))
                frees(act.activation(v_new[:, 2 * m:2 * m + 2, :, :], src.rearrange("p (j h d) -> p j h d", j=2, d=HD), ACT.Copy), t, f"V{m}")

            def neg_max_hi(t, g):
                G_next = NG * t.b + g + 1
                src = full(act, t, f"MAX{g}")
                above(act, maxrow, 32 * G_next)
                act.activation(max_hi[:, :], src[0:G, :], ACT.Copy, scale=-1.0).then_inc(neg_hi, 1)

            def outputs_out(b, g):
                act.wait_ge(pv_done, 16 * b + 4 * g)
                act.activation(oT_raw[:, :], ps[:, O, :], ACT.Copy).then_inc(o_free, 1)

            def copy_out(t, name, to, part=None):
                src = full(act, t, name)
                frees(act.activation(to, src if part is None else part(src), ACT.Copy), t, name)

            def tanh_gate(t, c):
                act.activation(sh_tanh[:, c % 2, :], full(act, t, f"SG{c}"), ACT.Tanh, scale=0.5).then_inc(tanh_s, 1)

            def between(t, g, u):
                if u == 0 and g == 0 and t.pre:
                    normalise(t)
                if u == 3:
                    if t.att or t.pre and g == 3:
                        if (g < 3 or t.pre):
                            neg_max_hi(t, g)
                    if t.att and (g or t.post) or t.post and g == 0:
                        outputs_out(t.b, g)
                if g == 0:
                    if t.pre and u in (4, 5):
                        to_hT(t, u - 4)
                    if t.pre and u in (8, 11, 13, 15):
                        round_qk(t, {8: 0, 11: 1, 13: 2, 15: 3}[u])
                    if t.post and u == 10:
                        for k in range(KD):
                            copy_out(t, f"OT{k}", oT[:, k, :])
                if g == 1:
                    if t.pre and u in (7, 8):
                        values_out(t, u - 7)
                    if t.post and u in (10, 11):
                        copy_out(t, f"HT{u - 10}", h2T[:, u - 10, :])
                    if t.post and u == 13:
                        copy_out(t, "LOG", lgT[:, :], lambda s: s[0:E + 1, :])
                    if t.post and u == 15:
                        copy_out(t, "LGT", lg[:, :, :],
                                 lambda s: s[:, 0:TJ * 64].rearrange("p (j e) -> p j e", j=TJ)[:, :, 0:E + 1])
                if t.post:
                    if (g, u) == (2, 0):
                        tanh_gate(t, 0)
                    if (g, u) == (2, 3):
                        act.wait_ge(ex_in, 2 * t.b)
                        act.activation(ex[:, :, :], ex[:, :, :], ACT.Exp).then_inc(ex_out, 1)
                        act.activation(sgt[:, :], lg[:, :, E], ACT.Exp, scale=-1.0).then_inc(ex_out, 1)
                    if (g, u) == (2, 5):
                        tanh_gate(t, 1)
                    if (g, u) == (2, 10):
                        tanh_gate(t, 2)
                    if (g, u) == (3, 4):
                        tanh_gate(t, 3)

            def turn(t):
                for g in range(NG):
                    for u in range(16):
                        if t.att:
                            act.wait_ge(st_full, 64 * t.b + 16 * g + u + 1)
                            if u % 4 == 0:
                                above(act, pv_done, 16 * t.b + 4 * g + u // 4 - 1)
                            act.activation(probs[:, u % 8, :], ps[:, ST[(16 * g + u) % 3], :], ACT.Exp).then_inc(exp_done, 1)
                        between(t, g, u)

            act.wait_ge(nmr_s, 1)
            normalise(lead)
            act.wait_ge(modT_s, 1)
            for k in range(KD):
                to_hT(lead, k)
            for c in range(4):
                round_qk(lead, c)
            for m in range(2):
                values_out(lead, m)
            neg_max_hi(lead, 3)
            act.wait_ge(nmr_s, 2)
            turn(first)
            with act.Fori(LOOP0, LOOP1, 1) as b:
                turn(middle(b))
            turn(last)
            turn(drain)

            def silu(m, r):
                act.wait_ge(u_full, m + 1)
                above(act, hid_s, m - 1)
                act.activation(e_silu[:, r % 2, :], ps[:, 2 + r % 2, 0:DM], ACT.Silu).then_inc(esilu_s, 1)

            def hidden_out(m, r):
                act.wait_ge(ht_full, m + 1)
                above(act, y_full, m - 1)
                act.activation(e_hidT[:, r % 2, :], ps[0:DM, 4 + r % 2, 0:P], ACT.Copy).then_inc(ht_done, 1)

            def result_out(m, r):
                act.wait_ge(y_full, m + 1)
                act.activation(y_sb[:, r % XR, :], ps[:, 6 + r % 2, 0:D], ACT.Copy).then_inc(y_done, 1)

            def slot(n, r, since=XR, until=0):
                if since >= 1 and until <= 1:
                    silu(n - 1, r - 1)
                if since >= 3:
                    result_out(n - 3, r - 3)
                if since >= 2 and until <= 2:
                    hidden_out(n - 2, r - 2)

            for r in range(XR):
                slot(r, r, since=r)
            with act.Fori(1, MT // XR, 1) as i:
                for r in range(XR):
                    slot(XR * i + r, r)
            for r in range(3):
                slot(MT + r, r, until=r + 1)
            for t in range(NT):
                act.wait_ge(x3_done, t + 1)
                b, j = divmod(t, TJ)
                act.dma_start(out[b, j * P:(j + 1) * P, :], x[:, t * D:(t + 1) * D]).then_inc(stored, 16)
            act.wait_ge(stored, 16 * NT)

        @block.tensor
        def _(pe):
            pe.wait_ge(mod_ld, 32)
            pe.wait_ge(c_rep_s, 1)
            for c in range(2 * KD):
                for k in range(KD):
                    mm = pe.matmul(ps[:, 0, c * B:(c + 1) * B], wmod[:, k, c * P:(c + 1) * P], c_rep[:, k, :, 0],
                                   start=(k == 0), stop=(k == KD - 1))
            mm.then_inc(modT_ps, 1)
            pe.wait_ge(consts, 1)

            def claim(t, name):
                m, n = t.use(name)
                above(pe, misc_free[m], n)
                return ps[:, MISC[m], :]

            def filled(ins, t, name):
                ins.then_inc(misc_full[t.use(name)[0]], 1)

            def rows_to_columns(t, name, src, k):
                bank = claim(t, name)
                for j in range(TJ):
                    mm = pe.transpose(bank[:, j * P:(j + 1) * P], src[:, j, k * P:(k + 1) * P], ident[:, :])
                filled(mm, t, name)

            def written(t, name):
                m, n = t.use(name)
                pe.wait_ge(misc_free[m], n + 1)

            def project_qk(t, c):
                if c == 0:
                    written(t, "TP0")
                    written(t, "TP1")
                bank = claim(t, f"QK{c}")
                w = (wq_sb, wk_sb)[c % 2]
                for k in range(KD):
                    mm = pe.matmul(bank, w[:, k, (c // 2) * P:(c // 2 + 1) * P], hT[:, k, :], start=(k == 0), stop=(k == KD - 1))
                filled(mm, t, f"QK{c}")

            def project_v(t, m):
                bank = claim(t, f"V{m}")
                for j in (2 * m, 2 * m + 1):
                    for k in range(KD):
                        mm = pe.matmul(bank[:, (j % 2) * D:(j % 2 + 1) * D], hT[:, k, j * P:(j + 1) * P], wv_sb[:, k, :],
                                       start=(k == 0), stop=(k == KD - 1))
                filled(mm, t, f"V{m}")

            def score(b, g, n):
                qt, i = divmod(n, G)
                if n == 0:
                    pe.wait_ge(stack_ld[g], 128 * b + 128)
                above(pe, max_done, 64 * b + 16 * g + n - 1)
                pe.matmul(ps[:, SC[n % 2], :], q_stack[0:64, G * g + i, qt * P:(qt + 1) * P], k_stack[0:64, G * g + i, :],
                          start=True, stop=True).then_inc(sc_full, 1)

            def turn_max(t, g):
                pe.wait_ge(max_done, 64 * t.b + 16 * g + 32)
                bank = claim(t, f"MAX{g}")
                for qt in range(TJ):
                    mm = pe.transpose(bank[0:G, qt * P:(qt + 1) * P], max_q[:, (g + 1) % 2, qt, :], ident[:, :])
                filled(mm, t, f"MAX{g}")

            def scoreT(b, g, n):
                kt, i = divmod(n, G)
                u = 16 * g + n
                if n == 0:
                    pe.wait_ge(maxrow, 32 * (NG * b + g) + 32)
                above(pe, exp_done, 64 * b + max(u - 2, 0))
                pe.matmul(ps[:, ST[u % 3], :], k_stack[:, G * g + i, kt * P:(kt + 1) * P], q_stack[:, G * g + i, :],
                          start=True, stop=True).then_inc(st_full, 1)

            def values(b, g, kt):
                pe.wait_ge(exp_done, 64 * b + 16 * g + 4 * kt + 4)
                if kt == 0:
                    above(pe, o_free, NG * b + g)
                    pe.wait_ge(v_in_place, NG * b + g + 1)
                for i in range(G):
                    mm = pe.matmul(ps[32 * i:32 * i + 32, O, :], v_ext[:, kt, G * g + i, :], probs[:, (4 * kt + i) % 8, :],
                                   start=(kt == 0), stop=(kt == TJ - 1), tile_position=(0, 32 * i))
                mm.then_inc(pv_done, 1)

            def outputs_back(t, b, g):
                pe.wait_ge(o_free, NG * b + g + 1)
                bank = claim(t, f"OUT{g}")
                for qt in range(TJ):
                    mm = pe.transpose(bank[:, qt * P:(qt + 1) * P], oT_raw[:, qt * P:(qt + 1) * P], ident[:, :])
                filled(mm, t, f"OUT{g}")

            def project_o(t, m):
                if m == 0:
                    written(t, "OT0")
                    written(t, "OT1")
                bank = claim(t, f"WO{m}")
                p = t.b - 1
                for j in (2 * m, 2 * m + 1):
                    for k in range(KD):
                        mm = pe.matmul(bank[:, (j % 2) * D:(j % 2 + 1) * D], oT[:, k, j * P:(j + 1) * P],
                                       wo_g[:, bass.ds(p * (KD * D) + k * D, D)], start=(k == 0), stop=(k == KD - 1))
                filled(mm, t, f"WO{m}")

            def modulate(t, s):
                bank = claim(t, f"MOD{s}")
                for k in range(KD):
                    mm = pe.matmul(bank, c_rep[:, k, s // 2, :], wmod[:, k, (2 + 2 * (s % 2)) * D:(4 + 2 * (s % 2)) * D],
                                   start=(k == 0), stop=(k == KD - 1))
                filled(mm, t, f"MOD{s}")

            def logits(t):
                written(t, "HT0")
                written(t, "HT1")
                bank = claim(t, "LOG")
                for k in range(KD):
                    mm = pe.matmul(bank[0:E + 1, :], gate_sb[:, k, :], h2T[:, k, :], start=(k == 0), stop=(k == KD - 1))
                filled(mm, t, "LOG")

            def turn_logits(t):
                written(t, "LOG")
                apart(pe)
                bank = claim(t, "LGT")
                apart(pe)
                for j in range(TJ):
                    mm = pe.transpose(bank[:, 64 * j:64 * j + E + 1], lgT[:, j * P:(j + 1) * P], ident[0:E + 1, 0:E + 1])
                filled(mm, t, "LGT")

            def ranks(t):
                pe.wait_ge(chosen_s, t.b)
                bank = claim(t, "RANK")
                pe.matmul(bank[:, 0:TJ * E], upper[:, :], chosen[:, :, :], start=True, stop=False)
                filled(pe.matmul(bank[:, 0:TJ * E], ones[:, :], before[:, 0:TJ, :], start=False, stop=True), t, "RANK")

            def shared_up(t, name, w, c):
                bank = claim(t, f"{name}{c}")
                for k in range(KD):
                    mm = pe.matmul(bank, w[:, k, c * P:(c + 1) * P], h2T[:, k, :], start=(k == 0), stop=(k == KD - 1))
                filled(mm, t, f"{name}{c}")

            def shared_down(t, m):
                if m == 0:
                    for c in range(4):
                        written(t, f"SU{c}")
                bank = claim(t, f"SD{m}")
                for j in (2 * m, 2 * m + 1):
                    for c in range(4):
                        mm = pe.matmul(bank[:, (j % 2) * D:(j % 2 + 1) * D], sh_hidT[:, c, j * P:(j + 1) * P], sdown_sb[:, c, :],
                                       start=(c == 0), stop=(c == 3))
                filled(mm, t, f"SD{m}")

            def between(t, g, u):
                if t.att and (g or t.post) and u == 1 or t.post and (g, u) == (0, 1):
                    values(t.b if g else t.b - 1, (g - 1) % NG, TJ - 1)
                if u == 2 and (t.att and g < 3 or t.pre and g == 3):
                    turn_max(t, g)
                if t.att and u in (5, 9, 13):
                    values(t.b, g, u // 4 - 1)
                if g == 0:
                    if t.pre and u == 3:
                        for k in range(KD):
                            rows_to_columns_x(t, k)
                    if t.post and u == 5:
                        outputs_back(t, t.b - 1, 3)
                    if t.mod and u == 6:
                        modulate(t, 0)
                    if t.pre and u == 7:
                        project_qk(t, 0)
                    if t.post and u == 9:
                        written(t, "OUT3")
                        for k in range(KD):
                            rows_to_columns(t, f"OT{k}", o_norm, k)
                    if t.pre and u == 10:
                        project_qk(t, 1)
                    if t.post and u == 11:
                        project_o(t, 0)
                    if t.mod and u == 11:
                        modulate(t, 1)
                    if t.pre and u == 12:
                        project_qk(t, 2)
                    if t.post and u == 13:
                        project_o(t, 1)
                    if t.pre and u == 14:
                        project_qk(t, 3)
                elif t.att and u == 5:
                    outputs_back(t, t.b, g - 1)
                if g == 1:
                    if t.pre and u in (6, 7):
                        project_v(t, u - 6)
                    if t.mod and u in (8, 12):
                        modulate(t, u // 4)
                    if t.post and u == 9:
                        pe.wait_ge(h2_ready, t.b)
                        for k in range(KD):
                            rows_to_columns(t, f"HT{k}", h2, k)
                    if t.post and u == 12:
                        logits(t)
                    if t.post and u == 14:
                        turn_logits(t)
                    if t.post and u == 15:
                        shared_up(t, "SG", sgate_sb, 0)
                        shared_up(t, "SU", sup_sb, 0)
                if g == 2:
                    if t.post and u == 4:
                        shared_up(t, "SG", sgate_sb, 1)
                    if t.post and u == 6:
                        shared_up(t, "SU", sup_sb, 1)
                    if t.post and u == 8:
                        ranks(t)
                    if t.mod and u in (8, 12):
                        modulate(t, 2 + u // 4)
                    if t.post and u == 9:
                        shared_up(t, "SG", sgate_sb, 2)
                    if t.post and u == 12:
                        shared_up(t, "SU", sup_sb, 2)
                if g == 3:
                    if t.post and u == 3:
                        shared_up(t, "SG", sgate_sb, 3)
                    if t.post and u == 6:
                        shared_up(t, "SU", sup_sb, 3)
                    if t.mod and u in (8, 12):
                        modulate(t, 4 + u // 4)
                    if t.post and u in (9, 12):
                        shared_down(t, u // 12)

            def rows_to_columns_x(t, k):
                if k == 0:
                    pe.wait_ge(xn_ready, TJ * (t.b + 1) + TJ)
                rows_to_columns(t, f"TP{k}", xn, k)

            def turn(t):
                for g in range(NG):
                    for u in range(16):
                        if t.att:
                            scoreT(t.b, g, u)
                            if g < 2:
                                score(t.b, g + 2, u)
                            elif t.pre:
                                score(t.b + 1, g - 2, u)
                        between(t, g, u)

            for k in range(KD):
                rows_to_columns_x(lead, k)
            pe.wait_ge(w_ld, 80)
            for c in range(4):
                project_qk(lead, c)
            for m in range(2):
                project_v(lead, m)
            for n in range(16):
                score(0, 0, n)
            turn_max(lead, 3)
            for n in range(16):
                score(0, 1, n)
            pe.wait_ge(sh_ld, 48)
            turn(first)
            with pe.Fori(LOOP0, LOOP1, 1) as b:
                turn(middle(b))
            turn(last)
            turn(drain)
            for m in range(2):
                pe.wait_ge(misc_free[m], all_uses[m])
            pe.matmul(ps[:, 6, 0:E], ones[:, :], before[:, TJ, :], start=True, stop=True).then_inc(cnt_ps, 1)
            pe.wait_ge(tcol_s, 1)
            for c in range(2):
                mm = pe.matmul(ps[0:1, 7, c * P:(c + 1) * P], tcol2[:, c:c + 1], ident[:, :], start=True, stop=True)
            mm.then_inc(tab_ps, 1)
            pe.wait_ge(up_ld, 48)
            pe.wait_ge(tab_s, 1)

            def expert(n):
                return pe.value_load(tab[0:1, bass.ds(n, 1)], min_val=0, max_val=E - 1)

            def turn_rows(i, n, r):
                pe.wait_ge(xe_ld[r], 16 * i + 16)
                above(pe, t_done, n - 1)
                for k in range(KD):
                    mm = pe.transpose(ps[:, r % 2, k * P:(k + 1) * P], xe[:, r, k * P:(k + 1) * P], ident[:, :])
                mm.then_inc(t_full, 1)

            def widen(m, r, e):
                pe.wait_ge(t_done, m + 1)
                above(pe, hid_s, m - 1)
                for k in range(KD):
                    mm = pe.matmul(ps[:, 2 + r % 2, 0:2 * DM], xeT[:, r % 2, k * P:(k + 1) * P],
                                   up_sb[:, bass.ds(e * (2 * DM) + k * E * 2 * DM, 2 * DM)], start=(k == 0), stop=(k == KD - 1))
                mm.then_inc(u_full, 1)

            def turn_hidden(m, r):
                pe.wait_ge(hid_s, m + 1)
                above(pe, ht_done, m - 1)
                pe.transpose(ps[0:DM, 4 + r % 2, 0:P], e_hid[:, r % 2, :], ident[:, :]).then_inc(ht_full, 1)

            def narrow(m, r, e):
                pe.wait_ge(ht_done, m + 1)
                above(pe, y_done, m - 1)
                pe.matmul(ps[:, 6 + r % 2, 0:D], e_hidT[:, r % 2, :], down_sb[:, bass.ds(e * D, D)],
                          start=True, stop=True).then_inc(y_full, 1)

            def slots(i, rs, since=None, until=None):
                es = {}
                for r in rs:
                    n = XR * i + r
                    behind = r if since is None else since + r
                    ahead = 0 if until is None else r + 1
                    if behind >= 1 and ahead <= 1:
                        es[r - 1] = expert(n - 1)
                        widen(n - 1, r - 1, es[r - 1])
                    if not ahead:
                        turn_rows(i, n, r)
                    if behind >= 3:
                        if r - 3 not in es:
                            es[r - 3] = expert(n - 3)
                        narrow(n - 3, r - 3, es[r - 3])
                    if behind >= 2 and ahead <= 2:
                        turn_hidden(n - 2, r - 2)

            slots(0, range(XR))
            with pe.Fori(1, MT // XR, 1) as i:
                slots(i, range(XR), since=XR)
            slots(MT // XR, range(3), since=XR, until=0)

        @block.vector
        def _(dve):
            st = Steps(dve, dve_s)

            def statistics(lo, hi, turn):
                for t in range(lo, hi):
                    if t % TJ == 0:
                        dve.wait_ge(x_ld[t // TJ], 16)
                    st.did(dve.bn_stats(bn[:, t, :], x[:, t * D:(t + 1) * D]))
                st.wait()
                for t in range(lo, hi):
                    ins = dve.bn_aggr(mv[:, t, :], bn[:, t, :])
                ins.then_inc(stats, 1)

            def minus_mean_over_deviation(lo, hi, turn):
                dve.wait_ge(rstd_s, turn)
                dve.scalar_tensor_tensor(out=nmr[:, lo:hi], in0=mv[:, lo:hi, 0], scalar=-1.0, in1=rstd[:, lo:hi],
                                         op0=ALU.mult, op1=ALU.mult).then_inc(nmr_s, 1)

            statistics(0, TJ, 1)
            dve.wait_ge(c_exp, 1)
            st.then(dve.tensor_scalar(ctmp[:, :], ctmp[:, :], 1.0, None, ALU.add))
            st.then(dve.reciprocal(ctmp[:, :], ctmp[:, :]))
            st.then(dve.tensor_tensor(cT[:, :], cT[:, :], ctmp[:, :], ALU.mult))
            dve.tensor_copy(c_rep[:, :, :, :].rearrange("p k b n -> p (k b) n"),
                            cT[:, :].unsqueeze(2).to_broadcast([P, KD * B, P])).then_inc(c_rep_s, 1)
            minus_mean_over_deviation(0, TJ, 1)
            dve.wait_ge(modT_ps, 1)
            st.then(dve.tensor_copy(modT[:, 0:KD * B], ps[:, 0, 0:KD * B]))
            dve.tensor_scalar(modT[:, KD * B:], ps[:, 0, KD * B:2 * KD * B], 1.0, None, ALU.add).then_inc(modT_s, 1)

            def rest_of_qk(t, c):
                m, n = t.use(f"QK{c}")
                dve.wait_ge(hi_done, 4 * (t.b + 1) + c + 1)
                frees(dve.tensor_tensor(qk_lo[:, c, :], ps[:, MISC[m], :], qk_hi[:, c, :].bitcast(F32), ALU.subtract), t, f"QK{c}")

            def score_max(b, g, n):
                qt, i = divmod(n, G)
                dve.wait_ge(sc_full, 64 * b + 16 * g + n + 1)
                dve.tensor_reduce(max_q[:, g % 2, qt, i:i + 1], ps[:, SC[n % 2], :], AXX, ALU.max).then_inc(max_done, 1)

            def neg_max_lo(t, g):
                m, n = t.use(f"MAX{g}")
                dve.wait_ge(neg_hi, NG * t.b + g + 2)
                frees(dve.scalar_tensor_tensor(out=max_lo[:, :], in0=ps[0:G, MISC[m], :], scalar=-1.0,
                                               in1=max_hi[:, :].bitcast(F32), op0=ALU.mult, op1=ALU.subtract), t, f"MAX{g}")

            def divide(t, g):
                heads = full(dve, t, f"OUT{g}").rearrange("p (q i d) -> p q i d", q=TJ, i=G)
                st.then(dve.reciprocal(rsum[:, :, :], heads[:, :, :, HD]))
                frees(dve.tensor_tensor(o_norm[:, :, G * HD * g:G * HD * (g + 1)].rearrange("p q (i d) -> p q i d", i=G),
                                        heads[:, :, :, 0:HD], rsum[:, :, :].unsqueeze(3).to_broadcast([P, TJ, G, HD]),
                                        ALU.mult), t, f"OUT{g}")

            def guarded_gate(to, src):
                st.then(dve.tensor_scalar(gtmp[:, 0, :], src, 0.0, 2.0, ALU.is_ge, ALU.mult))
                st.then(dve.tensor_scalar(gtmp[:, 0, :], gtmp[:, 0, :], -1.0, None, ALU.add))
                st.then(dve.tensor_tensor(gtmp[:, 1, :], src, gtmp[:, 0, :], ALU.mult))
                st.then(dve.scalar_tensor_tensor(out=to, in0=gtmp[:, 1, :], scalar=0.25, in1=gtmp[:, 0, :],
                                                 op0=ALU.max, op1=ALU.mult))

            def modulation(t, s):
                bank = full(dve, t, f"MOD{s}")
                b = s // 2
                at = 3 * D * b
                if s % 2 == 0:
                    guarded_gate(gtmp[:, 0, :], bank[:, 0:D])
                    for k in range(KD):
                        st.did(dve.tensor_tensor(wo_g[:, (b * KD + k) * D:(b * KD + k + 1) * D], wo_sb[:, k, :], gtmp[:, 0, :], ALU.mult))
                    st.wait()
                    frees(dve.tensor_copy(mod_b[:, at:at + D], bank[:, D:2 * D]), t, f"MOD{s}")
                else:
                    guarded_gate(mod_b[:, at + 2 * D:at + 3 * D], bank[:, D:2 * D])
                    frees(dve.tensor_scalar(mod_b[:, at + D:at + 2 * D], bank[:, 0:D], 1.0, None, ALU.add), t, f"MOD{s}")

            def residual(t, m):
                bank = full(dve, t, f"WO{m}")
                two = x[:, bass.ds((t.b - 1) * (TJ * D) + 2 * m * D, 2 * D)]
                frees(dve.tensor_tensor(two, bank, two, ALU.add), t, f"WO{m}")

            def statistics2(t):
                p = t.b - 1
                for m in range(2):
                    own_free(dve, t, f"WO{m}")
                    apart(dve)
                for j in range(TJ):
                    st.did(dve.bn_stats(bn[:, j, :], x[:, bass.ds((TJ * p + j) * D, D)]))
                st.wait()
                apart(dve)
                for j in range(TJ):
                    ins = dve.bn_aggr(mv2[:, j, :], bn[:, j, :])
                ins.then_inc(stats2, 1)

            def second_norm(t):
                p = t.b - 1
                dve.wait_ge(rstd2_s, p + 1)
                dve.wait_ge(v_in_place, min(4 * t.b + 4, 4 * B) if isinstance(t.b, int) else 4 * t.b + 4)
                for j in range(TJ):
                    st.did(dve.tensor_scalar(h2[:, j, 0:D], x[:, bass.ds((TJ * p + j) * D, D)], mv2[:, j, 0:1],
                                             rstd2[:, j:j + 1], ALU.subtract, ALU.mult))
                st.wait()
                st.then(dve.tensor_tensor(h2[:, :, 0:D], h2[:, :, 0:D],
                                          mod_b[:, bass.ds(p * (3 * D) + D, D)].unsqueeze(1).to_broadcast([P, TJ, D]), ALU.mult))
                dve.tensor_tensor(h2[:, :, 0:D], h2[:, :, 0:D],
                                  mod_b[:, bass.ds(p * (3 * D), D)].unsqueeze(1).to_broadcast([P, TJ, D]), ALU.add).then_inc(h2_ready, 1)

            def top_logits(t):
                own_free(dve, t, "LGT")
                apart(dve)
                for j in range(TJ):
                    st.did(dve.max(v8[:, j, :], lg[:, j, 0:E]))
                st.wait()
                apart(dve)
                for j in range(TJ):
                    st.did(dve.max_index(i8[:, j, :], v8[:, j, :], lg[:, j, 0:E]))
                top = v8[:, :, 0:1]
                dve.tensor_tensor(ex[:, :, 0:E], lg[:, :, 0:E], top.to_broadcast([P, TJ, E]), ALU.subtract).then_inc(ex_in, 1)
                dve.tensor_tensor(ex[:, :, E:E + TOPK], v8[:, :, 0:TOPK], top.to_broadcast([P, TJ, TOPK]),
                                  ALU.subtract).then_inc(ex_in, 1)
                st.wait()

            def choices(t):
                st.then(dve.tensor_copy(e4[:, :, :], i8[:, :, 0:TOPK]))
                st.then(dve.tensor_tensor(onehot[:, :, :], iota_ef[:, :].unsqueeze(1).to_broadcast([P, TJ * TOPK, E]),
                                          e4[:, :, :].rearrange("p j k -> p (j k)").unsqueeze(2).to_broadcast([P, TJ * TOPK, E]),
                                          ALU.is_equal))
                st.did(dve.tensor_copy(before[:, 0, :], before[:, TJ, :]))
                st.then(dve.tensor_reduce(chosen[:, :, :], onehot[:, :, :].rearrange("p (j k) e -> p j e k", k=TOPK), AXX, ALU.add))
                for j in range(TJ - 1):
                    st.then(dve.tensor_tensor(before[:, j + 1, :], before[:, j, :], chosen[:, j, :], ALU.add))
                dve.tensor_tensor(before[:, TJ, :], before[:, TJ - 1, :], chosen[:, TJ - 1, :], ALU.add).then_inc(chosen_s, 1)

            def weights(t):
                p = t.b - 1
                dve.wait_ge(ex_out, 2 * t.b)
                st.then(dve.tensor_reduce(z4[:, :], ex[:, :, 0:E], AXX, ALU.add))
                st.then(dve.reciprocal(z4[:, :], z4[:, :]))
                st.then(dve.tensor_tensor(p4[:, :, :], ex[:, :, E:E + TOPK], z4[:, :].unsqueeze(2).to_broadcast([P, TJ, TOPK]), ALU.mult))
                st.then(dve.tensor_reduce(s4[:, :], p4[:, :, :], AXX, ALU.add))
                st.then(dve.tensor_scalar(s4[:, :], s4[:, :], 1e-20, None, ALU.add))
                st.then(dve.reciprocal(s4[:, :], s4[:, :]))
                st.did(dve.tensor_tensor(w4[:, :, :], p4[:, :, :], s4[:, :].unsqueeze(2).to_broadcast([P, TJ, TOPK]), ALU.mult))
                st.then(dve.tensor_scalar(sgt[:, :], sgt[:, :], 2.0, 2.0, ALU.mult, ALU.add))
                st.then(dve.reciprocal(sg[:, bass.ds(p * TJ, TJ)], sgt[:, :]))

            def slots(t):
                bank = full(dve, t, "RANK")
                frees(dve.tensor_tensor(rank[:, :, :], bank[:, 0:TJ * E].rearrange("p (j e) -> p j e", e=E),
                                        base_f[:, :].unsqueeze(1).to_broadcast([P, TJ, E]), ALU.add), t, "RANK")
                own_free(dve, t, "RANK")
                st.then(dve.tensor_tensor(picked[:, :, :].rearrange("p (j k) e -> p j k e", k=TOPK),
                                          onehot[:, :, :].rearrange("p (j k) e -> p j k e", k=TOPK),
                                          rank[:, :, :].unsqueeze(2).to_broadcast([P, TJ, TOPK, E]), ALU.mult))
                st.then(dve.tensor_reduce(slot_f[:, :], picked[:, :, :], AXX, ALU.add))
                dve.tensor_copy(slot_i[:, :], slot_f[:, :]).then_inc(slots_s, 1)

            def hidden_gate(t, c):
                bank = full(dve, t, f"SG{c}")
                dve.wait_ge(tanh_s, 4 * (t.b - 1) + c + 1)
                frees(dve.scalar_tensor_tensor(out=sh_tanh[:, c % 2, :], in0=sh_tanh[:, c % 2, :], scalar=1.0, in1=bank,
                                               op0=ALU.add, op1=ALU.mult), t, f"SG{c}")

            def hidden_up(t, c):
                if c == 0:
                    for half in range(2):
                        dve.wait_ge(spill[half], min(32 * (t.b + 2), 32 * B) if isinstance(t.b, int) else 32 * t.b + 64)
                bank = full(dve, t, f"SU{c}")
                own_free(dve, t, f"SG{c}")
                ins = dve.tensor_tensor(sh_hidT[:, c, :], sh_tanh[:, c % 2, :], bank, ALU.mult)
                frees(ins, t, f"SU{c}")

            def add_shared(t, m):
                p = t.b - 1
                bank = full(dve, t, f"SD{m}")
                for j in (2 * m, 2 * m + 1):
                    ins = dve.scalar_tensor_tensor(out=gtmp[:, j % 2, :], in0=bank[:, (j % 2) * D:(j % 2 + 1) * D],
                                                   scalar=sg[:, bass.ds(TJ * p + j, 1)],
                                                   in1=mod_b[:, bass.ds(p * (3 * D) + 2 * D, D)], op0=ALU.mult, op1=ALU.mult)
                    if j % 2:
                        frees(ins, t, f"SD{m}")
                    else:
                        st.did(ins)
                st.wait()
                own_free(dve, t, f"SD{m}")
                two = x[:, bass.ds(p * (TJ * D) + 2 * m * D, 2 * D)]
                st.then(dve.tensor_tensor(two, two, gtmp[:, :, :].rearrange("p j d -> p (j d)"), ALU.add))

            def between(t, g, u):
                if u == 3 and (t.att and g < 3 or t.pre and g == 3):
                    neg_max_lo(t, g)
                if g == 0:
                    if t.post and u == 7:
                        divide(t, 3)
                    if t.mod and u == 8:
                        modulation(t, 0)
                    if t.pre and u in (9, 11, 14):
                        rest_of_qk(t, {9: 0, 11: 1, 14: 2}[u])
                    if t.post and u in (12, 15):
                        residual(t, u // 15)
                    if t.mod and u == 13:
                        modulation(t, 1)
                elif t.att and u == 7:
                    divide(t, g - 1)
                if g == 1:
                    if t.pre and u == 0:
                        rest_of_qk(t, 3)
                    if t.post and u == 1:
                        statistics2(t)
                    if t.post and u == 5:
                        second_norm(t)
                    if t.mod and u in (10, 14):
                        modulation(t, u // 4)
                if g == 2:
                    if t.mod and u in (10, 14):
                        modulation(t, 2 + u // 4)
                    if t.post and u == 0:
                        top_logits(t)
                    if t.post and u == 1:
                        hidden_gate(t, 0)
                        hidden_up(t, 0)
                    if t.post and u == 3:
                        choices(t)
                    if t.post and u == 6:
                        hidden_gate(t, 1)
                    if t.post and u == 8:
                        hidden_up(t, 1)
                        weights(t)
                    if t.post and u == 10:
                        slots(t)
                    if t.post and u == 11:
                        hidden_gate(t, 2)
                    if t.post and u == 14:
                        hidden_up(t, 2)
                if g == 3:
                    if t.mod and u in (10, 14):
                        modulation(t, 4 + u // 4)
                    if t.post and u == 5:
                        hidden_gate(t, 3)
                    if t.post and u == 8:
                        hidden_up(t, 3)
                    if t.post and u in (11, 14):
                        add_shared(t, u // 14)

            def turn(t):
                for g in range(NG):
                    for u in range(16):
                        if t.att and g < 2:
                            score_max(t.b, g + 2, u)
                        elif t.att and t.pre:
                            score_max(t.b + 1, g - 2, u)
                        between(t, g, u)

            for c in range(4):
                rest_of_qk(lead, c)
            statistics(TJ, NT, 2)
            dve.wait_ge(consts, 1)
            for to, of in ((iota_ef, iota_e), (base_f, base_i), (thr_f, thr_i), (tile_f, tile_i)):
                st.did(dve.tensor_copy(to[:, :], of[:, :]))
            for n in range(16):
                score_max(0, 0, n)
            neg_max_lo(lead, 3)
            minus_mean_over_deviation(TJ, NT, 2)
            for n in range(16):
                score_max(0, 1, n)
            dve.wait_ge(w_ld, 80)
            turn(first)
            st.wait()
            with dve.Fori(LOOP0, LOOP1, 1) as b:
                st.enter(b - LOOP0, DVE_STEPS)
                turn(middle(b))
            st.leave(LOOP1 - LOOP0)
            turn(last)
            turn(drain)
            dve.wait_ge(cnt_ps, 1)
            st.then(dve.tensor_copy(cnt[:, :], ps[:, 6, 0:E]))
            st.did(dve.tensor_tensor(pad_at[:, :], base_f[:, :], cnt[:, :], ALU.add))
            over = picked[:, :, :].rearrange("p a e -> p (a e)").rearrange("p (e r) -> p e r", r=NT)
            st.then(dve.tensor_tensor(over, cnt[:, :].unsqueeze(2).to_broadcast([P, E, NT]),
                                      thr_f[:, :].unsqueeze(1).to_broadcast([P, E, NT]), ALU.is_gt))
            st.then(dve.tensor_reduce(ntile[:, :], over, AXX, ALU.add))
            st.then(dve.tensor_tensor_scan(ctile[:, :], ones[:, 0:E], ntile[:, :], 0.0, ALU.mult, ALU.add))
            st.then(dve.tensor_scalar(past[:, :], ctile[:, :], tile_f[:, 0:1], None, ALU.is_le))
            st.did(dve.tensor_reduce(tcol[:, 0:1], past[:, :], AXX, ALU.add))
            st.then(dve.tensor_tensor(past_n[:, :], past[:, :], ntile[:, :], ALU.mult))
            st.then(dve.tensor_reduce(tcol[:, 1:2], past_n[:, :], AXX, ALU.add))
            st.did(dve.tensor_tensor(tcol[:, 2:3], tile_f[:, :], tcol[:, 1:2], ALU.subtract))
            st.did(dve.tensor_scalar(tcol[:, 3:4], tcol[:, 0:1], float(CAP), None, ALU.mult))
            st.then(dve.tensor_scalar(tcol2[:, 0:1], tcol[:, 0:1], float(E - 1), None, ALU.min))
            st.then(dve.scalar_tensor_tensor(out=tcol[:, 1:2], in0=tcol[:, 2:3], scalar=float(P), in1=tcol[:, 3:4],
                                             op0=ALU.mult, op1=ALU.add))
            dve.tensor_scalar(tcol2[:, 1:2], tcol[:, 1:2], float(E * CAP), None, ALU.min).then_inc(tcol_s, 1)
            dve.wait_ge(tab_ps, 1)
            dve.tensor_copy(tab[:, :], ps[0:1, 7, 0:2 * P]).then_inc(tab_s, 1)

            def columns_out(n, r):
                dve.wait_ge(t_full, n + 1)
                above(dve, u_full, n - 1)
                dve.tensor_copy(xeT[:, r % 2, :], ps[:, r % 2, 0:KD * P]).then_inc(t_done, 1)

            def gated(m, r):
                dve.wait_ge(esilu_s, m + 1)
                above(dve, ht_full, m - 1)
                dve.scalar_tensor_tensor(out=e_hid[:, r % 2, :], in0=ps[:, 2 + r % 2, DM:2 * DM],
                                         scalar=xe[:, r % XR, D + 1:D + 2], in1=e_silu[:, r % 2, :], op0=ALU.mult,
                                         op1=ALU.mult).then_inc(hid_s, 1)

            for r in range(XR):
                columns_out(r, r)
                if r:
                    gated(r - 1, r - 1)
            with dve.Fori(1, MT // XR, 1) as i:
                for r in range(XR):
                    columns_out(XR * i + r, r)
                    gated(XR * i + r - 1, r - 1)
            gated(MT - 1, XR - 1)
            st.wait()
            for t in range(NT):
                b = t // TJ
                dve.wait_ge(comb_ld[t % CR], 16 * (t // CR) + 16)
                dve.tensor_reduce(gtmp[:, t % 2, :], comb[:, t % CR, :].rearrange("p (k d) -> p d k", k=TOPK), AXX, ALU.add).then_inc(part_s, 1)
                dve.wait_ge(part_s, t + 1)
                st.then(dve.tensor_tensor(gtmp[:, t % 2, :], gtmp[:, t % 2, :], mod_b[:, (3 * b + 2) * D:(3 * b + 3) * D], ALU.mult))
                dve.tensor_tensor(x[:, t * D:(t + 1) * D], x[:, t * D:(t + 1) * D], gtmp[:, t % 2, :], ALU.add).then_inc(x3_done, 1)


def kernel(**inputs):
    import numpy as _np
    import concourse.bacc as _bacc
    from concourse import mybir as _mybir
    from concourse.bass_utils import run_bass_kernel_spmd as _run

    i = {k[3:]: _np.asarray(v) for k, v in inputs.items()}
    arrays = {
        "x": i["attn_x"],
        "wq": i["attn_wq"].T, "wk": i["attn_wk"].T, "wv": i["attn_wv"].T, "wo": i["attn_wo"].T,
        "gate": _np.concatenate([i["ffn_gate_w"], i["ffn_shared_expert_gate_w"]], axis=0).T,
        "up": i["ffn_gate_up_proj"].transpose(2, 0, 1).reshape(D, E * 2 * DM),
        "down": i["ffn_down_proj"].transpose(2, 0, 1).reshape(DM, E * D),
        "sgate": i["ffn_shared_gate_w"].T, "sup": i["ffn_shared_up_w"].T, "sdown": i["ffn_shared_down_w"].T,
        "c": i["c"].T, "wmod": i["wmod"],
    }
    arrays = {f"in_{k}": _np.ascontiguousarray(v) for k, v in arrays.items()}
    nc = _bacc.Bacc("TRN2", target_bir_lowering=False, num_devices=1)
    args = [nc.dram_tensor(k, v.shape, _mybir.dt.from_np(v.dtype), kind="ExternalInput").ap() for k, v in arrays.items()]
    out = nc.dram_tensor("out", (B, S, D), _mybir.dt.float32, kind="ExternalOutput").ap()
    adaln_moe_kernel(nc, *args, out)
    r = _run(nc, [arrays], core_ids=[0])
    return r.results[0]["out"]
```

```python
from contextlib import ExitStack

import concourse.bass as bass
from concourse import mybir

ALU = mybir.AluOpType
ACT = mybir.ActivationFunctionType
AXX = mybir.AxisListType.X
F32 = mybir.dt.float32
F32R = mybir.dt.float32r
I32 = mybir.dt.int32
U32 = mybir.dt.uint32

P = 128
B, S, D = 4, 512, 256
H, HD = 16, 16
KD = D // P
TJ = S // P
NT = B * TJ
G = 4
NG = H // G
E, TOPK, DM, DS = 32, 4, 96, 512
CAP = P + B * S
MT = B * S * TOPK // P + E
ROW = D + 2
SKIP = 1 << 20
NY = B * S * TOPK
EPS = 1e-5
XP = 8
YP = 4
CR = 8
DVE_STEPS = 31
POOL_STEPS = 27


class Steps:

    def __init__(self, eng, sem):
        self.eng, self.sem, self.base, self.n = eng, sem, 0, 0

    def did(self, ins):
        ins.then_inc(self.sem, 1)
        self.n += 1

    def wait(self):
        self.eng.wait_ge(self.sem, self.base + self.n)

    def then(self, ins):
        self.did(ins)
        self.wait()

    def enter(self, i, per):
        self.total, self.base, self.n, self.per = self.n, self.n + i * per, 0, per

    def leave(self, turns):
        assert self.n == self.per, (self.n, self.per)
        self.base, self.n = 0, self.total + turns * self.per


class Turn:

    ORDER = (
        ("MAX0", "att"), ("TP0", "pre"), ("TP1", "pre"), ("OUT3", "post"), ("MOD0", "mod"), ("QK0", "pre"),
        ("OT0", "post"), ("OT1", "post"),
        ("QK1", "pre"), ("WO0", "post"), ("MOD1", "mod"), ("QK2", "pre"), ("WO1", "post"), ("QK3", "pre"),
        ("MAX1", "att"), ("OUT0", "att"), ("V0", "pre"), ("V1", "pre"), ("MOD2", "mod"), ("HT0", "post"), ("HT1", "post"),
        ("MOD3", "mod"), ("LOG", "post"), ("LGT", "post"),
        ("MAX2", "att"), ("SG0", "post"), ("RANK", "end"), ("CNT", "end"), ("OUT1", "att"), ("SU0", "post"),
        ("MOD4", "mod"), ("SG1", "post"), ("SU1", "post"),
        ("MOD5", "mod"), ("SG2", "post"), ("RANK", "steady"), ("TAB", "end"), ("SU2", "post"),
        ("MAX3", "pre"), ("SG3", "post"), ("OUT2", "att"), ("SU3", "post"), ("MOD6", "mod"), ("SD0", "post"),
        ("MOD7", "mod"), ("SD1", "post"))

    def __init__(self, b, kinds, before, loop_from=None):
        self.b, self.kinds = b, kinds
        self.att, self.pre, self.post, self.mod, self.end = (kind in kinds for kind in ("att", "pre", "post", "mod", "end"))
        self.uses, self.count = {}, [0, 0]
        for n, name in enumerate(name for name, kind in self.ORDER if kind in kinds):
            self.uses[name] = (n % 2, self.count[n % 2])
            self.count[n % 2] += 1
        self.base = list(before) if loop_from is None else [
            before[m] + (b - loop_from) * self.count[m] for m in range(2)]

    def use(self, name):
        m, n = self.uses[name]
        return m, self.base[m] + n


def adaln_moe_kernel(nc, x_in, wq, wk, wv, wo, gate, up, down, sgate, sup, sdown, c_in, wmod_in, out):
    ctx = ExitStack()
    with ctx:
        def sb(name, shape, dt=F32):
            return ctx.enter_context(nc.sbuf_tensor(name, shape, dt))

        def sem(name):
            return ctx.enter_context(nc.semaphore(name))

        def overlay(first, second):
            made, ends = [], []
            for specs in (first, second):
                with ExitStack() as here:
                    for name, shape, dt in specs:
                        made.append(here.enter_context(nc.sbuf_tensor(name, shape, dt)))
                    ends.append(nc.sbuf_base)
            sb(f"{first[0][0]}_{second[0][0]}", [P, max(ends) - nc.sbuf_base], mybir.dt.uint8)
            return made

        q_stack, k_stack, probs, up_sb, down_sb = overlay(
            [("q_stack", [P, H, S], F32R), ("k_stack", [P, H, S], F32R), ("probs", [P, 2 * G, S], F32)],
            [("up_sb", [P, KD * E * 2 * DM], F32), ("down_sb", [DM, E * D], F32)])
        comb = up_sb[:, 0:CR * TOPK * D].rearrange("p (r n) -> p r n", r=CR)
        wmod, c_rep, wo_sb, h2, sh_tanh, onehot, picked, lgT, ex, rank, chosen = overlay(
            [("wmod", [P, KD, 6 * D], F32), ("c_rep", [P, KD, B, P], F32), ("wo_sb", [P, KD, D], F32)],
            [("h2", [P, TJ, ROW], F32), ("sh_tanh", [P, 2, S], F32), ("onehot", [P, TJ * TOPK, E], F32),
             ("picked", [P, TJ * TOPK, E], F32), ("lgT", [E + 1, S], F32), ("ex", [P, TJ, E + TOPK], F32),
             ("rank", [P, TJ, E], F32), ("chosen", [P, TJ, E], F32)])
        qk_hi, sh_hidT = overlay([("qk_hi", [P, 4, S], F32R)], [("sh_hidT", [P, 4, S], F32)])
        xn, qk_lo = overlay([("xn", [P, TJ, D], F32)], [("qk_lo", [P, 4, S], F32R)])
        y_sb = qk_lo[:, :, :].bitcast(F32).rearrange("p c (h d) -> p (c h) d", h=2)
        o_norm, e_hid, e_hidT = overlay(
            [("o_norm", [P, TJ, D], F32)], [("e_hid", [P, 2, 2 * DM], F32), ("e_hidT", [DM, 2, 2 * P], F32)])
        v_ext, v_new, hT, oT_raw, max_hi, max_lo, xe, e_silu, tabf, tab, cnt, past, past_n = overlay(
            [("v_ext", [P, TJ, H, 32], F32), ("v_new", [P, TJ, H, HD], F32), ("hT", [P, KD, S], F32),
             ("oT_raw", [P, S], F32), ("max_hi", [G, S], F32R), ("max_lo", [G, S], F32R)],
            [("xe", [P, 2 * XP, ROW], F32), ("e_silu", [P, 2, 2 * DM], F32), ("tabf", [1, 2 * P], F32), ("tab", [1, 2 * P], I32), ("cnt", [P, E], F32),
             ("past", [P, E], F32), ("past_n", [P, E], F32)])
        oT = sb("oT", [P, KD, S])
        h2T = oT
        xeT = oT

        x = sb("x", [P, NT * D])
        wq_sb, wk_sb, wv_sb = (sb(n, [P, KD, D]) for n in ("wq_sb", "wk_sb", "wv_sb"))
        wo_g = sb("wo_g", [P, B * KD * D])
        mod_b = sb("mod_b", [P, B * 3 * D])
        gate_sb = sb("gate_sb", [P, KD, E + 1])
        sgate_sb, sup_sb = (sb(n, [P, KD, DS]) for n in ("sgate_sb", "sup_sb"))
        sdown_sb = sb("sdown_sb", [P, DS // P, D])
        modT = sb("modT", [P, 2 * KD * B])
        ident, ones, upper = (sb(n, [P, P]) for n in ("ident", "ones", "upper"))
        cT = sb("cT", [P, KD * B])
        ctmp = sb("ctmp", [P, KD * B])
        gtmp = sb("gtmp", [P, 2, D])
        pad_rows = sb("pad_rows", [P, ROW])
        bn = sb("bn", [P, NT, 6])
        mv = sb("mv", [P, NT, 2])
        rstd = sb("rstd", [P, NT])
        nmr = sb("nmr", [P, NT])
        mv2 = sb("mv2", [P, TJ, 2])
        nmr2 = sb("nmr2", [P, TJ])
        rstd2 = sb("rstd2", [P, TJ])
        veps = sb("veps", [P, NT])
        mhalf = sb("mhalf", [P, NT])
        max_q = sb("max_q", [P, 2, TJ, G])
        rsum = sb("rsum", [P, TJ, G])
        iota_e, base_i = sb("iota_e", [P, E], I32), sb("base_i", [P, E], I32)
        iota_ef, base_f = sb("iota_ef", [P, E]), sb("base_f", [P, E])
        thr_i, thr_f = sb("thr_i", [P, NT], I32), sb("thr_f", [P, NT])
        tile_i, tile_f = sb("tile_i", [P, 1], I32), sb("tile_f", [P, 1])
        home = sb("home", [P, NT * TOPK], I32)
        tails = sb("tails", [P, NT, TOPK, 2])
        dest = sb("dest", [P, 2 * YP], I32)
        lg = sb("lg", [P, TJ, E + 1])
        v8 = sb("v8", [P, TJ, 8])
        i8 = sb("i8", [P, TJ, 8], U32)
        z4, s4, sgt = (sb(n, [P, TJ]) for n in ("z4", "s4", "sgt"))
        p4, e4 = sb("p4", [P, TJ, TOPK]), sb("e4", [P, TJ, TOPK])
        sg = sb("sg", [P, NT])
        before = sb("before", [P, TJ + 1, E])
        slot_f = sb("slot_f", [P, TJ * TOPK])
        slot_i = sb("slot_i", [P, TJ * TOPK], I32)
        ntile, ctile = sb("ntile", [P, E]), sb("ctile", [P, E])
        tcol = sb("tcol", [P, 6])
        tcol2 = sb("tcol2", [P, 2])
        ps = ctx.enter_context(nc.psum_tensor("ps", [P, 8, 512], F32))

        scr = nc.dram_tensor("qk_scratch", [B * 8, P, S], F32, kind="Internal").ap()
        xs = nc.dram_tensor("dispatched", [E * CAP + P, ROW], F32, kind="Internal").ap()
        yk = nc.dram_tensor("results", [NY, D], F32, kind="Internal").ap()

        mod_ld, qkv_ld, w_ld, sh_ld, up_ld = (sem(n) for n in ("mod_ld", "qkv_ld", "w_ld", "sh_ld", "up_ld"))
        x_ld = [sem(f"x_ld{i}") for i in range(B)]
        pool_s, dve_s, consts = sem("pool_s"), sem("dve_s"), sem("consts")
        c_exp, c_rep_s, stats, rstd_s, nmr_s, modT_ps, modT_s = (
            sem(n) for n in ("c_exp", "c_rep_s", "stats", "rstd_s", "nmr_s", "modT_ps", "modT_s"))
        xn_ready, hi_done = sem("xn_ready"), sem("hi_done")
        misc_full = [sem("misc0_full"), sem("misc1_full")]
        misc_free = [sem("misc0_free"), sem("misc1_free")]
        spill = [sem("spill0"), sem("spill1")]
        stack_ld = [sem(f"stack_ld{g}") for g in range(NG)]
        sc_full, max_done, neg_hi, maxrow = sem("sc_full"), sem("max_done"), sem("neg_hi"), sem("maxrow")
        st_full, exp_done, pv_done, o_free, v_in_place = (
            sem(n) for n in ("st_full", "exp_done", "pv_done", "o_free", "v_in_place"))
        stats2, rstd2_s, tanh_s = sem("stats2"), sem("rstd2_s"), sem("tanh_s")
        h2_ready, ex_in, ex_out, chosen_s, slots_s = (
            sem(n) for n in ("h2_ready", "ex_in", "ex_out", "chosen_s", "slots_s"))
        h2_norm, top_s, weights_s, dest_s = (sem(n) for n in ("h2_norm", "top_s", "weights_s", "dest_s"))
        disp = [sem(f"disp{j}") for j in range(TJ)]
        tcol_s, tab_s, pad_s = sem("tcol_s"), sem("tab_s"), sem("pad_s")
        xe_ld = [sem(f"xe_ld{i}") for i in range(XP)]
        t_full, t_done, u_full, esilu_s, hid_s, ht_full, ht_done, y_full, y_done = (
            sem(n) for n in ("t_full", "t_done", "u_full", "esilu_s", "hid_s", "ht_full", "ht_done", "y_full", "y_done"))
        y_out = [sem(f"y_out{i}") for i in range(YP)]
        comb_ld = [sem(f"comb_ld{i}") for i in range(CR)]
        part_s, prod_s, x3_done, stored = (sem(n) for n in ("part_s", "prod_s", "x3_done", "stored"))
        passed = sem("passed")

        SC, ST, O, MISC = (0, 1, 2), (3, 4), 5, (6, 7)

        LOOP0, LOOP1 = 1, B - 1
        lead = Turn(-1, {"pre"}, [0, 0])
        first = Turn(0, {"att", "pre", "mod"}, lead.count)
        at_loop = [lead.count[m] + first.count[m] for m in range(2)]

        def middle(b):
            return Turn(b, {"att", "pre", "post", "steady"}, at_loop, LOOP0)

        per_turn = middle(LOOP0).count
        last = Turn(B - 1, {"att", "post", "steady"}, [at_loop[m] + (LOOP1 - LOOP0) * per_turn[m] for m in range(2)])
        drain = Turn(B, {"post", "end"}, [last.base[m] + last.count[m] for m in range(2)])
        all_uses = [drain.base[m] + drain.count[m] for m in range(2)]
        PAIRS = MT // 2

        def apart(eng):
            eng.sem_inc(passed, 1)

        def full(eng, t, name):
            m, n = t.use(name)
            eng.wait_ge(misc_full[m], n + 1)
            return ps[:, MISC[m], :]

        def frees(ins, t, name):
            ins.then_inc(misc_free[t.use(name)[0]], 1)

        def own_free(eng, t, name):
            m, n = t.use(name)
            eng.wait_ge(misc_free[m], n + 1)

        def above(eng, sem_, value):
            if not isinstance(value, int) or value > 0:
                eng.wait_ge(sem_, value)

        block = ctx.enter_context(nc.Block())

        @block.sync
        def _(sp):
            sp.dma_start(cT[:, :].rearrange("p (k b) -> p k b", k=KD), c_in.rearrange("(k p) b -> p k b", p=P)).then_inc(mod_ld, 16)
            sp.dma_start(wmod[:, :, 0:2 * D], wmod_in[:, 0:2 * D].rearrange("(k p) n -> p k n", p=P)).then_inc(mod_ld, 16)
            for w_d, w_s in ((wq, wq_sb), (wk, wk_sb), (wv, wv_sb)):
                sp.dma_start(w_s[:, :, :], w_d.rearrange("(k p) n -> p k n", p=P)).then_inc(qkv_ld, 16)

            def spill_half(t, half):
                for c in (2 * half, 2 * half + 1):
                    m, n = t.use(f"QK{c}")
                    sp.wait_ge(misc_free[m], n + 1)
                    apart(sp)
                for comp, src in ((0, qk_hi), (1, qk_lo)):
                    sp.dma_start(scr[bass.ds(8 * (t.b + 1) + 4 * half + 2 * comp, 2), :, :].rearrange("q p n -> p q n"),
                                 src[:, 2 * half:2 * half + 2, :].bitcast(F32)).then_inc(spill[half], 16)

            def load_group(b, g):
                sp.wait_ge(spill[g // 2], 32 * b + 32)
                apart(sp)
                above(sp, pv_done, 16 * b + 4 * g - 12 if not isinstance(b, int) or b else 0)
                apart(sp)
                for r in range(4):
                    for qk, stack, comp in ((0, q_stack, r % 2), (1, k_stack, r // 2)):
                        rows = scr[bass.ds(8 * b + 4 * (g // 2) + 2 * comp + qk, 1), 64 * (g % 2):64 * (g % 2) + 64, :]
                        sp.dma_start(stack[16 * r:16 * r + 16, G * g:G * g + G, :].bitcast(F32),
                                     rows.rearrange("o (h d) n -> (o d) h n", d=HD)).then_inc(stack_ld[g], 16)

            def max_rows(t, g):
                sp.wait_ge(consts, 3)
                m, n = t.use(f"MAX{g}")
                sp.wait_ge(misc_free[m], n + 1)
                apart(sp)
                h = G * ((g + 1) % NG)
                for row, src in ((64, max_hi), (65, max_lo)):
                    sp.dma_start(q_stack[row:row + 1, h:h + G, :].bitcast(F32), src[:, :].bitcast(F32)).then_inc(maxrow, 16)

            def turn(t):
                max_rows(t, 0)
                load_group(t.b, 3)
                if t.pre:
                    spill_half(t, 0)
                    spill_half(t, 1)
                for g in (1, 2):
                    max_rows(t, g)
                    if t.pre:
                        load_group(t.b + 1, g - 1)
                if t.pre:
                    max_rows(t, 3)
                    load_group(t.b + 1, 2)

            for half in range(2):
                spill_half(lead, half)
                load_group(0, 2 * half)
                if half == 0:
                    load_group(0, 1)
            sp.dma_start(wmod[:, :, 2 * D:6 * D], wmod_in[:, 2 * D:6 * D].rearrange("(k p) n -> p k n", p=P)).then_inc(w_ld, 16)
            for w_d, w_s in ((wo, wo_sb), (gate, gate_sb)):
                sp.dma_start(w_s[:, :, :], w_d.rearrange("(k p) n -> p k n", p=P)).then_inc(w_ld, 16)
            max_rows(lead, 3)
            for w_d, w_s in ((sgate, sgate_sb), (sup, sup_sb), (sdown, sdown_sb)):
                sp.dma_start(w_s[:, :, :], w_d.rearrange("(k p) n -> p k n", p=P)).then_inc(sh_ld, 16)
            turn(first)
            with sp.Fori(LOOP0, LOOP1, 1) as b:
                turn(middle(b))
            turn(last)
            sp.wait_ge(consts, 3)
            with sp.Fori(0, E + 1, 1) as e:
                sp.dma_start(xs[bass.ds(e * CAP, P), :], pad_rows[:, :]).then_inc(pad_s, 16)
            sp.wait_ge(pv_done, 4 * NG * B)
            sp.wait_ge(h2_ready, B)
            for k in range(KD):
                sp.dma_start(up_sb[:, k * E * 2 * DM:(k + 1) * E * 2 * DM],
                             up[k * P:(k + 1) * P, :]).then_inc(up_ld, 16)
            sp.dma_start(down_sb[:, :], down).then_inc(up_ld, 16)
            sp.wait_ge(pad_s, 16 * (E + 1))
            sp.wait_ge(tab_s, 1)
            for j in range(TJ):
                sp.wait_ge(disp[j], 16 * B * TOPK)

            def load_pair(q, r):
                for half in range(2):
                    at = sp.value_load(tab[0:1, bass.ds(P + 2 * q + half, 1)], min_val=0, max_val=E * CAP)
                    sp.dma_start(xe[:, 2 * r + half, :], xs[bass.ds(at, P), :]).then_inc(xe_ld[r], 16)

            for r in range(XP):
                load_pair(r, r)
            with sp.Fori(1, PAIRS // XP, 1) as i:
                for r in range(XP):
                    sp.wait_ge(y_out[r % YP], 32 * (XP // YP * (i - 1) + r // YP + 1))
                    apart(sp)
                    load_pair(XP * i + r, r)
            for r in range(YP):
                sp.wait_ge(y_out[r], 32 * (PAIRS // YP))
            for t in range(NT):
                if t >= CR:
                    sp.wait_ge(part_s, t - CR + 1)
                sp.dma_start(comb[:, t % CR, :], yk[t * P * TOPK:(t + 1) * P * TOPK, :].rearrange(
                    "(p k) d -> p (k d)", k=TOPK)).then_inc(comb_ld[t % CR], 16)

        @block.gpsimd
        def _(pool):
            st = Steps(pool, pool_s)
            st.did(pool.memset(ident[:, :], 0.0))
            st.did(pool.memset(ones[:, :], 1.0))
            st.did(pool.memset(upper[:, :], 1.0))
            st.did(pool.iota(iota_e[:, :], pattern=[[1, E]], base=0, channel_multiplier=0))
            st.did(pool.iota(base_i[:, :], pattern=[[CAP, E]], base=P, channel_multiplier=0))
            st.did(pool.iota(thr_i[:, :], pattern=[[P, NT]], base=0, channel_multiplier=0))
            st.did(pool.iota(tile_i[:, :], pattern=[[0, 1]], base=0, channel_multiplier=1))
            st.did(pool.iota(home[:, :], pattern=[[P * TOPK, NT], [1, TOPK]], base=0, channel_multiplier=TOPK))
            st.did(pool.memset(mhalf[:, :], -0.5))
            st.did(pool.memset(pad_rows[:, :], 0.0))
            st.did(pool.memset(before[:, TJ, :], 0.0))
            st.wait()
            st.did(pool.affine_select(out=ident[:, :], in_=ident[:, :], compare_op=ALU.not_equal, fill=1.0, base=0,
                                      pattern=[[-1, P]], channel_multiplier=1))
            st.did(pool.affine_select(out=upper[:, :], in_=upper[:, :], compare_op=ALU.is_gt, fill=0.0, base=0,
                                      pattern=[[1, P]], channel_multiplier=-1))
            st.did(pool.memset(pad_rows[:, D:D + 1], float(SKIP)))
            st.wait()
            pool.sem_inc(consts, 1)

            def deviations(lo, hi, turn):
                pool.wait_ge(stats, turn)
                st.then(pool.tensor_scalar(veps[:, lo:hi], mv[:, lo:hi, 1], EPS, None, ALU.add))
                pool.tensor_tensor(rstd[:, lo:hi], veps[:, lo:hi], mhalf[:, lo:hi], ALU.pow).then_inc(rstd_s, 1)
                pool.wait_ge(rstd_s, turn)

            deviations(0, TJ, 1)
            pool.memset(v_ext[:, :, :, :], 1.0).then_inc(consts, 1)
            pool.wait_ge(consts, 2)
            st.then(pool.memset(k_stack[64:128, :, :].bitcast(F32), 0.0))
            st.then(pool.memset(k_stack[64:66, :, :].bitcast(F32), 1.0))
            pool.memset(q_stack[64:128, :, :].bitcast(F32), 0.0).then_inc(consts, 1)
            pool.wait_ge(consts, 3)
            deviations(TJ, NT, 2)

            def place_values(b, g, t):
                if t is not None:
                    m, n = t.use("V1")
                    pool.wait_ge(misc_free[m], n + 1)
                    apart(pool)
                above(pool, pv_done, 16 * b + 4 * g - 12 if not isinstance(b, int) or b else 0)
                apart(pool)
                pool.tensor_copy(v_ext[:, :, G * g:G * g + G, 0:HD], v_new[:, :, G * g:G * g + G, :]).then_inc(v_in_place, 1)
                pool.wait_ge(v_in_place, 4 * b + g + 1)
                apart(pool)

            def second_norm(t):
                p = t.b - 1
                pool.wait_ge(stats2, p + 1)
                apart(pool)
                st.then(pool.tensor_scalar(veps[:, 0:TJ], mv2[:, :, 1], EPS, None, ALU.add))
                st.then(pool.tensor_tensor(rstd2[:, :], veps[:, 0:TJ], mhalf[:, 0:TJ], ALU.pow))
                st.then(pool.tensor_tensor(nmr2[:, :], mv2[:, :, 0], rstd2[:, :], ALU.mult))
                apart(pool)
                pool.tensor_scalar(nmr2[:, :], nmr2[:, :], -1.0, None, ALU.mult).then_inc(rstd2_s, 1)
                if t.end:
                    pool.wait_ge(rstd2_s, p + 1)
                    return
                pool.wait_ge(h2_norm, p + 1)
                apart(pool)
                st.then(pool.tensor_tensor(h2[:, :, 0:D], h2[:, :, 0:D],
                                           mod_b[:, bass.ds(p * (3 * D) + D, D)].unsqueeze(1).to_broadcast([P, TJ, D]), ALU.mult))
                pool.tensor_tensor(h2[:, :, 0:D], h2[:, :, 0:D],
                                   mod_b[:, bass.ds(p * (3 * D), D)].unsqueeze(1).to_broadcast([P, TJ, D]), ALU.add).then_inc(h2_ready, 1)
                pool.wait_ge(h2_ready, p + 1)
                apart(pool)

            def choices(t):
                pool.wait_ge(top_s, t.b)
                apart(pool)
                st.then(pool.tensor_copy(before[:, 0, :], before[:, TJ, :]))
                four = onehot[:, :, :].rearrange("p (j k) e -> p j k e", k=TOPK)
                st.then(pool.tensor_tensor(chosen[:, :, :], four[:, :, 0, :], four[:, :, 1, :], ALU.add))
                st.then(pool.tensor_tensor(chosen[:, :, :], chosen[:, :, :], four[:, :, 2, :], ALU.add))
                st.then(pool.tensor_tensor(chosen[:, :, :], chosen[:, :, :], four[:, :, 3, :], ALU.add))
                for j in range(TJ - 1):
                    st.then(pool.tensor_tensor(before[:, j + 1, :], before[:, j, :], chosen[:, j, :], ALU.add))
                pool.tensor_tensor(before[:, TJ, :], before[:, TJ - 1, :], chosen[:, TJ - 1, :], ALU.add).then_inc(chosen_s, 1)
                pool.wait_ge(chosen_s, t.b)
                apart(pool)

            def turn(t):
                if t.att:
                    place_values(t.b, 3, None)
                if t.post:
                    second_norm(t)
                if t.pre:
                    place_values(t.b + 1, 0, t)
                    place_values(t.b + 1, 1, None)
                if t.post:
                    choices(t)
                    dispatch(t)
                if t.pre:
                    place_values(t.b + 1, 2, None)

            def dispatch(t):
                p = t.b - 1
                pool.wait_ge(slots_s, p + 1)
                apart(pool)
                pool.wait_ge(weights_s, p + 1)
                apart(pool)
                for k in range(TOPK):
                    for j in range(TJ):
                        if k:
                            pool.wait_ge(disp[j], 64 * p + 16 * k)
                            apart(pool)
                        st.then(pool.tensor_copy(h2[:, j, D:D + 2], tails[:, bass.ds(TJ * p + j, 1), k, :]))
                        apart(pool)
                        pool.indirect_dma_start(out=xs, out_offset=bass.IndirectOffsetOnAxis(
                            ap=slot_i[:, TOPK * j + k:TOPK * j + k + 1], axis=0), in_=h2[:, j, :], in_offset=None).then_inc(disp[j], 16)
                for j in range(TJ):
                    pool.wait_ge(disp[j], 64 * p + 64)
                    apart(pool)

            place_values(0, 0, lead)
            place_values(0, 1, None)
            place_values(0, 2, None)
            turn(first)
            with pool.Fori(LOOP0, LOOP1, 1) as b:
                st.enter(b - LOOP0, POOL_STEPS)
                turn(middle(b))
            st.leave(LOOP1 - LOOP0)
            turn(last)
            turn(drain)
            with pool.Fori(0, PAIRS // XP, 1) as i:
                for r in range(XP):
                    pool.wait_ge(y_done, XP * i + r + 1)
                    apart(pool)
                    at = 2 * (r % YP)
                    pool.tensor_copy(dest[:, at:at + 2], xe[:, 2 * r:2 * r + 2, D]).then_inc(dest_s, 1)
                    pool.wait_ge(dest_s, XP * i + r + 1)
                    apart(pool)
                    for half in range(2):
                        n = 2 * r + half
                        pool.indirect_dma_start(out=yk, out_offset=bass.IndirectOffsetOnAxis(
                            ap=dest[:, at + half:at + half + 1], axis=0), in_=y_sb[:, n % (2 * YP), :], in_offset=None,
                            bounds_check=NY - 1, oob_is_err=False).then_inc(y_out[r % YP], 16)
            for t in range(NT):
                pool.wait_ge(prod_s, t + 1)
                pool.tensor_tensor(x[:, t * D:(t + 1) * D], x[:, t * D:(t + 1) * D], y_sb[:, t % CR, :], ALU.add).then_inc(x3_done, 1)
                pool.wait_ge(x3_done, t + 1)

        @block.scalar
        def _(act):
            def load_x(b):
                act.dma_start(x[:, b * TJ * D:(b + 1) * TJ * D].rearrange("p (j d) -> p j d", d=D),
                              x_in[b].rearrange("(j p) d -> p j d", p=P)).then_inc(x_ld[b], 16)
            load_x(0)
            act.wait_ge(mod_ld, 32)
            act.activation(ctmp[:, :], cT[:, :], ACT.Exp, scale=-1.0).then_inc(c_exp, 1)
            for b in range(1, B):
                load_x(b)

            def normalise(t):
                n = t.b + 1
                for half in range(2):
                    above(act, spill[half], 32 * n)
                    apart(act)
                for j in range(TJ):
                    act.activation(xn[:, j, :], x[:, bass.ds((TJ * n + j) * D, D)], ACT.Identity,
                                   scale=rstd[:, bass.ds(TJ * n + j, 1)], bias=nmr[:, bass.ds(TJ * n + j, 1)]).then_inc(xn_ready, 1)

            def to_hT(t, k):
                n = t.b + 1
                frees(act.activation(hT[:, k, :], full(act, t, f"TP{k}"), ACT.Identity,
                                     scale=modT[:, bass.ds((2 + k) * B + n, 1)], bias=modT[:, bass.ds(k * B + n, 1)]), t, f"TP{k}")

            def round_qk(t, c):
                act.activation(qk_hi[:, c, :], full(act, t, f"QK{c}"), ACT.Copy).then_inc(hi_done, 1)

            def values_out(t, m):
                src = full(act, t, f"V{m}")
                above(act, v_in_place, 4 * (t.b + 1))
                frees(act.activation(v_new[:, 2 * m:2 * m + 2, :, :], src.rearrange("p (j h d) -> p j h d", j=2, d=HD), ACT.Copy), t, f"V{m}")

            def neg_max_hi(t, g):
                G_next = NG * t.b + g + 1
                src = full(act, t, f"MAX{g}")
                above(act, maxrow, 32 * G_next)
                act.activation(max_hi[:, :], src[0:G, :], ACT.Copy, scale=-1.0).then_inc(neg_hi, 1)

            def outputs_out(b, g):
                act.wait_ge(pv_done, 16 * b + 4 * g)
                act.activation(oT_raw[:, :], ps[:, O, :], ACT.Copy).then_inc(o_free, 1)

            def copy_out(t, name, to, part=None):
                src = full(act, t, name)
                frees(act.activation(to, src if part is None else part(src), ACT.Copy), t, name)

            def second_norm(t):
                p = t.b - 1
                act.wait_ge(rstd2_s, p + 1)
                for j in range(TJ):
                    ins = act.activation(h2[:, j, 0:D], x[:, bass.ds((TJ * p + j) * D, D)], ACT.Identity,
                                         scale=rstd2[:, j:j + 1], bias=nmr2[:, j:j + 1])
                ins.then_inc(h2_norm, 1)

            def tanh_gate(t, c):
                act.activation(sh_tanh[:, c % 2, :], full(act, t, f"SG{c}"), ACT.Tanh, scale=0.5).then_inc(tanh_s, 1)

            def between(t, g, u):
                if u == 0 and g == 0 and t.pre:
                    normalise(t)
                if u == 2 and (t.att and g < 3 or t.pre and g == 3):
                    neg_max_hi(t, g)
                if u == 3:
                    if t.att and (g or t.post) or t.post and g == 0:
                        outputs_out(t.b, g)
                if g == 0:
                    if t.pre and u in (4, 5):
                        to_hT(t, u - 4)
                    if t.pre and u in (7, 10, 12):
                        round_qk(t, {7: 0, 10: 1, 12: 2}[u])
                    if t.post and u == 9:
                        for k in range(KD):
                            copy_out(t, f"OT{k}", oT[:, k, :])
                if g == 1:
                    if t.pre and u == 1:
                        round_qk(t, 3)
                    if t.post and u == 4:
                        second_norm(t)
                    if t.pre and u in (8, 10):
                        values_out(t, u // 2 - 4)
                    if t.post and u in (13, 14):
                        copy_out(t, f"HT{u - 13}", h2T[:, u - 13, :])
                if t.post:
                    if (g, u) == (2, 0):
                        copy_out(t, "LOG", lgT[:, :], lambda s: s[0:E + 1, :])
                    if (g, u) == (2, 2):
                        copy_out(t, "LGT", lg[:, :, :],
                                 lambda s: s[:, 0:TJ * 64].rearrange("p (j e) -> p j e", j=TJ)[:, :, 0:E + 1])
                    if (g, u) in ((2, 4), (2, 9), (2, 12), (3, 4)):
                        tanh_gate(t, {4: 0, 9: 1, 12: 2}[u] if g == 2 else 3)
                    if (g, u) == (2, 8):
                        act.wait_ge(ex_in, 2 * t.b)
                        act.activation(ex[:, :, :], ex[:, :, :], ACT.Exp).then_inc(ex_out, 1)
                        act.activation(sgt[:, :], lg[:, :, E], ACT.Exp, scale=-1.0).then_inc(ex_out, 1)

            def turn(t):
                for g in range(NG):
                    for u in range(16):
                        if t.att:
                            act.wait_ge(st_full, 64 * t.b + 16 * g + u + 1)
                            if u % 4 == 0:
                                above(act, pv_done, 16 * t.b + 4 * g + u // 4 - 1)
                            act.activation(probs[:, u % 8, :], ps[:, ST[u % 2], :], ACT.Exp).then_inc(exp_done, 1)
                        between(t, g, u)

            act.wait_ge(nmr_s, 1)
            normalise(lead)
            act.wait_ge(modT_s, 1)
            for k in range(KD):
                to_hT(lead, k)
            for c in range(4):
                round_qk(lead, c)
            for m in range(2):
                values_out(lead, m)
            neg_max_hi(lead, 3)
            act.wait_ge(nmr_s, 2)
            turn(first)
            with act.Fori(LOOP0, LOOP1, 1) as b:
                turn(middle(b))
            turn(last)
            turn(drain)

            def silu(q, r):
                act.wait_ge(u_full, q + 1)
                above(act, hid_s, q - 1)
                act.activation(e_silu[:, r % 2, :].rearrange("p (h n) -> p h n", h=2),
                               ps[:, 2 + r % 2, 0:4 * DM].rearrange("p (h n) -> p h n", h=2)[:, :, 0:DM], ACT.Silu).then_inc(esilu_s, 1)

            def result_out(q, r, i=0):
                act.wait_ge(y_full, q + 1)
                above(act, y_out[r % YP], 32 * (XP // YP * i + r // YP))
                y_at = 2 * (r % YP)
                act.activation(y_sb[:, y_at:y_at + 2, :].rearrange("p h d -> p (h d)"), ps[:, 6 + r % 2, :],
                               ACT.Copy).then_inc(y_done, 1)

            def hidden_out(q, r):
                act.wait_ge(ht_full, q + 1)
                above(act, y_full, q - 1)
                act.activation(e_hidT[:, r % 2, :], ps[0:DM, 4 + r % 2, 0:2 * P], ACT.Copy).then_inc(ht_done, 1)

            def slot(i, q, r, begun, ended=0):
                if begun >= 1 and ended < 1:
                    silu(q - 1, r - 1)
                if begun >= 2 and ended < 2:
                    hidden_out(q - 2, r - 2)
                if begun >= 3:
                    result_out(q - 3, r - 3, i)

            for r in range(XP):
                slot(0, r, r, r)
            with act.Fori(1, PAIRS // XP, 1) as i:
                for r in range(XP):
                    slot(i, XP * i + r, r, XP)
            for r in range(3):
                slot(PAIRS // XP, PAIRS + r, r, XP, r)
            for t in range(NT):
                act.wait_ge(x3_done, t + 1)
                b, j = divmod(t, TJ)
                act.dma_start(out[b, j * P:(j + 1) * P, :], x[:, t * D:(t + 1) * D]).then_inc(stored, 16)
            act.wait_ge(stored, 16 * NT)

        @block.tensor
        def _(pe):
            pe.wait_ge(mod_ld, 32)
            pe.wait_ge(c_rep_s, 1)
            for c in range(2 * KD):
                for k in range(KD):
                    mm = pe.matmul(ps[:, 0, c * B:(c + 1) * B], wmod[:, k, c * P:(c + 1) * P], c_rep[:, k, :, 0],
                                   start=(k == 0), stop=(k == KD - 1))
            mm.then_inc(modT_ps, 1)
            pe.wait_ge(consts, 1)

            def claim(t, name):
                m, n = t.use(name)
                above(pe, misc_free[m], n)
                return ps[:, MISC[m], :]

            def filled(ins, t, name):
                ins.then_inc(misc_full[t.use(name)[0]], 1)

            def rows_to_columns(t, name, src, k):
                bank = claim(t, name)
                for j in range(TJ):
                    mm = pe.transpose(bank[:, j * P:(j + 1) * P], src[:, j, k * P:(k + 1) * P], ident[:, :])
                filled(mm, t, name)

            def written(t, name):
                m, n = t.use(name)
                pe.wait_ge(misc_free[m], n + 1)

            def project_qk(t, c):
                if c == 0:
                    written(t, "TP0")
                    written(t, "TP1")
                bank = claim(t, f"QK{c}")
                w = (wq_sb, wk_sb)[c % 2]
                for k in range(KD):
                    mm = pe.matmul(bank, w[:, k, (c // 2) * P:(c // 2 + 1) * P], hT[:, k, :], start=(k == 0), stop=(k == KD - 1))
                filled(mm, t, f"QK{c}")

            def project_v(t, m):
                bank = claim(t, f"V{m}")
                for j in (2 * m, 2 * m + 1):
                    for k in range(KD):
                        mm = pe.matmul(bank[:, (j % 2) * D:(j % 2 + 1) * D], hT[:, k, j * P:(j + 1) * P], wv_sb[:, k, :],
                                       start=(k == 0), stop=(k == KD - 1))
                filled(mm, t, f"V{m}")

            def score(b, g, n, banks=SC):
                qt, i = divmod(n, G)
                if n == 0:
                    pe.wait_ge(stack_ld[g], 128 * b + 128)
                u = 16 * g + n
                above(pe, max_done, 64 * b + max(u + 1 - len(banks), 0))
                pe.matmul(ps[:, banks[u % len(banks)], :], q_stack[0:64, G * g + i, qt * P:(qt + 1) * P], k_stack[0:64, G * g + i, :],
                          start=True, stop=True).then_inc(sc_full, 1)

            def turn_max(t, g):
                pe.wait_ge(max_done, 64 * t.b + 16 * g + 32)
                bank = claim(t, f"MAX{g}")
                for qt in range(TJ):
                    mm = pe.transpose(bank[0:G, qt * P:(qt + 1) * P], max_q[:, (g + 1) % 2, qt, :], ident[:, :])
                filled(mm, t, f"MAX{g}")

            def scoreT(b, g, n):
                kt, i = divmod(n, G)
                u = 16 * g + n
                if n == 0:
                    pe.wait_ge(maxrow, 32 * (NG * b + g) + 32)
                above(pe, exp_done, 64 * b + u - 1)
                pe.matmul(ps[:, ST[u % 2], :], k_stack[:, G * g + i, kt * P:(kt + 1) * P], q_stack[:, G * g + i, :],
                          start=True, stop=True).then_inc(st_full, 1)

            def values(b, g, kt):
                pe.wait_ge(exp_done, 64 * b + 16 * g + 4 * kt + 4)
                if kt == 0:
                    above(pe, o_free, NG * b + g)
                    pe.wait_ge(v_in_place, NG * b + g + 1)
                for i in range(G):
                    mm = pe.matmul(ps[32 * i:32 * i + 32, O, :], v_ext[:, kt, G * g + i, :], probs[:, (4 * kt + i) % 8, :],
                                   start=(kt == 0), stop=(kt == TJ - 1), tile_position=(0, 32 * i))
                mm.then_inc(pv_done, 1)

            def outputs_back(t, b, g):
                pe.wait_ge(o_free, NG * b + g + 1)
                bank = claim(t, f"OUT{g}")
                for qt in range(TJ):
                    mm = pe.transpose(bank[:, qt * P:(qt + 1) * P], oT_raw[:, qt * P:(qt + 1) * P], ident[:, :])
                filled(mm, t, f"OUT{g}")

            def project_o(t, m):
                if m == 0:
                    written(t, "OT0")
                    written(t, "OT1")
                bank = claim(t, f"WO{m}")
                p = t.b - 1
                for j in (2 * m, 2 * m + 1):
                    for k in range(KD):
                        mm = pe.matmul(bank[:, (j % 2) * D:(j % 2 + 1) * D], oT[:, k, j * P:(j + 1) * P],
                                       wo_g[:, bass.ds(p * (KD * D) + k * D, D)], start=(k == 0), stop=(k == KD - 1))
                filled(mm, t, f"WO{m}")

            def modulate(t, s):
                if s == 0:
                    pe.wait_ge(w_ld, 48)
                bank = claim(t, f"MOD{s}")
                for k in range(KD):
                    mm = pe.matmul(bank, c_rep[:, k, s // 2, :], wmod[:, k, (2 + 2 * (s % 2)) * D:(4 + 2 * (s % 2)) * D],
                                   start=(k == 0), stop=(k == KD - 1))
                filled(mm, t, f"MOD{s}")

            def logits(t):
                written(t, "HT0")
                written(t, "HT1")
                bank = claim(t, "LOG")
                for k in range(KD):
                    mm = pe.matmul(bank[0:E + 1, :], gate_sb[:, k, :], h2T[:, k, :], start=(k == 0), stop=(k == KD - 1))
                filled(mm, t, "LOG")

            def turn_logits(t):
                written(t, "LOG")
                apart(pe)
                bank = claim(t, "LGT")
                apart(pe)
                for j in range(TJ):
                    mm = pe.transpose(bank[:, 64 * j:64 * j + E + 1], lgT[:, j * P:(j + 1) * P], ident[0:E + 1, 0:E + 1])
                filled(mm, t, "LGT")

            def ranks(t):
                pe.wait_ge(chosen_s, t.b)
                bank = claim(t, "RANK")
                pe.matmul(bank[:, 0:TJ * E], upper[:, :], chosen[:, :, :], start=True, stop=False)
                filled(pe.matmul(bank[:, 0:TJ * E], ones[:, :], before[:, 0:TJ, :], start=False, stop=True), t, "RANK")

            def counts(t):
                filled(pe.matmul(claim(t, "CNT")[:, 0:E], ones[:, :], before[:, TJ, :], start=True, stop=True), t, "CNT")

            def table(t):
                pe.wait_ge(tcol_s, 1)
                bank = claim(t, "TAB")
                for c in range(2):
                    mm = pe.matmul(bank[0:1, c * P:(c + 1) * P], tcol2[:, c:c + 1], ident[:, :], start=True, stop=True)
                filled(mm, t, "TAB")

            def shared_up(t, name, w, c):
                bank = claim(t, f"{name}{c}")
                for k in range(KD):
                    mm = pe.matmul(bank, w[:, k, c * P:(c + 1) * P], h2T[:, k, :], start=(k == 0), stop=(k == KD - 1))
                filled(mm, t, f"{name}{c}")

            def shared_down(t, m):
                if m == 0:
                    written(t, "SU3")
                    apart(pe)
                bank = claim(t, f"SD{m}")
                for j in (2 * m, 2 * m + 1):
                    for c in range(4):
                        mm = pe.matmul(bank[:, (j % 2) * D:(j % 2 + 1) * D], sh_hidT[:, c, j * P:(j + 1) * P], sdown_sb[:, c, :],
                                       start=(c == 0), stop=(c == 3))
                filled(mm, t, f"SD{m}")

            def between(t, g, u):
                if t.pre and (g, u) == (1, 0):
                    project_qk(t, 3)
                if t.post and (g, u) == (2, 1):
                    turn_logits(t)
                if t.att and (g or t.post) and u == 1 or t.post and (g, u) == (0, 1):
                    values(t.b if g else t.b - 1, (g - 1) % NG, TJ - 1)
                if u == 1 and (t.att and g < 3 or t.pre and g == 3):
                    turn_max(t, g)
                if t.att and u in (5, 9, 13):
                    values(t.b, g, u // 4 - 1)
                if g == 0:
                    if t.pre and u == 4:
                        for k in range(KD):
                            tokens_to_columns(t, k)
                    if t.post and u == 5:
                        outputs_back(t, t.b - 1, 3)
                    if t.mod and u == 6:
                        modulate(t, 0)
                    if t.pre and u in (7, 10, 12):
                        project_qk(t, {7: 0, 10: 1, 12: 2}[u])
                    if t.post and u == 9:
                        written(t, "OUT3")
                        for k in range(KD):
                            rows_to_columns(t, f"OT{k}", o_norm, k)
                    if t.mod and u == 11:
                        modulate(t, 1)
                    if t.post and u in (11, 14):
                        project_o(t, u // 14)
                elif t.att and u == 5:
                    outputs_back(t, t.b, g - 1)
                if g == 1:
                    if t.pre and u in (7, 9):
                        project_v(t, u // 9)
                    if t.mod and u in (10, 14):
                        modulate(t, u // 4)
                    if t.post and u == 12:
                        pe.wait_ge(h2_ready, t.b)
                        for k in range(KD):
                            rows_to_columns(t, f"HT{k}", h2, k)
                    if t.post and u == 15:
                        logits(t)
                if g == 2:
                    if t.post and u in (3, 8, 12):
                        shared_up(t, "SG", sgate_sb, {3: 0, 8: 1, 12: 2}[u])
                    if t.post and u == (6 if t.end else 13):
                        ranks(t)
                    if t.end and u == 6:
                        counts(t)
                    if t.end and u == 14:
                        table(t)
                    if t.post and u in (7, 10, 15):
                        shared_up(t, "SU", sup_sb, {7: 0, 10: 1, 15: 2}[u])
                    if t.mod and u in (8, 12):
                        modulate(t, 2 + u // 4)
                if g == 3:
                    if t.post and u == 3:
                        shared_up(t, "SG", sgate_sb, 3)
                    if t.post and u == 7:
                        shared_up(t, "SU", sup_sb, 3)
                    if t.mod and u in (8, 12):
                        modulate(t, 4 + u // 4)
                    if t.post and u in (9, 12):
                        shared_down(t, u // 12)

            def tokens_to_columns(t, k):
                if k == 0:
                    pe.wait_ge(xn_ready, TJ * (t.b + 1) + TJ)
                rows_to_columns(t, f"TP{k}", xn, k)

            def turn(t):
                for g in range(NG):
                    for u in range(16):
                        if t.att:
                            scoreT(t.b, g, u)
                            if g < 2:
                                score(t.b, g + 2, u)
                            elif t.pre:
                                score(t.b + 1, g - 2, u)
                        between(t, g, u)

            for k in range(KD):
                tokens_to_columns(lead, k)
            pe.wait_ge(qkv_ld, 48)
            for c in range(4):
                project_qk(lead, c)
            for m in range(2):
                project_v(lead, m)
            for n in range(16):
                score(0, 0, n, SC + ST)
            turn_max(lead, 3)
            for n in range(16):
                score(0, 1, n, SC + ST)
            pe.wait_ge(max_done, 32)
            turn(first)
            pe.wait_ge(sh_ld, 48)
            with pe.Fori(LOOP0, LOOP1, 1) as b:
                turn(middle(b))
            turn(last)
            turn(drain)
            for m in range(2):
                pe.wait_ge(misc_free[m], all_uses[m])
            pe.wait_ge(up_ld, 48)
            pe.wait_ge(tab_s, 1)

            def experts(w):
                word = pe.value_load(tab[0:1, bass.ds(w, 1)], min_val=0, max_val=(1 << 20) - 1)
                return [pe.snap((word >> (5 * n)) & 31) for n in range(4)]

            def turn_rows(i, q, r):
                pe.wait_ge(xe_ld[r], 32 * i + 32)
                above(pe, t_done, q - 1)
                for half in range(2):
                    for k in range(KD):
                        mm = pe.transpose(ps[:, r % 2, (2 * half + k) * P:(2 * half + k + 1) * P],
                                          xe[:, 2 * r + half, k * P:(k + 1) * P], ident[:, :])
                mm.then_inc(t_full, 1)

            def widen(q, r, es):
                pe.wait_ge(t_done, q + 1)
                above(pe, hid_s, q - 1)
                for half in range(2):
                    for k in range(KD):
                        mm = pe.matmul(ps[:, 2 + r % 2, 2 * DM * half:2 * DM * (half + 1)],
                                       xeT[:, r % 2, (2 * half + k) * P:(2 * half + k + 1) * P],
                                       up_sb[:, bass.ds(es[half] * (2 * DM) + k * E * 2 * DM, 2 * DM)],
                                       start=(k == 0), stop=(k == KD - 1))
                mm.then_inc(u_full, 1)

            def turn_hidden(q, r):
                pe.wait_ge(hid_s, q + 1)
                above(pe, ht_done, q - 1)
                for half in range(2):
                    mm = pe.transpose(ps[0:DM, 4 + r % 2, half * P:(half + 1) * P],
                                      e_hid[:, r % 2, half * DM:(half + 1) * DM], ident[:, :])
                mm.then_inc(ht_full, 1)

            def narrow(q, r, es):
                pe.wait_ge(ht_done, q + 1)
                above(pe, y_done, q - 1)
                for half in range(2):
                    mm = pe.matmul(ps[:, 6 + r % 2, half * D:(half + 1) * D], e_hidT[:, r % 2, half * P:(half + 1) * P],
                                   down_sb[:, bass.ds(es[half] * D, D)], start=True, stop=True)
                mm.then_inc(y_full, 1)

            def slots(i, rs, begun, more):
                es = {}

                def known(r):
                    w = r // 2
                    if w not in es:
                        es[w] = experts(XP // 2 * i + w)
                    return es[w][2 * (r % 2):2 * (r % 2) + 2]

                for r in rs:
                    q = XP * i + r
                    old = r if begun is None else begun
                    if more:
                        turn_rows(i, q, r)
                    if old >= 1 and (more or r < 1):
                        widen(q - 1, r - 1, known(r - 1))
                    if more:
                        known(r)
                    if old >= 2 and (more or r < 2):
                        turn_hidden(q - 2, r - 2)
                    if old >= 3:
                        narrow(q - 3, r - 3, known(r - 3))

            slots(0, range(XP), None, True)
            with pe.Fori(1, PAIRS // XP, 1) as i:
                slots(i, range(XP), XP, True)
            slots(PAIRS // XP, range(3), XP, False)

        @block.vector
        def _(dve):
            st = Steps(dve, dve_s)

            def statistics(lo, hi):
                for t in range(lo, hi):
                    if t % TJ == 0:
                        dve.wait_ge(x_ld[t // TJ], 16)
                    st.did(dve.bn_stats(bn[:, t, :], x[:, t * D:(t + 1) * D]))
                st.wait()
                for t in range(lo, hi):
                    ins = dve.bn_aggr(mv[:, t, :], bn[:, t, :])
                ins.then_inc(stats, 1)

            def minus_mean_over_deviation(lo, hi, turn):
                dve.wait_ge(rstd_s, turn)
                dve.scalar_tensor_tensor(out=nmr[:, lo:hi], in0=mv[:, lo:hi, 0], scalar=-1.0, in1=rstd[:, lo:hi],
                                         op0=ALU.mult, op1=ALU.mult).then_inc(nmr_s, 1)

            statistics(0, TJ)
            dve.wait_ge(c_exp, 1)
            st.then(dve.tensor_scalar(ctmp[:, :], ctmp[:, :], 1.0, None, ALU.add))
            st.then(dve.reciprocal(ctmp[:, :], ctmp[:, :]))
            st.then(dve.tensor_tensor(cT[:, :], cT[:, :], ctmp[:, :], ALU.mult))
            dve.tensor_copy(c_rep[:, :, :, :].rearrange("p k b n -> p (k b) n"),
                            cT[:, :].unsqueeze(2).to_broadcast([P, KD * B, P])).then_inc(c_rep_s, 1)
            minus_mean_over_deviation(0, TJ, 1)
            dve.wait_ge(modT_ps, 1)
            st.then(dve.tensor_copy(modT[:, 0:KD * B], ps[:, 0, 0:KD * B]))
            dve.tensor_scalar(modT[:, KD * B:], ps[:, 0, KD * B:2 * KD * B], 1.0, None, ALU.add).then_inc(modT_s, 1)

            def rest_of_qk(t, c):
                m, n = t.use(f"QK{c}")
                dve.wait_ge(hi_done, 4 * (t.b + 1) + c + 1)
                frees(dve.tensor_tensor(qk_lo[:, c, :], ps[:, MISC[m], :], qk_hi[:, c, :].bitcast(F32), ALU.subtract), t, f"QK{c}")

            def score_max(b, g, n, banks=SC):
                qt, i = divmod(n, G)
                dve.wait_ge(sc_full, 64 * b + 16 * g + n + 1)
                dve.tensor_reduce(max_q[:, g % 2, qt, i:i + 1], ps[:, banks[(16 * g + n) % len(banks)], :], AXX, ALU.max).then_inc(max_done, 1)

            def neg_max_lo(t, g):
                m, n = t.use(f"MAX{g}")
                dve.wait_ge(neg_hi, NG * t.b + g + 2)
                frees(dve.scalar_tensor_tensor(out=max_lo[:, :], in0=ps[0:G, MISC[m], :], scalar=-1.0,
                                               in1=max_hi[:, :].bitcast(F32), op0=ALU.mult, op1=ALU.subtract), t, f"MAX{g}")

            def divide(t, g):
                heads = full(dve, t, f"OUT{g}").rearrange("p (q i d) -> p q i d", q=TJ, i=G)
                st.then(dve.reciprocal(rsum[:, :, :], heads[:, :, :, HD]))
                frees(dve.tensor_tensor(o_norm[:, :, G * HD * g:G * HD * (g + 1)].rearrange("p q (i d) -> p q i d", i=G),
                                        heads[:, :, :, 0:HD], rsum[:, :, :].unsqueeze(3).to_broadcast([P, TJ, G, HD]),
                                        ALU.mult), t, f"OUT{g}")

            def guarded_gate(to, src):
                st.then(dve.tensor_scalar(gtmp[:, 0, :], src, 0.0, 2.0, ALU.is_ge, ALU.mult))
                st.then(dve.tensor_scalar(gtmp[:, 0, :], gtmp[:, 0, :], -1.0, None, ALU.add))
                st.then(dve.tensor_tensor(gtmp[:, 1, :], src, gtmp[:, 0, :], ALU.mult))
                st.then(dve.scalar_tensor_tensor(out=to, in0=gtmp[:, 1, :], scalar=0.25, in1=gtmp[:, 0, :],
                                                 op0=ALU.max, op1=ALU.mult))

            def modulation(t, s):
                if s == 0:
                    dve.wait_ge(w_ld, 48)
                bank = full(dve, t, f"MOD{s}")
                b = s // 2
                at = 3 * D * b
                if s % 2 == 0:
                    guarded_gate(gtmp[:, 0, :], bank[:, 0:D])
                    for k in range(KD):
                        st.did(dve.tensor_tensor(wo_g[:, (b * KD + k) * D:(b * KD + k + 1) * D], wo_sb[:, k, :], gtmp[:, 0, :], ALU.mult))
                    st.wait()
                    frees(dve.tensor_copy(mod_b[:, at:at + D], bank[:, D:2 * D]), t, f"MOD{s}")
                else:
                    guarded_gate(mod_b[:, at + 2 * D:at + 3 * D], bank[:, D:2 * D])
                    frees(dve.tensor_scalar(mod_b[:, at + D:at + 2 * D], bank[:, 0:D], 1.0, None, ALU.add), t, f"MOD{s}")

            def residual(t, m):
                bank = full(dve, t, f"WO{m}")
                two = x[:, bass.ds((t.b - 1) * (TJ * D) + 2 * m * D, 2 * D)]
                frees(dve.tensor_tensor(two, bank, two, ALU.add), t, f"WO{m}")

            def statistics2(t, m):
                p = t.b - 1
                own_free(dve, t, f"WO{m}")
                apart(dve)
                for j in (2 * m, 2 * m + 1):
                    st.did(dve.bn_stats(bn[:, j, :], x[:, bass.ds((TJ * p + j) * D, D)]))
                if m:
                    st.wait()
                    apart(dve)
                    for j in range(TJ):
                        ins = dve.bn_aggr(mv2[:, j, :], bn[:, j, :])
                    ins.then_inc(stats2, 1)

            def scale_and_shift(t):
                p = t.b - 1
                dve.wait_ge(h2_norm, p + 1)
                st.then(dve.tensor_tensor(h2[:, :, 0:D], h2[:, :, 0:D],
                                          mod_b[:, (3 * p + 1) * D:(3 * p + 2) * D].unsqueeze(1).to_broadcast([P, TJ, D]), ALU.mult))
                dve.tensor_tensor(h2[:, :, 0:D], h2[:, :, 0:D],
                                  mod_b[:, 3 * p * D:(3 * p + 1) * D].unsqueeze(1).to_broadcast([P, TJ, D]), ALU.add).then_inc(h2_ready, 1)

            def top_logits(t):
                own_free(dve, t, "LGT")
                apart(dve)
                for j in range(TJ):
                    st.did(dve.max(v8[:, j, :], lg[:, j, 0:E]))

            def top_experts(t):
                st.wait()
                apart(dve)
                for j in range(TJ):
                    st.did(dve.max_index(i8[:, j, :], v8[:, j, :], lg[:, j, 0:E]))
                top = v8[:, :, 0:1]
                dve.tensor_tensor(ex[:, :, 0:E], lg[:, :, 0:E], top.to_broadcast([P, TJ, E]), ALU.subtract).then_inc(ex_in, 1)
                dve.tensor_tensor(ex[:, :, E:E + TOPK], v8[:, :, 0:TOPK], top.to_broadcast([P, TJ, TOPK]),
                                  ALU.subtract).then_inc(ex_in, 1)

            def choices_of_one(t):
                st.wait()
                st.then(dve.tensor_copy(e4[:, :, :], i8[:, :, 0:TOPK]))
                dve.tensor_tensor(onehot[:, :, :], iota_ef[:, :].unsqueeze(1).to_broadcast([P, TJ * TOPK, E]),
                                  e4[:, :, :].rearrange("p j k -> p (j k)").unsqueeze(2).to_broadcast([P, TJ * TOPK, E]),
                                  ALU.is_equal).then_inc(top_s, 1)

            def weights(t):
                p = t.b - 1
                dve.wait_ge(ex_out, 2 * t.b)
                st.then(dve.tensor_reduce(z4[:, :], ex[:, :, 0:E], AXX, ALU.add))
                st.then(dve.reciprocal(z4[:, :], z4[:, :]))
                st.then(dve.tensor_tensor(p4[:, :, :], ex[:, :, E:E + TOPK], z4[:, :].unsqueeze(2).to_broadcast([P, TJ, TOPK]), ALU.mult))
                st.then(dve.tensor_reduce(s4[:, :], p4[:, :, :], AXX, ALU.add))
                st.then(dve.tensor_scalar(s4[:, :], s4[:, :], 1e-20, None, ALU.add))
                st.then(dve.reciprocal(s4[:, :], s4[:, :]))
                st.did(dve.tensor_tensor(tails[:, bass.ds(p * TJ, TJ), :, 1], p4[:, :, :], s4[:, :].unsqueeze(2).to_broadcast([P, TJ, TOPK]), ALU.mult))
                st.then(dve.tensor_scalar(sgt[:, :], sgt[:, :], 2.0, 2.0, ALU.mult, ALU.add))
                dve.reciprocal(sg[:, bass.ds(p * TJ, TJ)], sgt[:, :]).then_inc(weights_s, 1)

            def ranks_out(t):
                bank = full(dve, t, "RANK")
                frees(dve.tensor_tensor(rank[:, :, :], bank[:, 0:TJ * E].rearrange("p (j e) -> p j e", e=E),
                                        base_f[:, :].unsqueeze(1).to_broadcast([P, TJ, E]), ALU.add), t, "RANK")

            def slots(t):
                own_free(dve, t, "RANK")
                st.then(dve.tensor_tensor(picked[:, :, :].rearrange("p (j k) e -> p j k e", k=TOPK),
                                          onehot[:, :, :].rearrange("p (j k) e -> p j k e", k=TOPK),
                                          rank[:, :, :].unsqueeze(2).to_broadcast([P, TJ, TOPK, E]), ALU.mult))
                st.then(dve.tensor_reduce(slot_f[:, :], picked[:, :, :], AXX, ALU.add))
                dve.tensor_copy(slot_i[:, :], slot_f[:, :]).then_inc(slots_s, 1)

            def tile_table(t):
                frees(dve.tensor_copy(cnt[:, :], full(dve, t, "CNT")[:, 0:E]), t, "CNT")
                own_free(dve, t, "CNT")
                over = gtmp[:, :, :].rearrange("p a e -> p (a e)").rearrange("p (e r) -> p e r", r=NT)
                st.then(dve.tensor_tensor(over, cnt[:, :].unsqueeze(2).to_broadcast([P, E, NT]),
                                          thr_f[:, :].unsqueeze(1).to_broadcast([P, E, NT]), ALU.is_gt))
                st.then(dve.tensor_reduce(ntile[:, :], over, AXX, ALU.add))
                st.then(dve.tensor_tensor_scan(ctile[:, :], ones[:, 0:E], ntile[:, :], 0.0, ALU.mult, ALU.add))
                st.then(dve.tensor_scalar(past[:, :], ctile[:, :], tile_f[:, 0:1], None, ALU.is_le))
                st.did(dve.tensor_reduce(tcol[:, 0:1], past[:, :], AXX, ALU.add))
                st.then(dve.tensor_tensor(past_n[:, :], past[:, :], ntile[:, :], ALU.mult))
                st.then(dve.tensor_reduce(tcol[:, 1:2], past_n[:, :], AXX, ALU.add))
                cur = past_n
                st.did(dve.tensor_scalar(cur[:, 0:1], past[:, 0:1], -1.0, 1.0, ALU.mult, ALU.add))
                st.then(dve.tensor_tensor(cur[:, 1:E], past[:, 0:E - 1], past[:, 1:E], ALU.subtract))
                st.then(dve.tensor_tensor(cur[:, :], cur[:, :], cnt[:, :], ALU.mult))
                st.did(dve.tensor_reduce(tcol[:, 4:5], cur[:, :], AXX, ALU.add))
                st.did(dve.tensor_tensor(tcol[:, 2:3], tile_f[:, :], tcol[:, 1:2], ALU.subtract))
                st.did(dve.tensor_scalar(tcol[:, 3:4], past[:, E - 1:E], float(P), float(-P), ALU.mult, ALU.add))
                st.then(dve.tensor_scalar(tcol2[:, 0:1], tcol[:, 0:1], float(E - 1), None, ALU.min))
                st.then(dve.scalar_tensor_tensor(out=tcol[:, 5:6], in0=tcol[:, 2:3], scalar=tcol[:, 3:4], in1=tcol[:, 4:5],
                                                 op0=ALU.mult, op1=ALU.add))
                dve.scalar_tensor_tensor(out=tcol2[:, 1:2], in0=tcol[:, 0:1], scalar=float(CAP), in1=tcol[:, 5:6],
                                         op0=ALU.mult, op1=ALU.add).then_inc(tcol_s, 1)

            def pack_table(t):
                frees(dve.tensor_copy(tabf[:, :], full(dve, t, "TAB")[0:1, 0:2 * P]), t, "TAB")
                own_free(dve, t, "TAB")
                four = tabf[:, 0:P].rearrange("o (w n) -> o w n", n=4)
                for n in (2, 1, 0):
                    st.then(dve.scalar_tensor_tensor(out=four[:, :, 3], in0=four[:, :, 3], scalar=32.0, in1=four[:, :, n],
                                                     op0=ALU.mult, op1=ALU.add))
                dve.tensor_copy(tab[:, 0:P // 4], four[:, :, 3])
                dve.tensor_copy(tab[:, P:2 * P], tabf[:, P:2 * P]).then_inc(tab_s, 1)

            def hidden_gate(t, c):
                bank = full(dve, t, f"SG{c}")
                dve.wait_ge(tanh_s, 4 * (t.b - 1) + c + 1)
                frees(dve.scalar_tensor_tensor(out=sh_tanh[:, c % 2, :], in0=sh_tanh[:, c % 2, :], scalar=1.0, in1=bank,
                                               op0=ALU.add, op1=ALU.mult), t, f"SG{c}")

            def hidden_up(t, c):
                if c == 0:
                    for half in range(2):
                        dve.wait_ge(spill[half], min(32 * (t.b + 2), 32 * B) if isinstance(t.b, int) else 32 * t.b + 64)
                bank = full(dve, t, f"SU{c}")
                own_free(dve, t, f"SG{c}")
                ins = dve.tensor_tensor(sh_hidT[:, c, :], sh_tanh[:, c % 2, :], bank, ALU.mult)
                frees(ins, t, f"SU{c}")

            def add_shared(t, m):
                p = t.b - 1
                bank = full(dve, t, f"SD{m}")
                for j in (2 * m, 2 * m + 1):
                    ins = dve.scalar_tensor_tensor(out=gtmp[:, j % 2, :], in0=bank[:, (j % 2) * D:(j % 2 + 1) * D],
                                                   scalar=sg[:, bass.ds(TJ * p + j, 1)],
                                                   in1=mod_b[:, bass.ds(p * (3 * D) + 2 * D, D)], op0=ALU.mult, op1=ALU.mult)
                    if j % 2:
                        frees(ins, t, f"SD{m}")
                    else:
                        st.did(ins)
                st.wait()
                own_free(dve, t, f"SD{m}")
                two = x[:, bass.ds(p * (TJ * D) + 2 * m * D, 2 * D)]
                st.then(dve.tensor_tensor(two, two, gtmp[:, :, :].rearrange("p j d -> p (j d)"), ALU.add))

            def between(t, g, u):
                if u == 2 and (t.att and g < 3 or t.pre and g == 3):
                    neg_max_lo(t, g)
                if g == 0:
                    if t.post and u == 7:
                        divide(t, 3)
                    if t.mod and u == 8:
                        modulation(t, 0)
                    if t.pre and u in (9, 11, 13):
                        rest_of_qk(t, {9: 0, 11: 1, 13: 2}[u])
                    if t.post and u in (12, 15):
                        residual(t, u // 15)
                    if t.post and u == 14:
                        statistics2(t, 0)
                    if t.mod and u == 13:
                        modulation(t, 1)
                elif t.att and u == 7:
                    divide(t, g - 1)
                if g == 1:
                    if t.post and u == 0:
                        statistics2(t, 1)
                    if t.end and u == 4:
                        scale_and_shift(t)
                    if t.pre and u == 2:
                        rest_of_qk(t, 3)
                    if t.mod and u in (12, 15):
                        modulation(t, {12: 2, 15: 3}[u])
                if g == 2:
                    if t.mod and u in (10, 14):
                        modulation(t, 2 + u // 4)
                    if t.post and u in (5, 10, 13):
                        hidden_gate(t, {5: 0, 10: 1, 13: 2}[u])
                    if t.post and u == 6:
                        top_logits(t)
                    if t.post and u == 7:
                        top_experts(t)
                    if t.post and u == 8:
                        choices_of_one(t)
                    if t.end and u == 8:
                        weights(t)
                        ranks_out(t)
                        slots(t)
                        tile_table(t)
                    if t.post and u == 8:
                        hidden_up(t, 0)
                    if t.post and u == 11:
                        hidden_up(t, 1)
                    if t.att and t.post and u == 12:
                        weights(t)
                    if t.att and t.post and u == 14:
                        ranks_out(t)
                    if t.att and t.post and u == 15:
                        slots(t)
                    if t.end and u == 15:
                        pack_table(t)
                if g == 3:
                    if t.post and u == 0:
                        hidden_up(t, 2)
                    if t.mod and u in (10, 14):
                        modulation(t, 4 + u // 4)
                    if t.post and u == 5:
                        hidden_gate(t, 3)
                    if t.post and u == 8:
                        hidden_up(t, 3)
                    if t.post and u in (11, 14):
                        add_shared(t, u // 14)

            def turn(t):
                for g in range(NG):
                    for u in range(16):
                        if t.att and g < 2:
                            score_max(t.b, g + 2, u)
                        elif t.att and t.pre:
                            score_max(t.b + 1, g - 2, u)
                        between(t, g, u)

            for c in range(4):
                rest_of_qk(lead, c)
            statistics(TJ, NT)
            dve.wait_ge(consts, 1)
            for to, of in ((iota_ef, iota_e), (base_f, base_i), (thr_f, thr_i), (tile_f, tile_i)):
                st.did(dve.tensor_copy(to[:, :], of[:, :]))
            st.did(dve.tensor_copy(tails[:, :, :, 0], home[:, :].rearrange("p (t k) -> p t k", k=TOPK)))
            for n in range(16):
                score_max(0, 0, n, SC + ST)
            neg_max_lo(lead, 3)
            minus_mean_over_deviation(TJ, NT, 2)
            for n in range(16):
                score_max(0, 1, n, SC + ST)
            turn(first)
            st.wait()
            with dve.Fori(LOOP0, LOOP1, 1) as b:
                st.enter(b - LOOP0, DVE_STEPS)
                turn(middle(b))
            st.leave(LOOP1 - LOOP0)
            turn(last)
            turn(drain)

            def columns_out(q, r):
                dve.wait_ge(t_full, q + 1)
                above(dve, u_full, q - 1)
                dve.tensor_copy(xeT[:, r % 2, :], ps[:, r % 2, :]).then_inc(t_done, 1)

            def gated(q, r):
                dve.wait_ge(esilu_s, q + 1)
                above(dve, ht_full, q - 1)
                for half in range(2):
                    ins = dve.scalar_tensor_tensor(
                        out=e_hid[:, r % 2, half * DM:(half + 1) * DM], in0=ps[:, 2 + r % 2, (2 * half + 1) * DM:(2 * half + 2) * DM],
                        scalar=xe[:, 2 * (r % XP) + half, D + 1:D + 2], in1=e_silu[:, r % 2, half * DM:(half + 1) * DM],
                        op0=ALU.mult, op1=ALU.mult)
                ins.then_inc(hid_s, 1)

            for r in range(XP):
                columns_out(r, r)
                if r:
                    gated(r - 1, r - 1)
            with dve.Fori(1, PAIRS // XP, 1) as i:
                for r in range(XP):
                    columns_out(XP * i + r, r)
                    gated(XP * i + r - 1, r - 1)
            gated(PAIRS - 1, XP - 1)
            for t in range(NT):
                b = t // TJ
                dve.wait_ge(comb_ld[t % CR], 16 * (t // CR) + 16)
                dve.tensor_reduce(gtmp[:, t % 2, :], comb[:, t % CR, :].rearrange("p (k d) -> p d k", k=TOPK), AXX, ALU.add).then_inc(part_s, 1)
                dve.wait_ge(part_s, t + 1)
                if t >= CR:
                    dve.wait_ge(x3_done, t - CR + 1)
                dve.tensor_tensor(y_sb[:, t % CR, :], gtmp[:, t % 2, :], mod_b[:, (3 * b + 2) * D:(3 * b + 3) * D],
                                  ALU.mult).then_inc(prod_s, 1)


def kernel(**inputs):
    import numpy as _np
    import concourse.bacc as _bacc
    from concourse import mybir as _mybir
    from concourse.bass_utils import run_bass_kernel_spmd as _run

    i = {k[3:]: _np.asarray(v) for k, v in inputs.items()}
    arrays = {
        "x": i["attn_x"],
        "wq": i["attn_wq"].T, "wk": i["attn_wk"].T, "wv": i["attn_wv"].T, "wo": i["attn_wo"].T,
        "gate": _np.concatenate([i["ffn_gate_w"], i["ffn_shared_expert_gate_w"]], axis=0).T,
        "up": i["ffn_gate_up_proj"].transpose(2, 0, 1).reshape(D, E * 2 * DM),
        "down": i["ffn_down_proj"].transpose(2, 0, 1).reshape(DM, E * D),
        "sgate": i["ffn_shared_gate_w"].T, "sup": i["ffn_shared_up_w"].T, "sdown": i["ffn_shared_down_w"].T,
        "c": i["c"].T, "wmod": i["wmod"],
    }
    arrays = {f"in_{k}": _np.ascontiguousarray(v) for k, v in arrays.items()}
    nc = _bacc.Bacc("TRN2", target_bir_lowering=False, num_devices=1)
    args = [nc.dram_tensor(k, v.shape, _mybir.dt.from_np(v.dtype), kind="ExternalInput").ap() for k, v in arrays.items()]
    out = nc.dram_tensor("out", (B, S, D), _mybir.dt.float32, kind="ExternalOutput").ap()
    adaln_moe_kernel(nc, *args, out)
    r = _run(nc, [arrays], core_ids=[0])
    return r.results[0]["out"]
```
